# Optimizing a Trainium2 kernel written in Bass

```python
import numpy as np
import jax
import jax.numpy as jnp

def _softmax(x, axis=-1):
    return jax.nn.softmax(x, axis=axis)

def _gelu(x):
    return jax.nn.gelu(x, approximate=True)

def _silu(x):
    return jax.nn.silu(x)

def _sigmoid(x):
    return jax.nn.sigmoid(x)

def _layernorm(x, axis=-1, eps=1e-05):
    m = jnp.mean(x, axis=axis, keepdims=True)
    v = jnp.var(x, axis=axis, keepdims=True)
    return (x - m) / jnp.sqrt(v + eps)

def _scatter_add(tgt, idx, src, axis=0):
    return tgt.at[idx].add(src)

def _segment_sum(src, seg, n):
    return jax.ops.segment_sum(src, seg, n)
kernel_name = 'mk_recurrent_d1_jaxref_r4_ee0288'

def setup_inputs(seed: int=0):
    np.random.seed(seed)
    _w = jnp.asarray

    def _L0_attn_setup():
        import jax, jax.numpy as jnp
        import numpy as np
        B, L, D_MODEL = (2, 1024, 256)
        D_STATE, D_CONV, EXPAND, HEADDIM = (128, 4, 2, 64)
        D_INNER = EXPAND * D_MODEL
        NHEADS = D_INNER // HEADDIM
        CONV_DIM = D_INNER + 2 * D_STATE
        D_IN_PROJ = 2 * D_INNER + 2 * D_STATE + NHEADS
        CHUNK = 128
        EPS = 1e-05

        def _segsum(a):
            T = a.shape[-1]
            cs = jnp.cumsum(a, axis=-1)
            seg = cs[..., :, None] - cs[..., None, :]
            mask = jnp.tril(jnp.ones((T, T), dtype=bool))
            return jnp.where(mask, seg, -jnp.inf)

        def _forward(x, norm_w, norm_b, in_proj_w, conv_w, conv_b, dt_bias, A_log, D, rms_w, out_proj_w):
            b, l, _ = x.shape
            mu = jnp.mean(x, -1, keepdims=True)
            var = jnp.mean(jnp.square(x - mu), -1, keepdims=True)
            xn = (x - mu) * jax.lax.rsqrt(var + EPS) * norm_w + norm_b
            zxbcdt = xn @ in_proj_w.T
            z = zxbcdt[..., :D_INNER]
            xBC = zxbcdt[..., D_INNER:D_INNER + CONV_DIM]
            dt = jax.nn.softplus(zxbcdt[..., -NHEADS:] + dt_bias)
            xc = jnp.pad(xBC.transpose(0, 2, 1), ((0, 0), (0, 0), (D_CONV - 1, 0)))
            xc = jax.lax.conv_general_dilated(xc, conv_w[:, None, :], (1,), 'VALID', feature_group_count=CONV_DIM, dimension_numbers=('NCH', 'OIH', 'NCH'))
            xBC = jax.nn.silu(xc + conv_b[None, :, None]).transpose(0, 2, 1)
            xs = xBC[..., :D_INNER].reshape(b, l, NHEADS, HEADDIM)
            Bm = xBC[..., D_INNER:D_INNER + D_STATE]
            Cm = xBC[..., D_INNER + D_STATE:]
            A = -jnp.exp(A_log)
            a = dt * A
            X = xs * dt[..., None]
            c = l // CHUNK
            a_c = a.reshape(b, c, CHUNK, NHEADS).transpose(0, 3, 1, 2)
            a_cum = jnp.cumsum(a_c, -1)
            Lmat = jnp.exp(_segsum(a_c))
            Xc = X.reshape(b, c, CHUNK, NHEADS, HEADDIM)
            Bc = Bm.reshape(b, c, CHUNK, D_STATE)
            Cc = Cm.reshape(b, c, CHUNK, D_STATE)
            Y_diag = jnp.einsum('bcln,bcsn,bhcls,bcshp->bclhp', Cc, Bc, Lmat, Xc)
            decay_states = jnp.exp(a_cum[..., -1:] - a_cum)
            states = jnp.einsum('bcln,bhcl,bclhp->bchpn', Bc, decay_states, Xc)
            states = jnp.concatenate([jnp.zeros_like(states[:, :1]), states], axis=1)
            chunk_decay = jnp.exp(_segsum(jnp.pad(a_cum[..., -1], ((0, 0), (0, 0), (1, 0)))))
            prev = jnp.einsum('bhzc,bchpn->bzhpn', chunk_decay, states)[:, :-1]
            Y_off = jnp.einsum('bcln,bchpn,bhcl->bclhp', Cc, prev, jnp.exp(a_cum))
            y = (Y_diag + Y_off).reshape(b, l, NHEADS, HEADDIM) + D[None, None, :, None] * xs
            y = y.reshape(b, l, D_INNER)
            y = y * jax.nn.silu(z)
            y = y * jax.lax.rsqrt(jnp.mean(jnp.square(y), -1, keepdims=True) + EPS) * rms_w
            return x + y @ out_proj_w.T
        key = jax.random.key(seed)
        ks = jax.random.split(key, 8)
        return {'x': jax.random.normal(ks[0], (B, L, D_MODEL), jnp.float32), 'norm_w': jnp.ones((D_MODEL,), jnp.float32), 'norm_b': jnp.zeros((D_MODEL,), jnp.float32), 'in_proj_w': 0.02 * jax.random.normal(ks[1], (D_IN_PROJ, D_MODEL), jnp.float32), 'conv_w': 0.2 * jax.random.normal(ks[2], (CONV_DIM, D_CONV), jnp.float32), 'conv_b': jnp.zeros((CONV_DIM,), jnp.float32), 'dt_bias': jax.random.uniform(ks[3], (NHEADS,), jnp.float32, -4.0, 0.0), 'A_log': jnp.log(jax.random.uniform(ks[4], (NHEADS,), jnp.float32, 1.0, 16.0)), 'D': jnp.ones((NHEADS,), jnp.float32), 'rms_w': jnp.ones((D_INNER,), jnp.float32), 'out_proj_w': 0.02 * jax.random.normal(ks[5], (D_MODEL, D_INNER), jnp.float32)}
    _L0_attn_in = _L0_attn_setup()

    def _L0_ffn_setup():
        import jax, jax.numpy as jnp
        import numpy as np
        B, S, D, T = (4, 1024, 256, 8)
        key = jax.random.key(seed)
        k1, k2, k3, k4 = jax.random.split(key, 4)
        x = jax.random.normal(k1, (B, S, D), dtype=jnp.float32)
        tile_sigs = jax.random.normal(k2, (T, D), dtype=jnp.float32)
        bound = 1.0 / np.sqrt(D)
        W = jax.random.uniform(k3, (T, D, D), minval=-bound, maxval=bound, dtype=jnp.float32)
        b = jax.random.uniform(k4, (T, D), minval=-bound, maxval=bound, dtype=jnp.float32)
        return {'x': x, 'tile_sigs': tile_sigs, 'W': W, 'b': b}
    _L0_ffn_in = _L0_ffn_setup()
    _d = {'L0_attn_x': _L0_attn_in['x'], 'L0_attn_norm_w': _L0_attn_in['norm_w'], 'L0_attn_norm_b': _L0_attn_in['norm_b'], 'L0_attn_in_proj_w': _L0_attn_in['in_proj_w'], 'L0_attn_conv_w': _L0_attn_in['conv_w'], 'L0_attn_conv_b': _L0_attn_in['conv_b'], 'L0_attn_dt_bias': _L0_attn_in['dt_bias'], 'L0_attn_A_log': _L0_attn_in['A_log'], 'L0_attn_D': _L0_attn_in['D'], 'L0_attn_rms_w': _L0_attn_in['rms_w'], 'L0_attn_out_proj_w': _L0_attn_in['out_proj_w'], 'L0_ffn_tile_sigs': _L0_ffn_in['tile_sigs'], 'L0_ffn_W': _L0_ffn_in['W'], 'L0_ffn_b': _L0_ffn_in['b']}
    _x0 = _d['L0_attn_x']
    _d['L0_attn_x'] = jax.random.normal(jax.random.fold_in(jax.random.key(seed), 1), (16, 512, 256), dtype=_x0.dtype)
    del _x0
    return _d

def reference(L0_attn_x, L0_attn_norm_w, L0_attn_norm_b, L0_attn_in_proj_w, L0_attn_conv_w, L0_attn_conv_b, L0_attn_dt_bias, L0_attn_A_log, L0_attn_D, L0_attn_rms_w, L0_attn_out_proj_w, L0_ffn_tile_sigs, L0_ffn_W, L0_ffn_b):

    def _L0_attn_ref(x, norm_w, norm_b, in_proj_w, conv_w, conv_b, dt_bias, A_log, D, rms_w, out_proj_w):
        import jax, jax.numpy as jnp
        import numpy as np
        B, L, D_MODEL = (2, 1024, 256)
        D_STATE, D_CONV, EXPAND, HEADDIM = (128, 4, 2, 64)
        D_INNER = EXPAND * D_MODEL
        NHEADS = D_INNER // HEADDIM
        CONV_DIM = D_INNER + 2 * D_STATE
        D_IN_PROJ = 2 * D_INNER + 2 * D_STATE + NHEADS
        CHUNK = 128
        EPS = 1e-05

        def _segsum(a):
            T = a.shape[-1]
            cs = jnp.cumsum(a, axis=-1)
            seg = cs[..., :, None] - cs[..., None, :]
            mask = jnp.tril(jnp.ones((T, T), dtype=bool))
            return jnp.where(mask, seg, -jnp.inf)

        def _forward(x, norm_w, norm_b, in_proj_w, conv_w, conv_b, dt_bias, A_log, D, rms_w, out_proj_w):
            b, l, _ = x.shape
            mu = jnp.mean(x, -1, keepdims=True)
            var = jnp.mean(jnp.square(x - mu), -1, keepdims=True)
            xn = (x - mu) * jax.lax.rsqrt(var + EPS) * norm_w + norm_b
            zxbcdt = xn @ in_proj_w.T
            z = zxbcdt[..., :D_INNER]
            xBC = zxbcdt[..., D_INNER:D_INNER + CONV_DIM]
            dt = jax.nn.softplus(zxbcdt[..., -NHEADS:] + dt_bias)
            xc = jnp.pad(xBC.transpose(0, 2, 1), ((0, 0), (0, 0), (D_CONV - 1, 0)))
            xc = jax.lax.conv_general_dilated(xc, conv_w[:, None, :], (1,), 'VALID', feature_group_count=CONV_DIM, dimension_numbers=('NCH', 'OIH', 'NCH'))
            xBC = jax.nn.silu(xc + conv_b[None, :, None]).transpose(0, 2, 1)
            xs = xBC[..., :D_INNER].reshape(b, l, NHEADS, HEADDIM)
            Bm = xBC[..., D_INNER:D_INNER + D_STATE]
            Cm = xBC[..., D_INNER + D_STATE:]
            A = -jnp.exp(A_log)
            a = dt * A
            X = xs * dt[..., None]
            c = l // CHUNK
            a_c = a.reshape(b, c, CHUNK, NHEADS).transpose(0, 3, 1, 2)
            a_cum = jnp.cumsum(a_c, -1)
            Lmat = jnp.exp(_segsum(a_c))
            Xc = X.reshape(b, c, CHUNK, NHEADS, HEADDIM)
            Bc = Bm.reshape(b, c, CHUNK, D_STATE)
            Cc = Cm.reshape(b, c, CHUNK, D_STATE)
            Y_diag = jnp.einsum('bcln,bcsn,bhcls,bcshp->bclhp', Cc, Bc, Lmat, Xc)
            decay_states = jnp.exp(a_cum[..., -1:] - a_cum)
            states = jnp.einsum('bcln,bhcl,bclhp->bchpn', Bc, decay_states, Xc)
            states = jnp.concatenate([jnp.zeros_like(states[:, :1]), states], axis=1)
            chunk_decay = jnp.exp(_segsum(jnp.pad(a_cum[..., -1], ((0, 0), (0, 0), (1, 0)))))
            prev = jnp.einsum('bhzc,bchpn->bzhpn', chunk_decay, states)[:, :-1]
            Y_off = jnp.einsum('bcln,bchpn,bhcl->bclhp', Cc, prev, jnp.exp(a_cum))
            y = (Y_diag + Y_off).reshape(b, l, NHEADS, HEADDIM) + D[None, None, :, None] * xs
            y = y.reshape(b, l, D_INNER)
            y = y * jax.nn.silu(z)
            y = y * jax.lax.rsqrt(jnp.mean(jnp.square(y), -1, keepdims=True) + EPS) * rms_w
            return x + y @ out_proj_w.T
        return _forward(x, norm_w, norm_b, in_proj_w, conv_w, conv_b, dt_bias, A_log, D, rms_w, out_proj_w)

    def _L0_ffn_ref(x, tile_sigs, W, b):
        import jax, jax.numpy as jnp
        import numpy as np
        B, S, D, T = (4, 1024, 256, 8)
        scores = jnp.einsum('bsd,td->bst', x, jnp.sign(tile_sigs))
        idx = jnp.argmax(scores, axis=-1)
        all_out = jnp.einsum('bsd,tde->bste', x, W) + b[None, None]
        out = jnp.take_along_axis(all_out, idx[:, :, None, None], axis=2)
        return out[:, :, 0, :]
    x = L0_attn_x
    xn = _layernorm(x, axis=-1)
    s = _L0_attn_ref(xn, L0_attn_norm_w, L0_attn_norm_b, L0_attn_in_proj_w, L0_attn_conv_w, L0_attn_conv_b, L0_attn_dt_bias, L0_attn_A_log, L0_attn_D, L0_attn_rms_w, L0_attn_out_proj_w)
    g = _silu(_L0_ffn_ref(xn, L0_ffn_tile_sigs, L0_ffn_W, L0_ffn_b))
    x = x + s * g
    return x

_drawn_inputs = setup_inputs


def setup_inputs(seed=0):
    import zlib

    import numpy as np

    out = dict(_drawn_inputs(seed))
    spreads = {'L0_attn_norm_w': (1.0, 0.2),
     'L0_attn_norm_b': (0.0, 0.448),
     'L0_attn_conv_b': (0.0, 0.1),
     'L0_attn_D': (1.0, 0.6),
     'L0_attn_rms_w': (1.0, 0.6)}
    factors = {'L0_attn_dt_bias': 8.0, 'L0_attn_A_log': 8.0, 'L0_ffn_b': 2.956}
    for name, (base, spread) in spreads.items():
        noise = np.random.default_rng([zlib.crc32(name.encode()), seed]).standard_normal(out[name].shape)
        drawn = base * np.exp(spread * noise) if base else spread * noise
        out[name] = jnp.asarray(drawn.astype(out[name].dtype))
    for name, factor in factors.items():
        out[name] = (out[name] * factor).astype(out[name].dtype)
    return out
```

```python
import concourse.bass as bass
from concourse import mybir
from contextlib import ExitStack
import numpy as np

P = 128
SEQS, SEQ, DM = 16, 512, 256
TOK = SEQS * SEQ
NCH = TOK // P
CPS = SEQ // P
KT = DM // P
H, HD, NST = 8, 64, 128
DI = H * HD
ZT = DI // P
XT = (DI + 2 * NST) // P
DPROJ = 2 * DI + 2 * NST + H
TAPS = 4
E = 8
FT = NCH + E
EPS = 1e-5
WS = 64.0
PARTS = 3


def program(nc, x, norm_w, norm_b, in_proj_w, conv_w, conv_b, dt_bias, A_log, D, rms_w, out_proj_w,
            tile_sigs, ffn_W, ffn_b, out):
    fp32, fp16, bf16, i32 = mybir.dt.float32, mybir.dt.float16, mybir.dt.bfloat16, mybir.dt.int32
    ACT, ALU, AX = mybir.ActivationFunctionType, mybir.AluOpType, mybir.AxisListType

    xT_d = nc.dram_tensor("xT_scratch", (SEQS, P, 2 * KT * SEQ), fp16).ap()
    cs_d = nc.dram_tensor("cs_scratch", (PARTS * H, TOK), bf16).ap()
    sorted_d = nc.dram_tensor("sorted_scratch", (FT * P, DM), fp32).ap()
    gate_d = nc.dram_tensor("gate_scratch", (FT * P, DM), fp32).ap()

    x_g = x.rearrange("b (c p) d -> b p c d", p=P)
    out_g = out.rearrange("b (c p) d -> b p c d", p=P)

    ctx = ExitStack()
    with ctx:
        def sem(name):
            return ctx.enter_context(nc.semaphore(name))

        def sbuf(stack, name, shape, dt=fp32):
            return stack.enter_context(nc.sbuf_tensor(name, shape, dt))

        bankL = ctx.enter_context(nc.psum_tensor("bankL", [P, 2 * 512], fp32))
        bank = [ctx.enter_context(nc.psum_tensor(f"bank{i}", [P, 512], fp32)) for i in range(6)]

        ident = sbuf(ctx, "ident", [P, P])
        ident_b = sbuf(ctx, "ident_b", [P, P], bf16)
        wz = sbuf(ctx, "w_in", [P, 2, KT, DPROJ], fp16)
        wo = sbuf(ctx, "w_out", [P, ZT, DM])
        zbias = sbuf(ctx, "zbias", [P, DI], fp16)
        pick = sbuf(ctx, "pick", [P, P], fp16)
        xbias = sbuf(ctx, "xbias", [P, XT])
        cw = sbuf(ctx, "cw", [P, XT, TAPS])
        cb = sbuf(ctx, "cb", [P, XT])
        D_bc = sbuf(ctx, "D_bc", [P, H])
        blk = sbuf(ctx, "blk", [PARTS * H, H, P], bf16)
        maskneg = sbuf(ctx, "maskneg", [P, P], bf16)
        norm_st = sbuf(ctx, "norm_st", [P, NCH, 2])
        dt_all = sbuf(ctx, "dt_all", [P, NCH, H])
        w_all = sbuf(ctx, "w_all", [P, NCH, H])
        ea_all = sbuf(ctx, "ea_all", [P, NCH, H])
        tot_all = sbuf(ctx, "tot_all", [P, NCH, H])
        pos_all = sbuf(ctx, "pos_all", [P, NCH], i32)
        epsc = sbuf(ctx, "epsc", [P, 1])
        mhalf = sbuf(ctx, "mhalf", [P, 8])

        ffn_stack = ExitStack()
        fw = sbuf(ffn_stack, "ffn_w", [P, 2, KT, E, DM], fp16)
        fb = sbuf(ffn_stack, "ffn_b", [P, E, DM], fp16)
        te = sbuf(ffn_stack, "tile_expert", [P, FT], i32)
        ft = sbuf(ffn_stack, "ffn_x", [P, 4, DM])
        fxT = sbuf(ffn_stack, "ffn_xT", [P, 2, 2, KT, P], fp16)
        gt = sbuf(ffn_stack, "ffn_gate", [P, 4, DM])
        pre_stack = ExitStack()
        xn_all = sbuf(pre_stack, "xn_all", [P, NCH, DM])
        sd_all = sbuf(pre_stack, "sd_all", [P, NCH, 2 * H])
        mhi = sbuf(pre_stack, "mhi", [P, KT, 2 * H], fp16)
        mlo = sbuf(pre_stack, "mlo", [P, KT, 2 * H], fp16)
        dtb = sbuf(pre_stack, "dtb", [P, H])
        a_bc = sbuf(pre_stack, "a_bc", [P, H])
        nwb = sbuf(pre_stack, "nwb", [P, 2, KT])
        rev = sbuf(pre_stack, "rev", [P, E])
        tri = sbuf(pre_stack, "tri", [P, P])
        suf = sbuf(pre_stack, "suf", [P, P])
        ones = sbuf(pre_stack, "ones", [P, P])
        ones_b = sbuf(pre_stack, "ones_b", [P, P], bf16)
        stri_b = sbuf(pre_stack, "stri_b", [P, P], bf16)
        zrow = sbuf(pre_stack, "zrow", [P, DM * 4])
        w_stack = ExitStack()
        wrow = sbuf(w_stack, "wrow", [P, 11, DM])
        wT = sbuf(w_stack, "wT", [P, KT, DPROJ])
        worow = sbuf(w_stack, "worow", [P, KT, DI])
        rmsw = sbuf(w_stack, "rmsw", [P, ZT])
        sig = sbuf(w_stack, "sig", [P, DM])
        neg = sbuf(w_stack, "neg", [P, KT, E])
        nbrep = sbuf(w_stack, "nbrep", [P, KT, P])
        nw64 = sbuf(w_stack, "nw64", [P, KT])
        fstage = sbuf(w_stack, "fstage", [P, E, DM])
        w_stack.close()
        p1_stack = ExitStack()
        xg = sbuf(p1_stack, "xg", [P, 4, CPS, DM])
        x1g = sbuf(p1_stack, "x1g", [P, 2, CPS, DM])
        xTs = sbuf(p1_stack, "xTs", [P, 2, 2, KT, SEQ], fp16)
        bst = sbuf(p1_stack, "bst", [P, CPS, 6])
        mv = sbuf(p1_stack, "mv", [P, CPS, 2])
        var2 = sbuf(p1_stack, "var2", [P, CPS, 2])
        rs2 = sbuf(p1_stack, "rs2", [P, CPS, 2])
        p1_stack.close()
        p2_stack = ExitStack()
        t = [sbuf(p2_stack, f"t{i}", [P, NCH * H]) for i in range(6)]
        csp = sbuf(p2_stack, "csp", [P, NCH, PARTS * H], bf16)
        csT = sbuf(p2_stack, "csT", [PARTS * H, TOK // 2], bf16)
        ohb = sbuf(p2_stack, "ohb", [P, NCH * E], bf16)
        keep = sbuf(p2_stack, "keep", [P, E, NCH])
        sm = sbuf(p2_stack, "sm", [P, 6, NCH])
        smi = sbuf(p2_stack, "smi", [P, E], i32)
        sx = sbuf(p2_stack, "sx", [P, 2, CPS, DM])
        idx = sbuf(p2_stack, "idx", [P, 2, CPS], i32)
        p2_stack.close()
        pre_stack.close()
        ffn_stack.close()

        xT = sbuf(ctx, "xT", [P, 2, 2, KT, SEQ], fp16)
        vraw = sbuf(ctx, "vraw", [P, XT, TAPS - 1 + SEQ])
        xc = sbuf(ctx, "xc", [P, 2, XT, SEQ])
        sz = sbuf(ctx, "sz", [P, 2, CPS, DI])
        Em = sbuf(ctx, "Em", [P, 2, H, P])
        xsT = sbuf(ctx, "xsT", [P, 2, DI])
        Xdt = sbuf(ctx, "Xdt", [P, 2, DI])
        Xw = sbuf(ctx, "Xw", [P, DI])
        xD = sbuf(ctx, "xD", [P, 2, DI])
        BT = sbuf(ctx, "BT", [P, NST])
        S = sbuf(ctx, "S", [P, DI])
        Sd = sbuf(ctx, "Sd", [P, DI])
        yo = sbuf(ctx, "yo", [P, DI])
        y = sbuf(ctx, "y", [P, 2, DI])
        ysq = sbuf(ctx, "ysq", [P, DI])
        ssq = sbuf(ctx, "ssq", [P, CPS])
        ms = sbuf(ctx, "ms", [P, CPS])
        rstd = sbuf(ctx, "rstd", [P, CPS])
        yT = sbuf(ctx, "yT", [P, ZT, P])
        xin = sbuf(ctx, "xin", [P, 2, CPS, DM])
        gin = sbuf(ctx, "gin", [P, 2, CPS, DM])
        gidx = sbuf(ctx, "gidx", [P, 2, CPS], i32)
        xn = sbuf(ctx, "xn", [P, CPS, DM])
        fo = sbuf(ctx, "fo", [P, 2, DM])
        ob = sbuf(ctx, "ob", [P, CPS, DM])
        csl = sbuf(ctx, "csl", [32, 2, SEQ], bf16)
        csr = sbuf(ctx, "csr", [32, 2, H, CPS, P], bf16)

        w_loaded, small_loaded, fw_loaded = sem("w_loaded"), sem("small_loaded"), [sem("fw_loaded0"), sem("fw_loaded1")]
        fb_loaded = sem("fb_loaded")
        const_ready, pstep = sem("const_ready"), sem("pool_setup_step")
        wtr_done, wtr_evac = sem("wtr_done"), sem("wtr_evac")
        wlink, bias_mm, nb_ready = sem("setup_vector_step"), sem("bias_mm"), sem("nb_ready")
        setup_done, zero_written, z_ready = sem("setup_done"), sem("zero_written"), sem("zeros_ready")
        x_loaded = [sem(f"x_loaded{r}") for r in range(4)]
        aggr_go, scatter_go, gather_go = sem("aggr_go"), sem("scatter_go"), sem("gather_go")
        stats, aggr, var_ready, rs_ready, x1_ready, xn_ready = (
            sem(n) for n in ("stats_done", "aggr_done", "var_ready", "rs_ready", "x1_ready", "xn_ready"))
        T_done, hi_ready, lo_ready, sc_done, sd_ready = (sem(n) for n in ("T_done", "hi_ready", "lo_ready", "sc_done", "sd_ready"))
        xT_stored = [sem(f"xT_stored{r}") for r in range(2)]
        vstep, softexp_in, softexp_out, a_ready, cs_mm, cs_copied, exps_done = (sem(n) for n in (
            "vstep", "softexp_in", "softexp_out", "a_ready", "cs_mm", "cs_copied", "exps_done"))
        csp_ready, csT_done, csT_evac, cs_stored = (sem(n) for n in ("csp_ready", "csT_done", "csT_evac", "cs_stored"))
        oh_ready, rank_mm, pos_ready = (sem(n) for n in ("oh_ready", "rank_mm", "pos_ready"))
        sx_ready, idx_ready = sem("sx_ready"), sem("idx_ready")
        scattered = [sem(f"scattered{r}") for r in range(2)]
        ft_loaded = [sem(f"ft_loaded{r}") for r in range(4)]
        fT_done, fhi, flo, fmm, fsilu = (sem(n) for n in ("fT_done", "ffn_hi", "ffn_lo", "ffn_mm", "ffn_silu"))
        g_stored = [sem(f"g_stored{r}") for r in range(4)]
        main_const = sem("main_const")
        xT_loaded = [sem(f"xT_loaded{b}") for b in range(2)]
        cs_loaded = [sem(f"cs_loaded{b}") for b in range(2)]
        xin_loaded = [sem(f"xin_loaded{b}") for b in range(2)]
        g_loaded = [sem(f"g_loaded{b}") for b in range(2)]
        inproj_done, inproj_evac, tap0, conv_step, xc_ready, sz_ready = (sem(n) for n in (
            "inproj_done", "inproj_evac", "tap0_ready", "conv_step", "xc_ready", "sz_ready"))
        xsT_done, xsT_evac, L_done, exp_done, B_done, B_evac, G_done = (sem(n) for n in (
            "xsT_done", "xsT_evac", "L_done", "exp_done", "B_done", "B_evac", "G_done"))
        yoff_done, yd_done, snew_done, yT_done, yT_evac, o_done = (sem(n) for n in (
            "yoff_done", "yd_done", "snew_done", "yT_done", "yT_evac", "o_done"))
        X_ready, M_ready, yo_ready, y_raw, S_ready, fin_step = (sem(n) for n in (
            "X_ready", "M_ready", "yo_ready", "y_raw", "S_ready", "fin_step"))
        Xw_ready, xD_ready, Sd_ready, yoD_ready, gated, sq_done, ms_ready, rstd_ready, gidx_ready, xn_done = (sem(n) for n in (
            "Xw_ready", "xD_ready", "Sd_ready", "yoD_ready", "gated", "sq_done", "ms_ready", "rstd_ready", "gidx_ready", "xn_done"))
        out_stored = sem("out_stored")

        NW = 11
        wcols = [(i * P, min(P, DPROJ - i * P)) for i in range(NW)]
        N_SMALL = 16 * 11

        block = ctx.enter_context(nc.Block())

        @block.sync
        def _(sp):
            sp.dma_start(wrow[:, 0:10, :], in_proj_w[0:10 * P, :].rearrange("(m p) d -> p m d", p=P)).then_inc(w_loaded, 16)
            sp.dma_start(wrow[0:H, 10, :], in_proj_w[10 * P:DPROJ, :]).then_inc(w_loaded, 16)
            sp.dma_start(worow[:, :, :], out_proj_w.rearrange("(m p) c -> p m c", p=P)).then_inc(w_loaded, 16)
            sp.dma_start(sig[0:E, :], tile_sigs).then_inc(w_loaded, 16)
            with nc.allow_non_contiguous_dma(reason="small vectors by channel"):
                sp.dma_start(nwb[:, 0, :], norm_w.rearrange("(k p) -> p k", p=P)).then_inc(small_loaded, 16)
                sp.dma_start(nwb[:, 1, :], norm_b.rearrange("(k p) -> p k", p=P)).then_inc(small_loaded, 16)
                sp.dma_start(rmsw[:, :], rms_w.rearrange("(k p) -> p k", p=P)).then_inc(small_loaded, 16)
                sp.dma_start(cw[:, :, :], conv_w.rearrange("(m p) t -> p m t", p=P)).then_inc(small_loaded, 16)
                sp.dma_start(cb[:, :], conv_b.rearrange("(m p) -> p m", p=P)).then_inc(small_loaded, 16)
                sp.dma_start(dtb[:, :], dt_bias.partition_broadcast(P)).then_inc(small_loaded, 16)
                sp.dma_start(a_bc[:, :], A_log.partition_broadcast(P)).then_inc(small_loaded, 16)
                sp.dma_start(D_bc[:, :], D.partition_broadcast(P)).then_inc(small_loaded, 16)
            for k in range(KT):
                if k:
                    sp.wait_ge(wlink, 2)
                sp.dma_start(fstage[:, :, :], ffn_W[:, k * P:(k + 1) * P, :].rearrange("e p d -> p e d")).then_inc(fw_loaded[k], 16)
            sp.wait_ge(wlink, 4)
            sp.dma_start(fstage[0:64, :, :], ffn_b.partition_broadcast(64)).then_inc(fb_loaded, 16)
            sp.wait_ge(z_ready, 1)
            for n in range(FT // 4):
                sp.dma_start(sorted_d[n * 4 * P:(n + 1) * 4 * P, :].rearrange("(p c) d -> p (c d)", p=P), zrow[:, :]).then_inc(zero_written, 16)
            sp.wait_ge(setup_done, 2)
            for r in range(4):
                sp.dma_start(xg[:, r, :, :], x_g[r]).then_inc(x_loaded[r], 16)

            def first_pass(q, more):
                for r in range(4):
                    j = 4 * q + r
                    sp.wait_ge(xn_ready, j + 1)
                    if more:
                        sp.dma_start(xg[:, r, :, :], x_g[j + 4]).then_inc(x_loaded[r], 16)
                    sp.wait_ge(lo_ready, j + 1)
                    sp.dma_start(xT_d[j], xTs[:, r % 2, :, :, :].rearrange("p a k t -> p (a k t)")).then_inc(xT_stored[r % 2], 16)

            with sp.Fori(0, 3) as q:
                first_pass(q, True)
            first_pass(3, False)
            for half in range(2):
                sp.wait_ge(csT_evac, 4 * (half + 1))
                sp.dma_start(cs_d[:, half * TOK // 2:(half + 1) * TOK // 2], csT[:, :]).then_inc(cs_stored, 16)
                sp.wait_ge(cs_stored, 16 * (half + 1))
            for b in range(2):
                sp.wait_ge(scattered[b], 16 * CPS * SEQS // 2)
            for r in range(4):
                sp.dma_start(ft[:, r, :], sorted_d[r * P:(r + 1) * P, :]).then_inc(ft_loaded[r], 16)

            def expert_io(q, more):
                for r in range(4):
                    n = 4 * q + r
                    if more:
                        sp.wait_ge(fT_done, n + 1)
                        sp.dma_start(ft[:, r, :], sorted_d.rearrange("(n p) d -> n p d", p=P)[n + 4]).then_inc(ft_loaded[r], 16)
                    sp.wait_ge(fsilu, n + 1)
                    sp.dma_start(gate_d.rearrange("(n p) d -> n p d", p=P)[n], gt[:, r, :]).then_inc(g_stored[r], 16)

            with sp.Fori(0, FT // 4 - 1) as q:
                expert_io(q, True)
            expert_io(FT // 4 - 1, False)
            for r in range(4):
                sp.wait_ge(g_stored[r], 16 * (FT // 4))
            for b in range(2):
                sp.wait_ge(xT_stored[b], 16 * (SEQS // 2 + 1))
            sp.wait_ge(main_const, 3)

            def load_seq(s, b):
                sp.dma_start(xT[:, b, :, :, :].rearrange("p a k t -> p (a k t)"), xT_d[s]).then_inc(xT_loaded[b], 16)

            def load_rest(s, b):
                sp.dma_start(xin[:, b, :, :], x_g[s]).then_inc(xin_loaded[b], 16)
                src = cs_d.rearrange("r (s t) -> s r t", t=SEQ)[s]
                sp.dma_start(csl[0:PARTS * H, b, :], src).then_inc(cs_loaded[b], 16)
                sp.dma_start(csr[PARTS * H:PARTS * (H + 1), b, :, :, :].rearrange("o h c l -> o h (c l)"),
                             src.rearrange("(o h) t -> o h t", h=H)).then_inc(cs_loaded[b], 16)

            load_seq(0, 0)
            load_rest(0, 0)
            load_seq(1, 1)

            def main_io(s, b, first, last):
                if not last:
                    if not first:
                        sp.wait_ge(fin_step, 12 * s)
                    load_rest(s + 1, 1 - b)
                    sp.wait_ge(inproj_done, 10 * (s + 1))
                    if not isinstance(s, int) or s < SEQS - 2:
                        load_seq(s + 2, b)
                if not first:
                    sp.wait_ge(fin_step, 12 * s)
                    sp.dma_start(out_g[s - 1], ob[:, :, :]).then_inc(out_stored, 16)

            main_io(0, 0, True, False)
            with sp.Fori(0, SEQS // 2 - 2) as p:
                main_io(2 * p + 1, 1, False, False)
                main_io(2 * p + 2, 0, False, False)
            main_io(SEQS - 3, 1, False, False)
            main_io(SEQS - 2, 0, False, False)
            main_io(SEQS - 1, 1, False, True)
            sp.wait_ge(fin_step, 12 * SEQS)
            sp.dma_start(out_g[SEQS - 1], ob[:, :, :]).then_inc(out_stored, 16)
            sp.wait_ge(out_stored, 16 * SEQS)

        @block.gpsimd
        def _(pool):
            steps = [0]

            def link(ins):
                steps[0] += 1
                ins.then_inc(pstep, 1)
                pool.wait_ge(pstep, steps[0])

            pool.memset(zrow[:, :], 0.0).then_inc(z_ready, 1)
            pool.memset(ident[:, :], 0.0)
            pool.memset(tri[:, :], 1.0)
            pool.memset(suf[:, :], 1.0)
            pool.memset(ones[:, :], 1.0)
            pool.memset(ones_b[:, :], 1.0)
            pool.memset(stri_b[:, :], 1.0)
            pool.memset(maskneg[:, :], 0.0)
            pool.memset(mhalf[:, :], -0.5)
            pool.memset(epsc[:, :], EPS)
            pool.memset(blk[:, :, :], 0.0)
            pool.memset(pick[:, :], 0.0)
            pool.memset(zbias[:, :], 0.0)
            pool.memset(fb[:, :, :], 0.0)
            link(pool.memset(mlo[:, :, :], 0.0))
            link(pool.memset(pick[0:1, :], 1.0))
            link(pool.memset(pick[32:33, :], 1.0))
            pool.affine_select(out=ident[:, :], in_=ident[:, :], compare_op=ALU.not_equal, fill=1.0, base=0,
                               pattern=[[-1, P]], channel_multiplier=1)
            pool.affine_select(out=tri[:, :], in_=tri[:, :], compare_op=ALU.is_ge, fill=0.0, base=0,
                               pattern=[[1, P]], channel_multiplier=-1)
            pool.affine_select(out=suf[:, :], in_=suf[:, :], compare_op=ALU.is_gt, fill=0.0, base=0,
                               pattern=[[-1, P]], channel_multiplier=1)
            pool.affine_select(out=stri_b[:, :], in_=stri_b[:, :], compare_op=ALU.is_gt, fill=0.0, base=0,
                               pattern=[[1, P]], channel_multiplier=-1)
            pool.affine_select(out=maskneg[:, :], in_=maskneg[:, :], compare_op=ALU.is_ge, fill=-1e30, base=0,
                               pattern=[[1, P]], channel_multiplier=-1)
            link(pool.iota(rev[:, :], pattern=[[-1, E]], base=E, channel_multiplier=0, allow_small_or_imprecise_dtypes=True))
            for part in range(PARTS):
                link(pool.affine_select(out=blk[:, :, :], in_=blk[:, :, :], compare_op=ALU.not_equal, fill=-1.0, base=-part * H,
                                        pattern=[[-1, H], [0, P]], channel_multiplier=1))
            pool.tensor_copy(ident_b[:, :], ident[:, :]).then_inc(const_ready, 1)
            def roots(q):
                for r in range(4):
                    pool.wait_ge(var_ready, 4 * q + r + 1)
                    pool.tensor_tensor(rs2[:, :, :], var2[:, :, :], mhalf[:, :].rearrange("p (c k) -> p c k", k=2), ALU.pow).then_inc(rs_ready, 1)

            with pool.Fori(0, 4) as q:
                roots(q)
            pool.wait_ge(sd_ready, SEQS)
            for b in range(2):
                pool.wait_ge(xT_stored[b], 16 * (SEQS // 2 + 1))
            pool.memset(keep[:, :, :], 1.0)
            link(pool.iota(t[5][:, 0:FT], pattern=[[1, FT]], base=0, channel_multiplier=0, allow_small_or_imprecise_dtypes=True))
            pool.memset(keep[:, :, 0:1], 0.0).then_inc(const_ready, 1)
            def scatter(q):
                for r in range(2):
                    pool.wait_ge(zero_written, 16 * (FT // 4))
                    pool.wait_ge(sx_ready, 2 * q + r + 1)
                    pool.wait_ge(idx_ready, 2 * q + r + 1)
                    pool.sem_inc(scatter_go, 1)
                    for c in range(CPS):
                        pool.indirect_dma_start(out=sorted_d, out_offset=bass.IndirectOffsetOnAxis(ap=idx[:, r, c:c + 1], axis=0),
                                                in_=sx[:, r, c, :], in_offset=None).then_inc(scattered[r], 16)

            with pool.Fori(0, SEQS // 2) as q:
                scatter(q)
            for r in range(4):
                pool.wait_ge(g_stored[r], 16 * (FT // 4))
            pool.wait_ge(cs_stored, 32)
            pool.memset(vraw[:, :, 0:TAPS - 1], 0.0).then_inc(main_const, 1)
            pool.memset(csl[:, :, :], 1.0).then_inc(main_const, 1)
            def gather(s, b, first):
                if not first:
                    pool.wait_ge(fin_step, 12 * (s - 1))
                pool.tensor_copy(gidx[:, b, :], pos_all[:, bass.ts(s, CPS)]).then_inc(gidx_ready, 1)
                pool.wait_ge(gidx_ready, s + 1)
                pool.sem_inc(gather_go, 1)
                for c in range(CPS):
                    pool.indirect_dma_start(out=gin[:, b, c, :], out_offset=None, in_=gate_d,
                                            in_offset=bass.IndirectOffsetOnAxis(ap=gidx[:, b, c:c + 1], axis=0)).then_inc(g_loaded[b], 16)

            def main(s, b, first, second):
                gather(s, b, first or second)
                for c in range(CPS):
                    n = 4 * s + c
                    hb = lambda a: a.unsqueeze(2).to_broadcast([P, H, HD])
                    xs3 = xsT[:, c % 2, :].rearrange("p (h d) -> p h d", d=HD)
                    pool.wait_ge(xsT_evac, n + 1)
                    pool.tensor_tensor(xD[:, c % 2, :].rearrange("p (h d) -> p h d", d=HD), xs3, hb(D_bc[:, :]), ALU.mult).then_inc(xD_ready, 1)
                    if c < CPS - 1:
                        pool.tensor_tensor(Xw[:, :].rearrange("p (h d) -> p h d", d=HD), xs3, hb(w_of(w_all, n)), ALU.mult).then_inc(Xw_ready, 1)
                    if c in (1, 2):
                        pool.wait_ge(S_ready, 3 * s + c)
                        pool.tensor_tensor(Sd[:, :].rearrange("p (h d) -> p h d", d=HD), S[:, :].rearrange("p (h d) -> p h d", d=HD),
                                           hb(w_of(tot_all, n)), ALU.mult).then_inc(Sd_ready, 1)
                    if c > 0:
                        pool.wait_ge(yo_ready, 3 * s + c)
                        pool.wait_ge(xD_ready, n + 1)
                        pool.tensor_tensor(yo[:, :], yo[:, :], xD[:, c % 2, :], ALU.add).then_inc(yoD_ready, 1)
                    pool.wait_ge(y_raw, n + 1)
                    if c == 0:
                        pool.wait_ge(sz_ready, s + 1)
                    pool.tensor_tensor(y[:, c % 2, :], y[:, c % 2, :], sz[:, b, c, :], ALU.mult).then_inc(gated, 1)
                    pool.wait_ge(sq_done, n + 1)
                    pool.tensor_tensor(ms[:, c:c + 1], ssq[:, c:c + 1], epsc[:, :], ALU.add).then_inc(ms_ready, 1)
                    pool.wait_ge(ms_ready, n + 1)
                    pool.tensor_tensor(rstd[:, c:c + 1], ms[:, c:c + 1], mhalf[:, 0:1], ALU.pow).then_inc(rstd_ready, 1)

            main(0, 0, True, False)
            main(1, 1, False, True)
            with pool.Fori(1, SEQS // 2) as p:
                main(2 * p, 0, False, False)
                main(2 * p + 1, 1, False, False)

        @block.scalar
        def _(act):
            n = 0
            for k in range(KT):
                for m, (c0, cn) in enumerate(wcols):
                    act.wait_ge(wtr_done, n + 1)
                    act.activation(wT[:, k, c0:c0 + cn], bank[n % 2][:, 0:cn], ACT.Copy).then_inc(wtr_evac, 1)
                    n += 1
            act.wait_ge(small_loaded, 16 * 8)
            for kc in range(ZT):
                act.wait_ge(wtr_done, n + 1)
                act.activation(wo[:, kc, :], bank[n % 2][:, 0:DM], ACT.Identity, scale=rmsw[:, kc:kc + 1]).then_inc(wtr_evac, 1)
                n += 1
            act.wait_ge(wtr_done, n + 1)
            act.activation(neg[:, :, :], bank[n % 2][:, 0:KT * E].rearrange("p (k e) -> p k e", e=E), ACT.Copy).then_inc(wtr_evac, 1)
            act.activation(a_bc[:, :], a_bc[:, :], ACT.Exp).then_inc(setup_done, 1)

            def highs(q):
                for r in range(4):
                    j = 4 * q + r
                    act.wait_ge(T_done, j + 1)
                    act.wait_ge(xT_stored[r % 2], 16 * (2 * q + r // 2 + 1))
                    for k in range(KT):
                        act.activation(xTs[:, r % 2, 0, k, :], bank[2 * (r % 2) + k][:, :], ACT.Copy).then_inc(hi_ready, 1)

            act.sem_inc(xT_stored[0], 16)
            act.sem_inc(xT_stored[1], 16)
            with act.Fori(0, 4) as q:
                highs(q)
            act.wait_ge(softexp_in, 1)
            act.activation(t[1][:, :], t[1][:, :], ACT.Exp).then_inc(softexp_out, 1)
            act.wait_ge(cs_copied, 1)
            act.activation(ea_all[:, :, :].rearrange("p c h -> p (c h)"), t[2][:, :], ACT.Exp).then_inc(exps_done, 1)
            act.activation(tot_all[:, :, :].rearrange("p c h -> p (c h)"), bank[1][:, :], ACT.Exp).then_inc(exps_done, 1)
            act.activation(w_all[:, :, :].rearrange("p c h -> p (c h)"), bank[2][:, :], ACT.Exp).then_inc(exps_done, 1)
            for g in range(8):
                act.wait_ge(csT_done, g + 1)
                if g == 4:
                    act.wait_ge(cs_stored, 16)
                act.activation(csT[:, (g % 4) * 1024:(g % 4 + 1) * 1024],
                               bank[3 + g % 2][0:PARTS * H, :].bitcast(bf16), ACT.Copy).then_inc(csT_evac, 1)

            def rows(q, first):
                for r in range(2):
                    if not first:
                        act.wait_ge(scattered[r], 16 * CPS * q)
                    act.activation(sx[:, r, :, :].rearrange("p c d -> p (c d)"),
                                   xn_all[:, bass.ts(2 * q + r, CPS), :].rearrange("p c d -> p (c d)"), ACT.Copy).then_inc(sx_ready, 1)

            rows(0, True)
            with act.Fori(1, SEQS // 2) as q:
                rows(q, False)

            def split_hi(n, r):
                act.wait_ge(fT_done, n + 1)
                act.activation(fxT[:, r % 2, 0, :, :], bank[r % 2][:, 0:DM].rearrange("p (k t) -> p k t", k=KT), ACT.Copy).then_inc(fhi, 1)

            def experts(q, more, first):
                for r in range(4):
                    n = 4 * q + r
                    if more or r < 3:
                        split_hi(n + 1, (r + 1) % 4)
                    act.wait_ge(fmm, n + 1)
                    if not first:
                        act.wait_ge(g_stored[r], 16 * q)
                    act.activation(gt[:, r, :], bank[2 + r % 2][:, 0:DM], ACT.Silu, scale=1.0 / WS).then_inc(fsilu, 1)

            split_hi(0, 0)
            experts(0, True, True)
            with act.Fori(1, FT // 4 - 1) as q:
                experts(q, True, False)
            experts(FT // 4 - 1, False, False)
            act.wait_ge(main_const, 3)
            for r in range(4):
                act.wait_ge(g_stored[r], 16 * (FT // 4))

            def evac(s, b, u, first):
                act.wait_ge(inproj_done, 10 * s + u + 1)
                if u < XT:
                    if u == 0 and not first:
                        act.wait_ge(conv_step, 18 * s)
                    act.activation(vraw[:, u, TAPS - 1:], bank[u % 2][:, :], ACT.Identity, bias=xbias[:, u:u + 1], scale=1.0 / WS).then_inc(inproj_evac, 1)
                    act.wait_ge(inproj_evac, 10 * s + u + 1)
                    act.activation(xc[:, b, u, :], vraw[:, u, TAPS - 1:], ACT.Identity, bias=cb[:, u:u + 1],
                                   scale=cw[:, u, TAPS - 1:TAPS]).then_inc(tap0, 1)
                else:
                    act.activation(sz[:, b, u - XT, :], bank[u % 2][:, :], ACT.Copy, scale=1.0 / WS).then_inc(inproj_evac, 1)

            def silus(s, b):
                act.wait_ge(conv_step, 18 * (s + 1))
                act.activation(xc[:, b, :, :], xc[:, b, :, :], ACT.Silu).then_inc(xc_ready, 1)
                act.wait_ge(inproj_evac, 10 * (s + 1))
                act.activation(sz[:, b, :, :], sz[:, b, :, :], ACT.Silu).then_inc(sz_ready, 1)

            def yT_out(n):
                act.wait_ge(yT_done, n + 1)
                act.activation(yT[:, :, :].rearrange("p k t -> p (k t)"), bank[5][:, :], ACT.Copy).then_inc(yT_evac, 1)

            def main(s, b, first, last):
                for c in range(CPS):
                    n = 4 * s + c
                    act.wait_ge(xsT_done, n + 1)
                    act.activation(xsT[:, c % 2, :], bank[2][:, :], ACT.Copy).then_inc(xsT_evac, 1)
                    if c == 1:
                        if not first:
                            act.wait_ge(fin_step, 12 * s)
                        act.wait_ge(xin_loaded[b], 8 * (s - b) + 16)
                        for cc in range(CPS):
                            act.activation(xn[:, cc, :], xin[:, b, cc, :], ACT.Identity, bias=st_of(norm_st, 4 * s + cc, 1),
                                           scale=st_of(norm_st, 4 * s + cc, 0)).then_inc(xn_done, 1)
                    act.wait_ge(L_done, n + 1)
                    act.activation(Em[:, c % 2, :, :].rearrange("p h l -> p (h l)"), bankL[:, :], ACT.Exp).then_inc(exp_done, 1)
                    act.wait_ge(B_done, n + 1)
                    act.activation(BT[:, :], bank[4][:, 0:NST], ACT.Copy).then_inc(B_evac, 1)
                    if not (first and c == 0):
                        yT_out(n - 1)
                    if not last:
                        for u in ((0, 1, 2), (3, 4, 5), (6, 7), (8, 9))[c]:
                            evac(s + 1, 1 - b, u, False)
                    act.wait_ge(gated, n + 1)
                    act.activation(ysq[:, :], y[:, c % 2, :], ACT.Square, scale=float(DI ** -0.5), accum_out=ssq[:, c:c + 1]).then_inc(sq_done, 1)
                if not last:
                    silus(s + 1, 1 - b)

            for u in range(XT + CPS):
                evac(0, 0, u, True)
            silus(0, 0)
            main(0, 0, True, False)
            with act.Fori(0, SEQS // 2 - 1) as p:
                main(2 * p + 1, 1, False, False)
                main(2 * p + 2, 0, False, False)
            main(SEQS - 1, 1, False, True)
            yT_out(NCH - 1)

        @block.vector
        def _(dve):
            steps = [0]

            def wl(ins):
                steps[0] += 1
                ins.then_inc(wlink, 1)
                dve.wait_ge(wlink, steps[0])

            for k in range(KT):
                dve.wait_ge(fw_loaded[k], 16)
                wl(nc.vector.tensor_scalar(fw[:, 0, k, :, :], fstage[:, :, :], WS, None, ALU.mult))
                wl(nc.vector.scalar_tensor_tensor(fw[:, 1, k, :, :].rearrange("p e d -> p (e d)"), fstage[:, :, :].rearrange("p e d -> p (e d)"),
                                                  WS, fw[:, 0, k, :, :].rearrange("p e d -> p (e d)"), ALU.mult, ALU.subtract))
            dve.wait_ge(const_ready, 1)
            dve.wait_ge(fb_loaded, 16)
            f2 = lambda a: a.rearrange("p e d -> p (e d)")
            wl(nc.vector.tensor_scalar(f2(fb[0:64, :, :]), f2(fstage[0:64, :, :]), WS, None, ALU.mult))
            wl(nc.vector.scalar_tensor_tensor(f2(fb[32:64, :, :]), f2(fstage[32:64, :, :]), WS, f2(fb[32:64, :, :]), ALU.mult, ALU.subtract))
            dve.wait_ge(small_loaded, 16 * 8)
            for k in range(KT):
                last = nc.vector.tensor_scalar(nbrep[:, k, :], ones[:, :], nwb[:, 1, k:k + 1], WS, ALU.mult, ALU.mult)
            last.then_inc(nb_ready, 1)
            wl(nc.vector.tensor_scalar(nw64[:, :], nwb[:, 0, :], WS, None, ALU.mult))
            dve.wait_ge(wtr_evac, 2 * NW)
            for k in range(KT):
                wl(nc.vector.tensor_scalar(wz[:, 0, k, :], wT[:, k, :], nw64[:, k:k + 1], None, ALU.mult))
                wl(nc.vector.scalar_tensor_tensor(wz[:, 1, k, :], wT[:, k, :], nw64[:, k:k + 1], wz[:, 0, k, :], ALU.mult, ALU.subtract))
            dve.wait_ge(wtr_evac, 2 * NW + ZT + 1)
            wl(nc.vector.tensor_scalar(mhi[:, :, 0:E], neg[:, :, :], 0.0, None, ALU.is_gt))
            wl(nc.vector.tensor_scalar(neg[:, :, :], neg[:, :, :], 0.0, None, ALU.is_lt))
            wl(nc.vector.tensor_tensor(mhi[:, :, 0:E], mhi[:, :, 0:E], neg[:, :, :], ALU.subtract))
            wl(nc.vector.tensor_copy(mhi[:, :, E:2 * E], wz[:, 0, :, DPROJ - H:DPROJ]))
            wl(nc.vector.tensor_copy(mlo[:, :, E:2 * E], wz[:, 1, :, DPROJ - H:DPROJ]))
            dve.wait_ge(bias_mm, 1)
            wl(nc.vector.tensor_copy(zbias[0:64, :], bank[2][0:64, :]))
            wl(nc.vector.tensor_tensor(zbias[32:64, :], bank[2][32:64, :], zbias[32:64, :], ALU.subtract))
            wl(nc.vector.tensor_copy(xbias[:, :], bank[3][:, 0:XT]))
            wl(nc.vector.scalar_tensor_tensor(dtb[:, :], bank[4][:, 0:H], 1.0 / WS, dtb[:, :], ALU.mult, ALU.add))
            dve.wait_ge(setup_done, 1)
            nc.vector.tensor_scalar(a_bc[:, :], a_bc[:, :], -1.0, None, ALU.mult).then_inc(setup_done, 1)

            def norm(q):
                for r in range(4):
                    j = 4 * q + r
                    dve.wait_ge(x_loaded[r], 16 * (q + 1))
                    for c in range(CPS):
                        last = nc.vector.bn_stats(bst[:, c, :], xg[:, r, c, :])
                    last.then_inc(stats, 1)
                    dve.wait_ge(stats, j + 1)
                    dve.sem_inc(aggr_go, 1)
                    for c in range(CPS):
                        last = nc.vector.bn_aggr(mv[:, c, :], bst[:, c, :])
                    last.then_inc(aggr, 1)
                    dve.wait_ge(aggr, j + 1)
                    nc.vector.tensor_scalar(var2[:, :, 0:1], mv[:, :, 1:2], EPS, None, ALU.add)
                    nc.vector.tensor_scalar(var2[:, :, 1:2], mv[:, :, 1:2], 1.0 + EPS, EPS * EPS, ALU.mult, ALU.add).then_inc(var_ready, 1)
                    dve.wait_ge(rs_ready, j + 1)
                    for c in range(CPS):
                        last = nc.vector.tensor_scalar(x1g[:, r % 2, c, :], xg[:, r, c, :], mv[:, c, 0:1], rs2[:, c, 1:2], ALU.subtract, ALU.mult)
                    last.then_inc(x1_ready, 1)
                    nc.vector.tensor_copy(norm_st[:, bass.ts(j, CPS), 0:1], rs2[:, :, 0:1])
                    nc.vector.scalar_tensor_tensor(norm_st[:, bass.ts(j, CPS), 1:2], mv[:, :, 0:1], -1.0, rs2[:, :, 0:1], ALU.mult, ALU.mult)
                    for c in range(CPS):
                        last = nc.vector.tensor_scalar(row_of(xn_all, 4 * j + c), xg[:, r, c, :], mv[:, c, 0:1], rs2[:, c, 0:1], ALU.subtract, ALU.mult)
                    last.then_inc(xn_ready, 1)
                    dve.wait_ge(hi_ready, 2 * (j + 1))
                    for k in range(KT):
                        last = nc.vector.tensor_tensor(xTs[:, r % 2, 1, k, :], bank[2 * (r % 2) + k][:, :], xTs[:, r % 2, 0, k, :], ALU.subtract)
                    last.then_inc(lo_ready, 1)
                    dve.wait_ge(sc_done, j + 1)
                    nc.vector.tensor_copy(sd_all[:, bass.ts(j, CPS), :], bankL[:, (r % 2) * 512:(r % 2) * 512 + CPS * 2 * H].rearrange(
                        "p (c k) -> p c k", k=2 * H)).then_inc(sd_ready, 1)

            with dve.Fori(0, 4) as q:
                norm(q)

            vs = [0]

            def link(ins):
                vs[0] += 1
                ins.then_inc(vstep, 1)
                dve.wait_ge(vstep, vs[0])

            c3 = lambda a: a.rearrange("p (c h) -> p c h", h=H)
            bc = lambda a: a.unsqueeze(1).to_broadcast([P, NCH, H])
            dve.wait_ge(sd_ready, SEQS)
            for b in range(2):
                dve.wait_ge(xT_stored[b], 16 * (SEQS // 2 + 1))
            link(nc.vector.tensor_scalar(c3(t[0][:, :]), sd_all[:, :, H:2 * H], 1.0 / WS, None, ALU.mult))
            link(nc.vector.tensor_tensor(c3(t[0][:, :]), c3(t[0][:, :]), bc(dtb[:, :]), ALU.add))
            nc.vector.scalar_tensor_tensor(t[1][:, :], t[0][:, :], -1.0, t[0][:, :], ALU.mult, ALU.min).then_inc(softexp_in, 1)
            dve.wait_ge(softexp_out, 1)
            link(nc.vector.tensor_scalar(t[2][:, :], t[1][:, :], 2.0, None, ALU.add))
            link(nc.vector.reciprocal(t[2][:, :], t[2][:, :]))
            link(nc.vector.tensor_tensor(t[1][:, :], t[1][:, :], t[2][:, :], ALU.mult))
            link(nc.vector.tensor_tensor(t[2][:, :], t[1][:, :], t[1][:, :], ALU.mult))
            link(nc.vector.tensor_scalar(t[3][:, :], t[2][:, :], 1.0 / 15, None, ALU.mult))
            for k in (13, 11, 9, 7, 5, 3):
                link(nc.vector.scalar_tensor_tensor(t[3][:, :], t[3][:, :], 1.0 / k, t[2][:, :], ALU.add, ALU.mult))
            link(nc.vector.scalar_tensor_tensor(t[3][:, :], t[3][:, :], 1.0, t[1][:, :], ALU.add, ALU.mult))
            link(nc.vector.tensor_scalar(t[0][:, :], t[0][:, :], 0.0, None, ALU.max))
            link(nc.vector.scalar_tensor_tensor(dt_all[:, :, :].rearrange("p c h -> p (c h)"), t[3][:, :], 2.0, t[0][:, :], ALU.mult, ALU.add))
            nc.vector.tensor_tensor(c3(t[0][:, :]), dt_all[:, :, :], bc(a_bc[:, :]), ALU.mult).then_inc(a_ready, 1)
            dve.wait_ge(cs_mm, 1)
            nc.vector.tensor_copy(t[2][:, :], bank[0][:, :]).then_inc(cs_copied, 1)
            dve.wait_ge(cs_copied, 1)
            top = -65536
            part = lambda k: csp[:, :, k * H:(k + 1) * H]
            link(nc.vector.tensor_scalar(t[3][:, :].bitcast(i32), t[2][:, :].bitcast(i32), top, None, ALU.bitwise_and))
            nc.vector.tensor_copy(part(0), c3(t[3][:, :]))
            link(nc.vector.tensor_tensor(t[3][:, :], t[2][:, :], t[3][:, :], ALU.subtract))
            link(nc.vector.tensor_scalar(t[4][:, :].bitcast(i32), t[3][:, :].bitcast(i32), top, None, ALU.bitwise_and))
            nc.vector.tensor_copy(part(1), c3(t[4][:, :]))
            nc.vector.tensor_tensor(part(2), c3(t[3][:, :]), c3(t[4][:, :]), ALU.subtract).then_inc(csp_ready, 1)
            dve.wait_ge(exps_done, 3)
            link(nc.vector.tensor_tensor(w_all[:, :, :], w_all[:, :, :], dt_all[:, :, :], ALU.mult))
            sc = sd_all[:, :, 0:E]
            big = lambda a: a.unsqueeze(2).to_broadcast([P, NCH, E])
            link(nc.vector.tensor_reduce(sm[:, 0, :], sc, AX.X, ALU.max))
            link(nc.vector.tensor_tensor(c3(t[0][:, :]), sc, big(sm[:, 0, :]), ALU.is_ge))
            link(nc.vector.tensor_tensor(c3(t[0][:, :]), c3(t[0][:, :]), bc(rev[:, :]), ALU.mult))
            link(nc.vector.tensor_reduce(sm[:, 1, :], c3(t[0][:, :]), AX.X, ALU.max))
            nc.vector.tensor_tensor(c3(ohb[:, :]), c3(t[0][:, :]), big(sm[:, 1, :]), ALU.is_equal).then_inc(oh_ready, 1)
            dve.wait_ge(rank_mm, 1)
            dve.wait_ge(const_ready, 2)
            e3 = lambda a: a.rearrange("p (e c) -> p e c", c=NCH)
            ec = lambda a: a.rearrange("p (c e) -> p e c", e=E)
            link(nc.vector.tensor_copy(e3(t[1][:, :]), ec(bank[1][:, :])))
            link(nc.vector.tensor_tensor_scan(t[3][:, :], keep[:, :, :].rearrange("p e c -> p (e c)"), t[1][:, :], 0.0, ALU.mult, ALU.add))
            link(nc.vector.tensor_tensor(t[1][:, :], t[3][:, :], t[1][:, :], ALU.subtract))
            link(nc.vector.tensor_scalar(smi[:, :].unsqueeze(2), e3(t[3][:, :])[:, :, NCH - 1:NCH], float(P - 1), None, ALU.add))
            link(nc.vector.tensor_scalar(smi[:, :], smi[:, :], 7, None, ALU.arith_shift_right))
            link(nc.vector.tensor_copy(sm[:, 2, 0:E], smi[:, :]))
            link(nc.vector.tensor_tensor_scan(sm[:, 3, 0:E], ones[:, 0:E], sm[:, 2, 0:E], 0.0, ALU.mult, ALU.add))
            link(nc.vector.tensor_tensor(sm[:, 2, 0:E], sm[:, 3, 0:E], sm[:, 2, 0:E], ALU.subtract))
            link(nc.vector.tensor_scalar(sm[:, 2, 0:E], sm[:, 2, 0:E], float(P), None, ALU.mult))
            link(nc.vector.tensor_tensor(c3(t[0][:, :]), c3(bank[0][:, :]), e3(t[1][:, :]).rearrange("p e c -> p c e"), ALU.add))
            link(nc.vector.tensor_tensor(c3(t[0][:, :]), c3(t[0][:, :]), bc(sm[:, 2, 0:E]), ALU.add))
            link(nc.vector.tensor_tensor(t[0][:, :], t[0][:, :], ohb[:, :], ALU.mult))
            link(nc.vector.tensor_reduce(sm[:, 4, :], c3(t[0][:, :]), AX.X, ALU.add))
            link(nc.vector.tensor_copy(pos_all[:, :], sm[:, 4, :]))
            tv = t[3][:, 0:FT // 2 * E].rearrange("p (n e) -> p n e", e=E)
            for half in range(2):
                f0 = half * (FT // 2)
                link(nc.vector.tensor_tensor(tv, t[5][:, f0:f0 + FT // 2].unsqueeze(2).to_broadcast([P, FT // 2, E]),
                                             sm[:, 3, 0:E].unsqueeze(1).to_broadcast([P, FT // 2, E]), ALU.is_ge))
                link(nc.vector.tensor_reduce(t[4][:, f0:f0 + FT // 2], tv, AX.X, ALU.add))
            link(nc.vector.tensor_scalar(t[4][:, 0:FT], t[4][:, 0:FT], float(E - 1), None, ALU.min))
            nc.vector.tensor_copy(te[:, :], t[4][:, 0:FT]).then_inc(pos_ready, 1)

            def slots(q, first):
                for r in range(2):
                    if not first:
                        dve.wait_ge(scattered[r], 16 * CPS * q)
                    nc.vector.tensor_copy(idx[:, r, :], pos_all[:, bass.ts(2 * q + r, CPS)]).then_inc(idx_ready, 1)

            slots(0, True)
            with dve.Fori(1, SEQS // 2) as q:
                slots(q, False)

            def lows(q):
                for r in range(4):
                    n = 4 * q + r
                    dve.wait_ge(fhi, n + 1)
                    nc.vector.tensor_tensor(fxT[:, r % 2, 1, :, :], bank[r % 2][:, 0:DM].rearrange("p (k t) -> p k t", k=KT),
                                            fxT[:, r % 2, 0, :, :], ALU.subtract).then_inc(flo, 1)

            with dve.Fori(0, FT // 4) as q:
                lows(q)
            for r in range(4):
                dve.wait_ge(g_stored[r], 16 * (FT // 4))
            dve.wait_ge(cs_stored, 32)
            for b in range(2):
                last = nc.vector.tensor_copy(csr[0:PARTS * H, b, :, :, :], blk[:, :, :].unsqueeze(2).to_broadcast([PARTS * H, H, CPS, P]))
            last.then_inc(main_const, 1)

            def conv(s, b, g):
                for tap in range(1, TAPS):
                    for i in range(3):
                        m = 3 * g + i
                        if tap == 1:
                            dve.wait_ge(tap0, 6 * s + m + 1)
                        else:
                            dve.wait_ge(conv_step, 18 * s + 9 * g + 3 * (tap - 2) + i + 1)
                        nc.vector.scalar_tensor_tensor(xc[:, b, m, :], vraw[:, m, TAPS - 1 - tap:TAPS - 1 - tap + SEQ],
                                                       cw[:, m, TAPS - 1 - tap:TAPS - tap], xc[:, b, m, :], ALU.mult, ALU.add).then_inc(conv_step, 1)

            def finish(s, b, c):
                n = 4 * s + c
                i = c % 2
                dve.wait_ge(o_done, n + 1)
                dve.wait_ge(rstd_ready, n + 1)
                if c == 0:
                    dve.wait_ge(xn_done, 4 * (s + 1))
                    dve.wait_ge(g_loaded[b], 32 * (s - b) + 64)
                    dve.wait_ge(xin_loaded[b], 8 * (s - b) + 16)
                    if not (isinstance(s, int) and s == 0):
                        dve.wait_ge(out_stored, 16 * s)
                nc.vector.scalar_tensor_tensor(fo[:, i, :], bank[2][:, 0:DM], rstd[:, c:c + 1], xn[:, c, :], ALU.mult, ALU.add).then_inc(fin_step, 1)
                dve.wait_ge(fin_step, 3 * n + 1)
                nc.vector.tensor_tensor(fo[:, i, :], fo[:, i, :], gin[:, b, c, :], ALU.mult).then_inc(fin_step, 1)
                dve.wait_ge(fin_step, 3 * n + 2)
                nc.vector.tensor_tensor(ob[:, c, :], fo[:, i, :], xin[:, b, c, :], ALU.add).then_inc(fin_step, 1)

            def main(s, b, first, last):
                for c in range(CPS):
                    n = 4 * s + c
                    h3 = lambda a: a.rearrange("p (h d) -> p h d", d=HD)
                    hb = lambda a: a.unsqueeze(2).to_broadcast([P, H, HD])
                    dve.wait_ge(xsT_evac, n + 1)
                    if not (first and c < 2):
                        dve.wait_ge(yd_done, n - 1)
                    nc.vector.tensor_tensor(h3(Xdt[:, c % 2, :]), h3(xsT[:, c % 2, :]), hb(w_of(dt_all, n)), ALU.mult).then_inc(X_ready, 1)
                    dve.wait_ge(exp_done, n + 1)
                    dve.wait_ge(G_done, n + 1)
                    nc.vector.scalar_tensor_tensor(Em[:, c % 2, :, :], Em[:, c % 2, :, :], 1.0, bank[3][:, 0:P].unsqueeze(1).to_broadcast([P, H, P]),
                                                   ALU.min, ALU.mult).then_inc(M_ready, 1)
                    if not (first and c == 0):
                        if c == 0:
                            finish(s - 1, 1 - b, CPS - 1)
                        else:
                            finish(s, b, c - 1)
                    if c > 0:
                        dve.wait_ge(yoff_done, 3 * s + c)
                        nc.vector.tensor_tensor(h3(yo[:, :]), h3(bank[5][:, :]), hb(w_of(ea_all, n)), ALU.mult).then_inc(yo_ready, 1)
                    if not last:
                        if c in (1, 2):
                            conv(s + 1, 1 - b, c - 1)
                    dve.wait_ge(yd_done, n + 1)
                    if c > 0:
                        dve.wait_ge(yoD_ready, 3 * s + c)
                        nc.vector.tensor_tensor(y[:, c % 2, :], bank[4][:, :], yo[:, :], ALU.add).then_inc(y_raw, 1)
                    else:
                        dve.wait_ge(xD_ready, n + 1)
                        nc.vector.tensor_tensor(y[:, c % 2, :], bank[4][:, :], xD[:, c % 2, :], ALU.add).then_inc(y_raw, 1)
                    if c < CPS - 1:
                        dve.wait_ge(snew_done, 3 * s + c + 1)
                        if c == 0:
                            nc.vector.tensor_copy(S[:, :], bank[2][:, :]).then_inc(S_ready, 1)
                        else:
                            dve.wait_ge(Sd_ready, 2 * s + c)
                            nc.vector.tensor_tensor(S[:, :], bank[2][:, :], Sd[:, :], ALU.add).then_inc(S_ready, 1)

            conv(0, 0, 0)
            conv(0, 0, 1)
            main(0, 0, True, False)
            with dve.Fori(0, SEQS // 2 - 1) as p:
                main(2 * p + 1, 1, False, False)
                main(2 * p + 2, 0, False, False)
            main(SEQS - 1, 1, False, True)
            finish(SEQS - 1, 1, CPS - 1)

        @block.tensor
        def _(pe):
            mm, tr = nc.tensor.matmul, nc.tensor.transpose
            pe.wait_ge(const_ready, 1)
            pe.wait_ge(w_loaded, 64)
            n = 0
            for k in range(KT):
                for m, (c0, cn) in enumerate(wcols):
                    if n >= 2:
                        pe.wait_ge(wtr_evac, n - 1)
                    tr(bank[n % 2][:, 0:cn], wrow[0:cn, m, k * P:(k + 1) * P], ident[0:cn, 0:cn]).then_inc(wtr_done, 1)
                    n += 1
            for kc in range(ZT):
                pe.wait_ge(wtr_evac, n - 1)
                for m in range(KT):
                    last = tr(bank[n % 2][:, m * P:(m + 1) * P], worow[:, m, kc * P:(kc + 1) * P], ident[:, :])
                last.then_inc(wtr_done, 1)
                n += 1
            pe.wait_ge(wtr_evac, n - 1)
            for k in range(KT):
                last = tr(bank[n % 2][:, k * E:(k + 1) * E], sig[0:E, k * P:(k + 1) * P], ident[0:E, 0:E])
            last.then_inc(wtr_done, 1)
            pe.wait_ge(nb_ready, 1)
            pe.wait_ge(wtr_evac, 2 * NW)
            for k in range(KT):
                mm(bank[2][:, :], nbrep[:, k, :], wT[:, k, 0:DI], start=(k == 0), stop=(k == KT - 1))
            for m in range(XT):
                for k in range(KT):
                    mm(bank[3][:, m:m + 1], wT[:, k, DI + m * P:DI + (m + 1) * P], nwb[:, 1, k:k + 1], start=(k == 0), stop=(k == KT - 1))
            for k in range(KT):
                last = mm(bank[4][:, 0:H], nbrep[:, k, :], wT[:, k, DPROJ - H:DPROJ], start=(k == 0), stop=(k == KT - 1))
            last.then_inc(bias_mm, 1)
            pe.wait_ge(setup_done, 2)

            def first_pass(q):
                for r in range(4):
                    j = 4 * q + r
                    pe.wait_ge(x1_ready, j + 1)
                    for c in range(CPS):
                        for k in range(KT):
                            last = tr(bank[2 * (r % 2) + k][:, c * P:(c + 1) * P], x1g[:, r % 2, c, k * P:(k + 1) * P], ident[:, :])
                    last.then_inc(T_done, 1)
                    pe.wait_ge(lo_ready, j + 1)
                    for c in range(CPS):
                        o = (r % 2) * 512 + c * 2 * H
                        terms = [(xTs[:, r % 2, a, k, c * P:(c + 1) * P], w[:, k, :]) for k in range(KT) for a, w in ((0, mhi), (1, mhi), (0, mlo))]
                        for i, (lhs, rhs) in enumerate(terms):
                            last = mm(bankL[:, o:o + 2 * H], lhs, rhs, start=(i == 0), stop=(i == len(terms) - 1))
                    last.then_inc(sc_done, 1)

            with pe.Fori(0, 4) as q:
                first_pass(q)
            pe.wait_ge(a_ready, 1)
            for i, m in enumerate((tri, ones, suf)):
                last = mm(bank[i][:, :], m[:, :], t[0][:, :], start=True, stop=True)
            last.then_inc(cs_mm, 1)
            pe.wait_ge(csp_ready, 1)
            for g in range(8):
                if g >= 2:
                    pe.wait_ge(csT_evac, g - 1)
                for i in range(8):
                    last = tr(bank[3 + g % 2][0:PARTS * H, :].bitcast(bf16)[:, i * P:(i + 1) * P], csp[:, 8 * g + i, :], ident_b[:, :])
                last.then_inc(csT_done, 1)
            pe.wait_ge(oh_ready, 1)
            mm(bank[0][:, :], stri_b[:, :], ohb[:, :], start=True, stop=True)
            mm(bank[1][:, :], ones_b[:, :], ohb[:, :], start=True, stop=True).then_inc(rank_mm, 1)
            pe.wait_ge(pos_ready, 1)

            def transposes(n, r, q):
                pe.wait_ge(ft_loaded[r], 16 * (q + 1))
                for k in range(KT):
                    last = tr(bank[r % 2][:, k * P:(k + 1) * P], ft[:, r, k * P:(k + 1) * P], ident[:, :])
                last.then_inc(fT_done, 1)

            def experts(q, more, first):
                for r in range(4):
                    n = 4 * q + r
                    if r < 3:
                        transposes(n + 1, r + 1, q)
                    elif more:
                        transposes(n + 1, 0, q + 1)
                    e = nc.tensor.value_load(te[0:1, bass.ds(n, 1)], min_val=0, max_val=E - 1)
                    pe.wait_ge(flo, n + 1)
                    if not (first and r < 2):
                        pe.wait_ge(fsilu, n - 1)
                    o = bank[2 + r % 2][:, 0:DM]
                    mm(o, pick[:, :], fb[:, bass.ds(e, 1), :].rearrange("p e d -> p (e d)"), start=True, stop=False)
                    i = 0
                    for k in range(KT):
                        for a, w in ((0, 0), (1, 0), (0, 1)):
                            i += 1
                            last = mm(o, fxT[:, r % 2, a, k, :], fw[:, w, k, bass.ds(e, 1), :].rearrange("p e d -> p (e d)"),
                                      start=False, stop=(i == 3 * KT))
                    last.then_inc(fmm, 1)

            transposes(0, 0, 0)
            experts(0, True, True)
            with pe.Fori(1, FT // 4 - 1) as q:
                experts(q, True, False)
            experts(FT // 4 - 1, False, False)
            pe.wait_ge(main_const, 3)

            def in_proj(s, b, u, first):
                if u == 0:
                    pe.wait_ge(xT_loaded[b], 8 * (s - b) + 16)
                if not (first and u < 2):
                    pe.wait_ge(inproj_evac, 10 * s + u - 1)
                o = bank[u % 2][:, :]
                i = 0
                if u >= XT:
                    mm(o, pick[:, :], zbias[:, :], start=True, stop=False)
                for k in range(KT):
                    for a, w in ((0, 0), (1, 0), (0, 1)):
                        i += 1
                        if u < XT:
                            last = mm(o, wz[:, w, k, DI + u * P:DI + (u + 1) * P], xT[:, b, a, k, :], start=(i == 1), stop=(i == 3 * KT))
                        else:
                            c = u - XT
                            last = mm(o, xT[:, b, a, k, c * P:(c + 1) * P], wz[:, w, k, 0:DI], start=False, stop=(i == 3 * KT))
                last.then_inc(inproj_done, 1)

            def yT_in(n, c):
                pe.wait_ge(gated, n + 1)
                for k in range(ZT):
                    last = tr(bank[5][:, k * P:(k + 1) * P], y[:, c % 2, k * P:(k + 1) * P], ident[:, :])
                last.then_inc(yT_done, 1)

            def out_proj(n):
                pe.wait_ge(yT_evac, n + 1)
                for k in range(ZT):
                    last = mm(bank[2][:, 0:DM], yT[:, k, :], wo[:, k, :], start=(k == 0), stop=(k == ZT - 1))
                last.then_inc(o_done, 1)

            def main(s, b, first, last_seq):
                for c in range(CPS):
                    n = 4 * s + c
                    tok = slice(c * P, (c + 1) * P)
                    head = first and c == 0
                    if c == 0:
                        pe.wait_ge(xc_ready, s + 1)
                    else:
                        pe.wait_ge(S_ready, 3 * s + c)
                    if c == 0 and not first:
                        pe.wait_ge(fin_step, 3 * (n - 1) - 2)
                    for k in range(ZT):
                        last = tr(bank[2][:, k * P:(k + 1) * P], xc[:, b, k, tok], ident[:, :])
                    last.then_inc(xsT_done, 1)
                    if not head:
                        pe.wait_ge(exp_done, n)
                    if c == 0:
                        pe.wait_ge(cs_loaded[b], 16 * (s - b) + 32)
                    for half in range(2):
                        hs = slice(half * 4, half * 4 + 4)
                        o = bankL[:, half * 512:(half + 1) * 512]
                        mm(o, csl[0:PARTS * H + PARTS, b, tok], csr[0:PARTS * H + PARTS, b, hs, c, :], start=True, stop=False)
                        last = mm(o, ident_b[:, :], maskneg[:, :].unsqueeze(1).to_broadcast([P, 4, P]), start=False, stop=True)
                    last.then_inc(L_done, 1)
                    if not head:
                        pe.wait_ge(y_raw, n)
                    tr(bank[4][:, 0:NST], xc[:, b, ZT, tok], ident[:, :]).then_inc(B_done, 1)
                    if not head:
                        pe.wait_ge(M_ready, n)
                    mm(bank[3][:, 0:P], xc[:, b, ZT, tok], xc[:, b, ZT + 1, tok], start=True, stop=True).then_inc(G_done, 1)
                    if not head:
                        yT_in(n - 1, (c - 1) % 2)
                    if not last_seq:
                        for u in ((0, 1, 2), (3, 4, 5), (6, 7), (8, 9))[c]:
                            in_proj(s + 1, 1 - b, u, False)
                    if not head:
                        pe.wait_ge(xsT_evac, n + 1)
                        out_proj(n - 1)
                    if c > 0:
                        mm(bank[5][:, :], xc[:, b, ZT + 1, tok], S[:, :], start=True, stop=True).then_inc(yoff_done, 1)
                    pe.wait_ge(B_evac, n + 1)
                    pe.wait_ge(X_ready, n + 1)
                    pe.wait_ge(M_ready, n + 1)
                    for h in range(H):
                        last = mm(bank[4][:, h * HD:(h + 1) * HD], Em[:, c % 2, h, :], Xdt[:, c % 2, h * HD:(h + 1) * HD], start=True, stop=True)
                    last.then_inc(yd_done, 1)
                    if c < CPS - 1:
                        pe.wait_ge(Xw_ready, 3 * s + c + 1)
                        if not head:
                            pe.wait_ge(fin_step, 3 * (n - 1) + 1)
                        else:
                            pe.wait_ge(xsT_evac, n + 1)
                        mm(bank[2][:, :], BT[:, :], Xw[:, :], start=True, stop=True).then_inc(snew_done, 1)

            for u in range(XT + CPS):
                in_proj(0, 0, u, True)
            main(0, 0, True, False)
            with pe.Fori(0, SEQS // 2 - 1) as p:
                main(2 * p + 1, 1, False, False)
                main(2 * p + 2, 0, False, False)
            main(SEQS - 1, 1, False, True)
            yT_in(NCH - 1, (CPS - 1) % 2)
            pe.wait_ge(fin_step, 3 * (NCH - 2) + 1)
            out_proj(NCH - 1)


def w_of(a, n):
    return a[:, bass.ds(n, 1), :].rearrange("p o h -> p (o h)") if not isinstance(n, int) else a[:, n, :]


def st_of(a, n, k):
    return a[:, bass.ds(n, 1), k:k + 1].rearrange("p o k -> p (o k)") if not isinstance(n, int) else a[:, n, k:k + 1]


def row_of(a, n):
    return a[:, bass.ds(n, 1), :].rearrange("p o d -> p (o d)") if not isinstance(n, int) else a[:, n, :]


_INS = ["L0_attn_x", "L0_attn_norm_w", "L0_attn_norm_b", "L0_attn_in_proj_w", "L0_attn_conv_w", "L0_attn_conv_b", "L0_attn_dt_bias",
        "L0_attn_A_log", "L0_attn_D", "L0_attn_rms_w", "L0_attn_out_proj_w", "L0_ffn_tile_sigs", "L0_ffn_W", "L0_ffn_b"]


def kernel(**inputs):
    import concourse.bacc as _bacc
    from concourse.bass_utils import run_bass_kernel_spmd as _run

    nc = _bacc.Bacc("TRN2", target_bir_lowering=False, num_devices=1)
    arrays, args = {}, []
    for name in _INS:
        a = np.ascontiguousarray(inputs[name])
        arrays[f"in_{name}"] = a
        args.append(nc.dram_tensor(f"in_{name}", a.shape, mybir.dt.from_np(a.dtype), kind="ExternalInput").ap())
    out = nc.dram_tensor("out_0", (SEQS, SEQ, DM), mybir.dt.float32, kind="ExternalOutput").ap()
    program(nc, *args, out)
    r = _run(nc, [arrays], core_ids=[0])
    return r.results[0]["out_0"]
```

```python
import concourse.bass as bass
from concourse import mybir
from contextlib import ExitStack
import numpy as np

P = 128
SEQS, SEQ, DM = 16, 512, 256
TOK = SEQS * SEQ
NCH = TOK // P
CPS = SEQ // P
KT = DM // P
H, HD, NST = 8, 64, 128
DI = H * HD
ZT = DI // P
XT = (DI + 2 * NST) // P
DPROJ = 2 * DI + 2 * NST + H
TAPS = 4
E = 8
FT = NCH + E
EPS = 1e-5
WS = 64.0
PARTS = 3


def program(nc, x, norm_w, norm_b, in_proj_w, conv_w, conv_b, dt_bias, A_log, D, rms_w, out_proj_w,
            tile_sigs, ffn_W, ffn_b, out):
    fp32, fp16, bf16, i32 = mybir.dt.float32, mybir.dt.float16, mybir.dt.bfloat16, mybir.dt.int32
    ACT, ALU, AX = mybir.ActivationFunctionType, mybir.AluOpType, mybir.AxisListType

    xT_d = nc.dram_tensor("xT_scratch", (SEQS, P, 2 * KT * SEQ), fp16).ap()
    cs_d = nc.dram_tensor("cs_scratch", (PARTS * H, TOK), bf16).ap()
    sorted_d = nc.dram_tensor("sorted_scratch", (FT * P, DM), fp32).ap()
    gate_d = nc.dram_tensor("gate_scratch", (FT * P, DM), fp32).ap()

    x_g = x.rearrange("b (c p) d -> b p c d", p=P)
    out_g = out.rearrange("b (c p) d -> b p c d", p=P)

    ctx = ExitStack()
    with ctx:
        def sem(name):
            return ctx.enter_context(nc.semaphore(name))

        def sbuf(stack, name, shape, dt=fp32):
            return stack.enter_context(nc.sbuf_tensor(name, shape, dt))

        bankL = ctx.enter_context(nc.psum_tensor("bankL", [P, 2 * 512], fp32))
        bank = [ctx.enter_context(nc.psum_tensor(f"bank{i}", [P, 512], fp32)) for i in range(6)]

        ident = sbuf(ctx, "ident", [P, P])
        ident_b = sbuf(ctx, "ident_b", [P, P], bf16)
        wz = sbuf(ctx, "w_in", [P, 2, KT, DPROJ], fp16)
        wo = sbuf(ctx, "w_out", [P, ZT, DM])
        zbias = sbuf(ctx, "zbias", [P, DI], fp16)
        pick = sbuf(ctx, "pick", [P, P], fp16)
        xbias = sbuf(ctx, "xbias", [P, XT])
        cw = sbuf(ctx, "cw", [P, XT, TAPS])
        cb = sbuf(ctx, "cb", [P, XT])
        D_bc = sbuf(ctx, "D_bc", [P, H])
        blk = sbuf(ctx, "blk", [PARTS * H, H, P], bf16)
        maskneg = sbuf(ctx, "maskneg", [P, P], bf16)
        norm_st = sbuf(ctx, "norm_st", [P, NCH, 2])
        dt_all = sbuf(ctx, "dt_all", [P, NCH, H])
        w_all = sbuf(ctx, "w_all", [P, NCH, H])
        ea_all = sbuf(ctx, "ea_all", [P, NCH, H])
        tot_all = sbuf(ctx, "tot_all", [P, NCH, H])
        pos_all = sbuf(ctx, "pos_all", [P, NCH], i32)
        epsc = sbuf(ctx, "epsc", [P, 1])
        mhalf = sbuf(ctx, "mhalf", [P, 8])

        ffn_stack = ExitStack()
        fw = sbuf(ffn_stack, "ffn_w", [P, 2, KT, E, DM], fp16)
        fb = sbuf(ffn_stack, "ffn_b", [P, E, DM], fp16)
        te = sbuf(ffn_stack, "tile_expert", [P, FT], i32)
        ft = sbuf(ffn_stack, "ffn_x", [P, 4, DM])
        fxT = sbuf(ffn_stack, "ffn_xT", [P, 2, 2, KT, P], fp16)
        gt = sbuf(ffn_stack, "ffn_gate", [P, 4, DM])
        pre_stack = ExitStack()
        xn_all = sbuf(pre_stack, "xn_all", [P, NCH, DM])
        sd_all = sbuf(pre_stack, "sd_all", [P, NCH, 2 * H])
        mhi = sbuf(pre_stack, "mhi", [P, KT, 2 * H], fp16)
        mlo = sbuf(pre_stack, "mlo", [P, KT, 2 * H], fp16)
        dtb = sbuf(pre_stack, "dtb", [P, H])
        a_bc = sbuf(pre_stack, "a_bc", [P, H])
        nwb = sbuf(pre_stack, "nwb", [P, 2, KT])
        rev = sbuf(pre_stack, "rev", [P, E])
        tri = sbuf(pre_stack, "tri", [P, P])
        suf = sbuf(pre_stack, "suf", [P, P])
        ones = sbuf(pre_stack, "ones", [P, P])
        ones_b = sbuf(pre_stack, "ones_b", [P, P], bf16)
        stri_b = sbuf(pre_stack, "stri_b", [P, P], bf16)
        zrow = sbuf(pre_stack, "zrow", [P, DM * 4])
        xg = sbuf(pre_stack, "xg", [P, 4, CPS, DM])
        fstage = sbuf(pre_stack, "fstage", [P, KT, E, DM])
        w_stack = ExitStack()
        wrow = sbuf(w_stack, "wrow", [P, 11, DM])
        wT = sbuf(w_stack, "wT", [P, KT, DPROJ])
        worow = sbuf(w_stack, "worow", [P, KT, DI])
        rmsw = sbuf(w_stack, "rmsw", [P, ZT])
        sig = sbuf(w_stack, "sig", [P, DM])
        neg = sbuf(w_stack, "neg", [P, KT, E])
        nbrep = sbuf(w_stack, "nbrep", [P, KT, P])
        nw64 = sbuf(w_stack, "nw64", [P, KT])
        w_stack.close()
        p1_stack = ExitStack()
        x1g = sbuf(p1_stack, "x1g", [P, 2, CPS, DM])
        xTs = sbuf(p1_stack, "xTs", [P, 2, 2, KT, SEQ], fp16)
        bst = sbuf(p1_stack, "bst", [P, 2, CPS, 6])
        mv = sbuf(p1_stack, "mv", [P, 2, CPS, 2])
        var2 = sbuf(p1_stack, "var2", [P, 2, CPS, 2])
        rs2 = sbuf(p1_stack, "rs2", [P, 2, CPS, 2])
        p1_stack.close()
        p2_stack = ExitStack()
        t = [sbuf(p2_stack, f"t{i}", [P, NCH * H]) for i in range(6)]
        rt = [sbuf(p2_stack, f"rt{i}", [P, NCH * H]) for i in range(3)]
        csp = sbuf(p2_stack, "csp", [P, NCH, PARTS * H], bf16)
        csT = sbuf(p2_stack, "csT", [PARTS * H, TOK // 2], bf16)
        ohb = sbuf(p2_stack, "ohb", [P, NCH * E], bf16)
        keep = sbuf(p2_stack, "keep", [P, E, NCH])
        sm = sbuf(p2_stack, "sm", [P, 6, NCH])
        smi = sbuf(p2_stack, "smi", [P, E], i32)
        sx = sbuf(p2_stack, "sx", [P, 2, CPS, DM])
        idx = sbuf(p2_stack, "idx", [P, 2, CPS], i32)
        p2_stack.close()
        pre_stack.close()
        ffn_stack.close()

        xT = sbuf(ctx, "xT", [P, 2, 2, KT, SEQ], fp16)
        vraw = sbuf(ctx, "vraw", [P, XT, TAPS - 1 + SEQ])
        xc = sbuf(ctx, "xc", [P, 2, XT, SEQ])
        sz = sbuf(ctx, "sz", [P, 2, CPS, DI])
        Em = sbuf(ctx, "Em", [P, 2, H, P])
        xsT = sbuf(ctx, "xsT", [P, 2, DI])
        Xdt = sbuf(ctx, "Xdt", [P, 2, DI])
        Xw = sbuf(ctx, "Xw", [P, 2, DI])
        xD = sbuf(ctx, "xD", [P, 2, DI])
        BT = sbuf(ctx, "BT", [P, NST])
        S = sbuf(ctx, "S", [P, DI])
        Sd = sbuf(ctx, "Sd", [P, DI])
        yo = sbuf(ctx, "yo", [P, DI])
        y = sbuf(ctx, "y", [P, 2, DI])
        ysq = sbuf(ctx, "ysq", [P, DI])
        ssq = sbuf(ctx, "ssq", [P, CPS])
        ms = sbuf(ctx, "ms", [P, CPS])
        rstd = sbuf(ctx, "rstd", [P, CPS])
        yT = sbuf(ctx, "yT", [P, ZT, P])
        xin = sbuf(ctx, "xin", [P, 2, CPS, DM])
        gin = sbuf(ctx, "gin", [P, 2, CPS, DM])
        gidx = sbuf(ctx, "gidx", [P, 2, CPS], i32)
        xn = sbuf(ctx, "xn", [P, CPS, DM])
        fo = sbuf(ctx, "fo", [P, 2, DM])
        ob = sbuf(ctx, "ob", [P, CPS, DM])
        csl = sbuf(ctx, "csl", [32, 2, SEQ], bf16)
        csr = sbuf(ctx, "csr", [32, 2, H, CPS, P], bf16)

        w_loaded, small_loaded, fw_loaded = sem("w_loaded"), sem("small_loaded"), [sem("fw_loaded0"), sem("fw_loaded1")]
        fb_loaded, fw_split, fstep, fw_ready, st_ready = (sem(n) for n in ("fb_loaded", "fw_split", "ffn_weight_step", "fw_ready", "st_ready"))
        const_ready, pstep = sem("const_ready"), sem("pool_setup_step")
        wtr_done, wtr_evac = sem("wtr_done"), sem("wtr_evac")
        wlink, bias_mm, nb_ready = sem("setup_vector_step"), sem("bias_mm"), sem("nb_ready")
        setup_done, zero_written, z_ready = sem("setup_done"), sem("zero_written"), sem("zeros_ready")
        x_loaded = [sem(f"x_loaded{r}") for r in range(4)]
        aggr_go, scatter_go, gather_go = sem("aggr_go"), sem("scatter_go"), sem("gather_go")
        stats, aggr, var_ready, rs_ready, x1_ready, xn_ready = (
            sem(n) for n in ("stats_done", "aggr_done", "var_ready", "rs_ready", "x1_ready", "xn_ready"))
        T_done, hi_ready, lo_ready, sc_done, sd_ready = (sem(n) for n in ("T_done", "hi_ready", "lo_ready", "sc_done", "sd_ready"))
        xT_stored = [sem(f"xT_stored{r}") for r in range(2)]
        vstep, softexp_in, softexp_out, a_ready, cs_mm, cs_copied, exps_done = (sem(n) for n in (
            "vstep", "softexp_in", "softexp_out", "a_ready", "cs_mm", "cs_copied", "exps_done"))
        csp_ready, csT_done, csT_evac, cs_stored = (sem(n) for n in ("csp_ready", "csT_done", "csT_evac", "cs_stored"))
        oh_ready, rank_mm, pos_ready = (sem(n) for n in ("oh_ready", "rank_mm", "pos_ready"))
        sx_ready, idx_ready = sem("sx_ready"), sem("idx_ready")
        scattered = [sem(f"scattered{r}") for r in range(2)]
        ft_loaded = [sem(f"ft_loaded{r}") for r in range(4)]
        fT_done, fhi, flo, fmm, fsilu = (sem(n) for n in ("fT_done", "ffn_hi", "ffn_lo", "ffn_mm", "ffn_silu"))
        g_stored = [sem(f"g_stored{r}") for r in range(4)]
        main_const = sem("main_const")
        xT_loaded = [sem(f"xT_loaded{b}") for b in range(2)]
        cs_loaded = [sem(f"cs_loaded{b}") for b in range(2)]
        xin_loaded = [sem(f"xin_loaded{b}") for b in range(2)]
        g_loaded = [sem(f"g_loaded{b}") for b in range(2)]
        inproj_done, inproj_evac, tap0, conv_step, xc_ready, sz_ready = (sem(n) for n in (
            "inproj_done", "inproj_evac", "tap0_ready", "conv_step", "xc_ready", "sz_ready"))
        xsT_done, xsT_evac, L_done, exp_done, B_done, B_evac, G_done = (sem(n) for n in (
            "xsT_done", "xsT_evac", "L_done", "exp_done", "B_done", "B_evac", "G_done"))
        yoff_done, yd_done, snew_done, yT_done, yT_evac, o_done = (sem(n) for n in (
            "yoff_done", "yd_done", "snew_done", "yT_done", "yT_evac", "o_done"))
        X_ready, M_ready, yo_ready, y_raw, S_ready, fin_step = (sem(n) for n in (
            "X_ready", "M_ready", "yo_ready", "y_raw", "S_ready", "fin_step"))
        Xw_ready, xD_ready, Sd_ready, yD_ready, gated, sq_done, ms_ready, rstd_ready, gidx_ready, xn_done = (sem(n) for n in (
            "Xw_ready", "xD_ready", "Sd_ready", "yD_ready", "gated", "sq_done", "ms_ready", "rstd_ready", "gidx_ready", "xn_done"))
        out_stored = sem("out_stored")

        NW = 11
        wcols = [(i * P, min(P, DPROJ - i * P)) for i in range(NW)]
        N_SMALL = 16 * 11

        block = ctx.enter_context(nc.Block())

        @block.sync
        def _(sp):
            sp.dma_start(wrow[:, 0:10, :], in_proj_w[0:10 * P, :].rearrange("(m p) d -> p m d", p=P)).then_inc(w_loaded, 16)
            sp.dma_start(wrow[0:H, 10, :], in_proj_w[10 * P:DPROJ, :]).then_inc(w_loaded, 16)
            sp.dma_start(worow[:, :, :], out_proj_w.rearrange("(m p) c -> p m c", p=P)).then_inc(w_loaded, 16)
            sp.dma_start(sig[0:E, :], tile_sigs).then_inc(w_loaded, 16)
            with nc.allow_non_contiguous_dma(reason="small vectors by channel"):
                sp.dma_start(nwb[:, 0, :], norm_w.rearrange("(k p) -> p k", p=P)).then_inc(small_loaded, 16)
                sp.dma_start(nwb[:, 1, :], norm_b.rearrange("(k p) -> p k", p=P)).then_inc(small_loaded, 16)
                sp.dma_start(rmsw[:, :], rms_w.rearrange("(k p) -> p k", p=P)).then_inc(small_loaded, 16)
                sp.dma_start(cw[:, :, :], conv_w.rearrange("(m p) t -> p m t", p=P)).then_inc(small_loaded, 16)
                sp.dma_start(cb[:, :], conv_b.rearrange("(m p) -> p m", p=P)).then_inc(small_loaded, 16)
                sp.dma_start(dtb[:, :], dt_bias.partition_broadcast(P)).then_inc(small_loaded, 16)
                sp.dma_start(a_bc[:, :], A_log.partition_broadcast(P)).then_inc(small_loaded, 16)
                sp.dma_start(D_bc[:, :], D.partition_broadcast(P)).then_inc(small_loaded, 16)
            for r in range(4):
                sp.dma_start(xg[:, r, :, :], x_g[r]).then_inc(x_loaded[r], 16)
            for k in range(KT):
                sp.dma_start(fstage[:, k, :, :], ffn_W[:, k * P:(k + 1) * P, :].rearrange("e p d -> p e d")).then_inc(fw_loaded[k], 16)
            sp.wait_ge(z_ready, 1)
            for n in range(FT // 4):
                sp.dma_start(sorted_d[n * 4 * P:(n + 1) * 4 * P, :].rearrange("(p c) d -> p (c d)", p=P), zrow[:, :]).then_inc(zero_written, 16)

            def first_pass(q, more):
                for r in range(4):
                    j = 4 * q + r
                    sp.wait_ge(xn_ready, j + 1)
                    if more:
                        sp.dma_start(xg[:, r, :, :], x_g[j + 4]).then_inc(x_loaded[r], 16)
                    sp.wait_ge(lo_ready, j + 1)
                    sp.dma_start(xT_d[j], xTs[:, r % 2, :, :, :].rearrange("p a k t -> p (a k t)")).then_inc(xT_stored[r % 2], 16)

            with sp.Fori(0, 3) as q:
                first_pass(q, True)
            first_pass(3, False)
            for half in range(2):
                sp.wait_ge(csT_evac, 4 * (half + 1))
                sp.dma_start(cs_d[:, half * TOK // 2:(half + 1) * TOK // 2], csT[:, :]).then_inc(cs_stored, 16)
                sp.wait_ge(cs_stored, 16 * (half + 1))
            sp.wait_ge(fw_split, 1)
            sp.dma_start(fstage[0:64, 0, :, :], ffn_b.partition_broadcast(64)).then_inc(fb_loaded, 16)
            for b in range(2):
                sp.wait_ge(scattered[b], 16 * CPS * SEQS // 2)
            for r in range(4):
                sp.dma_start(ft[:, r, :], sorted_d[r * P:(r + 1) * P, :]).then_inc(ft_loaded[r], 16)

            def expert_io(q, more):
                for r in range(4):
                    n = 4 * q + r
                    if more:
                        sp.wait_ge(fT_done, n + 1)
                        sp.dma_start(ft[:, r, :], sorted_d.rearrange("(n p) d -> n p d", p=P)[n + 4]).then_inc(ft_loaded[r], 16)
                    sp.wait_ge(fsilu, n + 1)
                    sp.dma_start(gate_d.rearrange("(n p) d -> n p d", p=P)[n], gt[:, r, :]).then_inc(g_stored[r], 16)

            with sp.Fori(0, FT // 4 - 1) as q:
                expert_io(q, True)
            expert_io(FT // 4 - 1, False)
            for r in range(4):
                sp.wait_ge(g_stored[r], 16 * (FT // 4))
            for b in range(2):
                sp.wait_ge(xT_stored[b], 16 * (SEQS // 2 + 1))
            sp.wait_ge(main_const, 3)

            def load_seq(s, b):
                sp.dma_start(xT[:, b, :, :, :].rearrange("p a k t -> p (a k t)"), xT_d[s]).then_inc(xT_loaded[b], 16)

            def load_rest(s, b):
                sp.dma_start(xin[:, b, :, :], x_g[s]).then_inc(xin_loaded[b], 16)
                src = cs_d.rearrange("r (s t) -> s r t", t=SEQ)[s]
                sp.dma_start(csl[0:PARTS * H, b, :], src).then_inc(cs_loaded[b], 16)
                sp.dma_start(csr[PARTS * H:PARTS * (H + 1), b, :, :, :].rearrange("o h c l -> o h (c l)"),
                             src.rearrange("(o h) t -> o h t", h=H)).then_inc(cs_loaded[b], 16)

            load_seq(0, 0)
            load_rest(0, 0)
            load_seq(1, 1)

            def main_io(s, b, first, last):
                if not last:
                    if not first:
                        sp.wait_ge(fin_step, 12 * s)
                    load_rest(s + 1, 1 - b)
                    sp.wait_ge(inproj_done, 10 * (s + 1))
                    if not isinstance(s, int) or s < SEQS - 2:
                        load_seq(s + 2, b)
                if not first:
                    sp.wait_ge(fin_step, 12 * s)
                    sp.dma_start(out_g[s - 1], ob[:, :, :]).then_inc(out_stored, 16)

            main_io(0, 0, True, False)
            with sp.Fori(0, SEQS // 2 - 2) as p:
                main_io(2 * p + 1, 1, False, False)
                main_io(2 * p + 2, 0, False, False)
            main_io(SEQS - 3, 1, False, False)
            main_io(SEQS - 2, 0, False, False)
            main_io(SEQS - 1, 1, False, True)
            sp.wait_ge(fin_step, 12 * SEQS)
            sp.dma_start(out_g[SEQS - 1], ob[:, :, :]).then_inc(out_stored, 16)
            sp.wait_ge(out_stored, 16 * SEQS)

        @block.gpsimd
        def _(pool):
            steps = [0]

            def link(ins):
                steps[0] += 1
                ins.then_inc(pstep, 1)
                pool.wait_ge(pstep, steps[0])

            pool.memset(zrow[:, :], 0.0).then_inc(z_ready, 1)
            pool.memset(ident[:, :], 0.0)
            pool.memset(tri[:, :], 1.0)
            pool.memset(suf[:, :], 1.0)
            pool.memset(ones[:, :], 1.0)
            pool.memset(ones_b[:, :], 1.0)
            pool.memset(stri_b[:, :], 1.0)
            pool.memset(maskneg[:, :], 0.0)
            pool.memset(mhalf[:, :], -0.5)
            pool.memset(epsc[:, :], EPS)
            pool.memset(blk[:, :, :], 0.0)
            pool.memset(pick[:, :], 0.0)
            pool.memset(zbias[:, :], 0.0)
            pool.memset(fb[:, :, :], 0.0)
            link(pool.memset(mlo[:, :, :], 0.0))
            link(pool.memset(pick[0:1, :], 1.0))
            link(pool.memset(pick[32:33, :], 1.0))
            pool.affine_select(out=ident[:, :], in_=ident[:, :], compare_op=ALU.not_equal, fill=1.0, base=0,
                               pattern=[[-1, P]], channel_multiplier=1)
            pool.affine_select(out=tri[:, :], in_=tri[:, :], compare_op=ALU.is_ge, fill=0.0, base=0,
                               pattern=[[1, P]], channel_multiplier=-1)
            pool.affine_select(out=suf[:, :], in_=suf[:, :], compare_op=ALU.is_gt, fill=0.0, base=0,
                               pattern=[[-1, P]], channel_multiplier=1)
            pool.affine_select(out=stri_b[:, :], in_=stri_b[:, :], compare_op=ALU.is_gt, fill=0.0, base=0,
                               pattern=[[1, P]], channel_multiplier=-1)
            pool.affine_select(out=maskneg[:, :], in_=maskneg[:, :], compare_op=ALU.is_ge, fill=-1e30, base=0,
                               pattern=[[1, P]], channel_multiplier=-1)
            link(pool.iota(rev[:, :], pattern=[[-1, E]], base=E, channel_multiplier=0, allow_small_or_imprecise_dtypes=True))
            for part in range(PARTS):
                link(pool.affine_select(out=blk[:, :, :], in_=blk[:, :, :], compare_op=ALU.not_equal, fill=-1.0, base=-part * H,
                                        pattern=[[-1, H], [0, P]], channel_multiplier=1))
            pool.tensor_copy(ident_b[:, :], ident[:, :]).then_inc(const_ready, 1)
            def roots(q):
                for r in range(4):
                    pool.wait_ge(var_ready, 4 * q + r + 1)
                    pool.tensor_tensor(rs2[:, r % 2, :, :], var2[:, r % 2, :, :], mhalf[:, :].rearrange("p (c k) -> p c k", k=2), ALU.pow).then_inc(rs_ready, 1)

            with pool.Fori(0, 4) as q:
                roots(q)
            pool.wait_ge(sd_ready, SEQS)
            for b in range(2):
                pool.wait_ge(xT_stored[b], 16 * (SEQS // 2 + 1))
            pool.memset(keep[:, :, :], 1.0)
            link(pool.iota(t[5][:, 0:FT], pattern=[[1, FT]], base=0, channel_multiplier=0, allow_small_or_imprecise_dtypes=True))
            pool.memset(keep[:, :, 0:1], 0.0).then_inc(const_ready, 1)
            def scatter(q):
                for r in range(2):
                    pool.wait_ge(zero_written, 16 * (FT // 4))
                    pool.wait_ge(sx_ready, 2 * q + r + 1)
                    pool.wait_ge(idx_ready, 2 * q + r + 1)
                    pool.sem_inc(scatter_go, 1)
                    for c in range(CPS):
                        pool.indirect_dma_start(out=sorted_d, out_offset=bass.IndirectOffsetOnAxis(ap=idx[:, r, c:c + 1], axis=0),
                                                in_=sx[:, r, c, :], in_offset=None).then_inc(scattered[r], 16)

            with pool.Fori(0, SEQS // 2) as q:
                scatter(q)
            for r in range(4):
                pool.wait_ge(g_stored[r], 16 * (FT // 4))
            pool.wait_ge(cs_stored, 32)
            pool.memset(vraw[:, :, 0:TAPS - 1], 0.0).then_inc(main_const, 1)
            pool.memset(csl[:, :, :], 1.0).then_inc(main_const, 1)

            def x_products(s, c):
                n = 4 * s + c
                hb = lambda a: a.unsqueeze(2).to_broadcast([P, H, HD])
                xs3 = xsT[:, c % 2, :].rearrange("p (h d) -> p h d", d=HD)
                pool.wait_ge(xsT_evac, n + 1)
                if c < CPS - 1:
                    pool.tensor_tensor(Xw[:, c % 2, :].rearrange("p (h d) -> p h d", d=HD), xs3, hb(w_of(w_all, n)), ALU.mult).then_inc(Xw_ready, 1)
                pool.tensor_tensor(xD[:, c % 2, :].rearrange("p (h d) -> p h d", d=HD), xs3, hb(D_bc[:, :]), ALU.mult).then_inc(xD_ready, 1)
                if c in (1, 2):
                    pool.wait_ge(S_ready, 3 * s + c)
                    pool.tensor_tensor(Sd[:, :].rearrange("p (h d) -> p h d", d=HD), S[:, :].rearrange("p (h d) -> p h d", d=HD),
                                       hb(w_of(tot_all, n)), ALU.mult).then_inc(Sd_ready, 1)

            def root(n, c):
                pool.wait_ge(sq_done, n + 1)
                pool.tensor_tensor(ms[:, c:c + 1], ssq[:, c:c + 1], epsc[:, :], ALU.add).then_inc(ms_ready, 1)
                pool.wait_ge(ms_ready, n + 1)
                pool.tensor_tensor(rstd[:, c:c + 1], ms[:, c:c + 1], mhalf[:, 0:1], ALU.pow).then_inc(rstd_ready, 1)

            def gather(s, b, chunks, fin):
                if chunks[0] == 0:
                    if fin is not None:
                        pool.wait_ge(fin_step, fin)
                    pool.tensor_copy(gidx[:, b, :], pos_all[:, bass.ts(s, CPS)]).then_inc(gidx_ready, 1)
                    pool.wait_ge(gidx_ready, s + 1)
                    pool.sem_inc(gather_go, 1)
                for c in chunks:
                    pool.indirect_dma_start(out=gin[:, b, c, :], out_offset=None, in_=gate_d,
                                            in_offset=bass.IndirectOffsetOnAxis(ap=gidx[:, b, c:c + 1], axis=0)).then_inc(g_loaded[b], 16)

            def main(s, b, first, more):
                for c in range(CPS):
                    n = 4 * s + c
                    if not (first and c == 0):
                        root(n - 1, (c - 1) % CPS)
                    pool.wait_ge(y_raw, n + 1)
                    if c > 0:
                        pool.tensor_tensor(y[:, c % 2, :], y[:, c % 2, :], xD[:, c % 2, :], ALU.add).then_inc(yD_ready, 1)
                        pool.wait_ge(yD_ready, 3 * s + c)
                    if c == 0:
                        pool.wait_ge(sz_ready, s + 1)
                        pool.wait_ge(inproj_evac, 10 * (s + 1))
                    pool.tensor_tensor(y[:, c % 2, :], y[:, c % 2, :], sz[:, b, c, :], ALU.mult).then_inc(gated, 1)
                    if c < CPS - 1:
                        x_products(s, c + 1)
                    elif more:
                        x_products(s + 1, 0)
                    if more and c > 0:
                        gather(s + 1, 1 - b, ((), (0,), (1,), (2, 3))[c], None if first else 12 * s)

            gather(0, 0, (0, 1, 2, 3), None)
            x_products(0, 0)
            main(0, 0, True, True)
            with pool.Fori(0, SEQS // 2 - 1) as p:
                main(2 * p + 1, 1, False, True)
                main(2 * p + 2, 0, False, True)
            main(SEQS - 1, 1, False, False)
            root(NCH - 1, CPS - 1)

        @block.scalar
        def _(act):
            n = 0
            for k in range(KT):
                for m, (c0, cn) in enumerate(wcols):
                    act.wait_ge(wtr_done, n + 1)
                    act.activation(wT[:, k, c0:c0 + cn], bank[n % 2][:, 0:cn], ACT.Copy).then_inc(wtr_evac, 1)
                    n += 1
            act.wait_ge(small_loaded, 16 * 8)
            for kc in range(ZT):
                act.wait_ge(wtr_done, n + 1)
                act.activation(wo[:, kc, :], bank[n % 2][:, 0:DM], ACT.Identity, scale=rmsw[:, kc:kc + 1]).then_inc(wtr_evac, 1)
                n += 1
            act.wait_ge(wtr_done, n + 1)
            act.activation(neg[:, :, :], bank[n % 2][:, 0:KT * E].rearrange("p (k e) -> p k e", e=E), ACT.Copy).then_inc(wtr_evac, 1)
            act.activation(a_bc[:, :], a_bc[:, :], ACT.Exp).then_inc(setup_done, 1)

            def highs(q):
                for r in range(4):
                    j = 4 * q + r
                    act.wait_ge(T_done, j + 1)
                    act.wait_ge(xT_stored[r % 2], 16 * (2 * q + r // 2 + 1))
                    for k in range(KT):
                        act.activation(xTs[:, r % 2, 0, k, :], bank[2 * (r % 2) + k][:, :], ACT.Copy).then_inc(hi_ready, 1)
                    act.wait_ge(st_ready, j + 1)
                    for c in range(CPS):
                        last = act.activation(row_of(xn_all, 4 * j + c), xg[:, r, c, :], ACT.Identity, bias=st_of(norm_st, 4 * j + c, 1),
                                              scale=st_of(norm_st, 4 * j + c, 0))
                    last.then_inc(xn_ready, 1)

            act.sem_inc(xT_stored[0], 16)
            act.sem_inc(xT_stored[1], 16)
            with act.Fori(0, 4) as q:
                highs(q)
            act.wait_ge(softexp_in, 1)
            act.activation(t[1][:, :], t[1][:, :], ACT.Exp).then_inc(softexp_out, 1)
            def rows(q, first):
                for r in range(2):
                    if not first:
                        act.wait_ge(scattered[r], 16 * CPS * q)
                    act.activation(sx[:, r, :, :].rearrange("p c d -> p (c d)"),
                                   xn_all[:, bass.ts(2 * q + r, CPS), :].rearrange("p c d -> p (c d)"), ACT.Copy).then_inc(sx_ready, 1)
                    if first and r == 0:
                        act.wait_ge(pos_ready, 1)
                    act.activation(idx[:, r, :], pos_all[:, bass.ts(2 * q + r, CPS)], ACT.Copy).then_inc(idx_ready, 1)

            rows(0, True)
            act.wait_ge(cs_copied, 1)
            act.activation(ea_all[:, :, :].rearrange("p c h -> p (c h)"), t[2][:, :], ACT.Exp).then_inc(exps_done, 1)
            act.activation(tot_all[:, :, :].rearrange("p c h -> p (c h)"), bank[1][:, :], ACT.Exp).then_inc(exps_done, 1)
            act.activation(w_all[:, :, :].rearrange("p c h -> p (c h)"), bank[2][:, :], ACT.Exp).then_inc(exps_done, 1)
            with act.Fori(1, SEQS // 2) as q:
                rows(q, False)

            def split_hi(n, r):
                act.wait_ge(fT_done, n + 1)
                act.activation(fxT[:, r % 2, 0, :, :], bank[r % 2][:, 0:DM].rearrange("p (k t) -> p k t", k=KT), ACT.Copy).then_inc(fhi, 1)

            def experts(q, more, first):
                for r in range(4):
                    n = 4 * q + r
                    if more or r < 3:
                        split_hi(n + 1, (r + 1) % 4)
                    act.wait_ge(fmm, n + 1)
                    if not first:
                        act.wait_ge(g_stored[r], 16 * q)
                    act.activation(gt[:, r, :], bank[2 + r % 2][:, 0:DM], ACT.Silu, scale=1.0 / WS).then_inc(fsilu, 1)

            split_hi(0, 0)
            experts(0, True, True)
            with act.Fori(1, FT // 4 - 1) as q:
                experts(q, True, False)
            experts(FT // 4 - 1, False, False)
            act.wait_ge(main_const, 3)
            for r in range(4):
                act.wait_ge(g_stored[r], 16 * (FT // 4))

            def evac(s, b, u, first):
                act.wait_ge(inproj_done, 10 * s + u + 1)
                if u < XT:
                    if not first:
                        act.wait_ge(conv_step, 18 * s)
                    act.activation(vraw[:, u, TAPS - 1:], bank[u % 2][:, :], ACT.Identity, bias=xbias[:, u:u + 1], scale=1.0 / WS).then_inc(inproj_evac, 1)
                    act.wait_ge(inproj_evac, 10 * s + u + 1)
                    act.activation(xc[:, b, u, :], vraw[:, u, TAPS - 1:], ACT.Identity, bias=cb[:, u:u + 1],
                                   scale=cw[:, u, TAPS - 1:TAPS]).then_inc(tap0, 1)
                elif u < XT + 2:
                    act.activation(sz[:, b, u - XT, :], bank[u % 2][:, :], ACT.Copy, scale=1.0 / WS).then_inc(inproj_evac, 1)
                else:
                    act.activation(sz[:, b, u - XT, :], bank[u % 2][:, :], ACT.Silu, scale=1.0 / WS).then_inc(inproj_evac, 1)

            def silu_x(s, b):
                act.wait_ge(conv_step, 18 * (s + 1))
                act.activation(xc[:, b, :, :], xc[:, b, :, :], ACT.Silu).then_inc(xc_ready, 1)

            def silu_z(s, b):
                act.wait_ge(inproj_evac, 10 * s + XT + 2)
                act.activation(sz[:, b, 0:2, :], sz[:, b, 0:2, :], ACT.Silu).then_inc(sz_ready, 1)

            def front(n, c):
                act.wait_ge(L_done, n + 1)
                act.activation(Em[:, c % 2, :, :].rearrange("p h l -> p (h l)"), bankL[:, :], ACT.Exp).then_inc(exp_done, 1)
                act.wait_ge(xsT_done, n + 1)
                act.activation(xsT[:, c % 2, :], bank[2][:, :], ACT.Copy).then_inc(xsT_evac, 1)

            def main(s, b, first, more, more2):
                for c in range(CPS):
                    n = 4 * s + c
                    if c < CPS - 1 or more:
                        front(n + 1, (c + 1) % CPS)
                    if c == 2 and more:
                        silu_z(s + 1, 1 - b)
                    for ds, bb, u in units(c, b, more, more2):
                        evac(s + ds, bb, u, False)
                    if c == 0:
                        if not first:
                            act.wait_ge(fin_step, 12 * s)
                        act.wait_ge(xin_loaded[b], 8 * (s - b) + 16)
                    act.activation(xn[:, c, :], xin[:, b, c, :], ACT.Identity, bias=st_of(norm_st, n, 1), scale=st_of(norm_st, n, 0)).then_inc(xn_done, 1)
                    act.wait_ge(gated, n + 1)
                    act.activation(ysq[:, :], y[:, c % 2, :], ACT.Square, scale=float(DI ** -0.5), accum_out=ssq[:, c:c + 1]).then_inc(sq_done, 1)
                    act.wait_ge(yT_done, n + 1)
                    act.activation(yT[:, :, :].rearrange("p k t -> p (k t)"), bank[2][:, :], ACT.Copy).then_inc(yT_evac, 1)
                    if c == 2 and more:
                        silu_x(s + 1, 1 - b)

            for u in range(XT + CPS):
                evac(0, 0, u, True)
            silu_z(0, 0)
            silu_x(0, 0)
            for u in range(2):
                evac(1, 1, u, False)
            front(0, 0)
            main(0, 0, True, True, True)
            with act.Fori(0, SEQS // 2 - 2) as p:
                main(2 * p + 1, 1, False, True, True)
                main(2 * p + 2, 0, False, True, True)
            main(SEQS - 3, 1, False, True, True)
            main(SEQS - 2, 0, False, True, False)
            main(SEQS - 1, 1, False, False, False)

        @block.vector
        def _(dve):
            steps = [0]

            def wl(ins):
                steps[0] += 1
                ins.then_inc(wlink, 1)
                dve.wait_ge(wlink, steps[0])

            dve.wait_ge(const_ready, 1)
            dve.wait_ge(small_loaded, 16 * 8)
            for k in range(KT):
                last = nc.vector.tensor_scalar(nbrep[:, k, :], ones[:, :], nwb[:, 1, k:k + 1], WS, ALU.mult, ALU.mult)
            last.then_inc(nb_ready, 1)
            wl(nc.vector.tensor_scalar(nw64[:, :], nwb[:, 0, :], WS, None, ALU.mult))
            dve.wait_ge(wtr_evac, 2 * NW)
            for k in range(KT):
                wl(nc.vector.tensor_scalar(wz[:, 0, k, :], wT[:, k, :], nw64[:, k:k + 1], None, ALU.mult))
                wl(nc.vector.scalar_tensor_tensor(wz[:, 1, k, :], wT[:, k, :], nw64[:, k:k + 1], wz[:, 0, k, :], ALU.mult, ALU.subtract))
            dve.wait_ge(wtr_evac, 2 * NW + ZT + 1)
            wl(nc.vector.tensor_scalar(mhi[:, :, 0:E], neg[:, :, :], 0.0, None, ALU.is_gt))
            wl(nc.vector.tensor_scalar(neg[:, :, :], neg[:, :, :], 0.0, None, ALU.is_lt))
            wl(nc.vector.tensor_tensor(mhi[:, :, 0:E], mhi[:, :, 0:E], neg[:, :, :], ALU.subtract))
            wl(nc.vector.tensor_copy(mhi[:, :, E:2 * E], wz[:, 0, :, DPROJ - H:DPROJ]))
            wl(nc.vector.tensor_copy(mlo[:, :, E:2 * E], wz[:, 1, :, DPROJ - H:DPROJ]))
            dve.wait_ge(bias_mm, 1)
            wl(nc.vector.tensor_copy(zbias[0:64, :], bank[2][0:64, :]))
            wl(nc.vector.tensor_tensor(zbias[32:64, :], bank[2][32:64, :], zbias[32:64, :], ALU.subtract))
            wl(nc.vector.tensor_copy(xbias[:, :], bank[3][:, 0:XT]))
            wl(nc.vector.scalar_tensor_tensor(dtb[:, :], bank[4][:, 0:H], 1.0 / WS, dtb[:, :], ALU.mult, ALU.add))
            dve.wait_ge(setup_done, 1)
            nc.vector.tensor_scalar(a_bc[:, :], a_bc[:, :], -1.0, None, ALU.mult).then_inc(setup_done, 1)

            def moments(r, q):
                dve.wait_ge(x_loaded[r], 16 * (q + 1))
                for c in range(CPS):
                    last = nc.vector.bn_stats(bst[:, r % 2, c, :], xg[:, r, c, :])
                last.then_inc(stats, 1)

            def low(j, r):
                dve.wait_ge(hi_ready, 2 * (j + 1))
                for k in range(KT):
                    last = nc.vector.tensor_tensor(xTs[:, r % 2, 1, k, :], bank[2 * (r % 2) + k][:, :], xTs[:, r % 2, 0, k, :], ALU.subtract)
                last.then_inc(lo_ready, 1)

            def scores(j, r):
                dve.wait_ge(sc_done, j + 1)
                nc.vector.tensor_copy(sd_all[:, bass.ts(j, CPS), :], bankL[:, (r % 2) * 512:(r % 2) * 512 + CPS * 2 * H].rearrange(
                    "p (c k) -> p c k", k=2 * H)).then_inc(sd_ready, 1)

            def norm(q, first, last_q):
                for r in range(4):
                    j = 4 * q + r
                    dve.wait_ge(stats, j + 1)
                    dve.sem_inc(aggr_go, 1)
                    for c in range(CPS):
                        last = nc.vector.bn_aggr(mv[:, r % 2, c, :], bst[:, r % 2, c, :])
                    last.then_inc(aggr, 1)
                    dve.wait_ge(aggr, j + 1)
                    nc.vector.tensor_scalar(var2[:, r % 2, :, 0:1], mv[:, r % 2, :, 1:2], EPS, None, ALU.add)
                    nc.vector.tensor_scalar(var2[:, r % 2, :, 1:2], mv[:, r % 2, :, 1:2], 1.0 + EPS, EPS * EPS, ALU.mult, ALU.add).then_inc(var_ready, 1)
                    if r < 3:
                        moments(r + 1, q)
                    elif not last_q:
                        moments(0, q + 1)
                    lagging = not (first and r == 0)
                    if lagging:
                        low(j - 1, (r - 1) % 4)
                    dve.wait_ge(rs_ready, j + 1)
                    for c in range(CPS):
                        last = nc.vector.tensor_scalar(x1g[:, r % 2, c, :], xg[:, r, c, :], mv[:, r % 2, c, 0:1], rs2[:, r % 2, c, 1:2], ALU.subtract, ALU.mult)
                    last.then_inc(x1_ready, 1)
                    nc.vector.tensor_copy(norm_st[:, bass.ts(j, CPS), 0:1], rs2[:, r % 2, :, 0:1])
                    nc.vector.scalar_tensor_tensor(norm_st[:, bass.ts(j, CPS), 1:2], mv[:, r % 2, :, 0:1], -1.0, rs2[:, r % 2, :, 0:1], ALU.mult, ALU.mult).then_inc(st_ready, 1)
                    if lagging:
                        scores(j - 1, (r - 1) % 4)

            moments(0, 0)
            norm(0, True, False)
            with dve.Fori(1, 3) as q:
                norm(q, False, False)
            norm(3, False, True)
            low(SEQS - 1, 3)
            scores(SEQS - 1, 3)

            vs = [0]

            def link(ins):
                vs[0] += 1
                ins.then_inc(vstep, 1)
                dve.wait_ge(vstep, vs[0])

            c3 = lambda a: a.rearrange("p (c h) -> p c h", h=H)
            bc = lambda a: a.unsqueeze(1).to_broadcast([P, NCH, H])
            dve.wait_ge(sd_ready, SEQS)
            for b in range(2):
                dve.wait_ge(xT_stored[b], 16 * (SEQS // 2 + 1))
            link(nc.vector.tensor_scalar(c3(t[0][:, :]), sd_all[:, :, H:2 * H], 1.0 / WS, None, ALU.mult))
            link(nc.vector.tensor_tensor(c3(t[0][:, :]), c3(t[0][:, :]), bc(dtb[:, :]), ALU.add))
            nc.vector.scalar_tensor_tensor(t[1][:, :], t[0][:, :], -1.0, t[0][:, :], ALU.mult, ALU.min).then_inc(softexp_in, 1)
            sc = sd_all[:, :, 0:E]
            big = lambda a: a.unsqueeze(2).to_broadcast([P, NCH, E])
            link(nc.vector.tensor_reduce(sm[:, 0, :], sc, AX.X, ALU.max))
            link(nc.vector.tensor_tensor(c3(rt[0][:, :]), sc, big(sm[:, 0, :]), ALU.is_ge))
            link(nc.vector.tensor_tensor(c3(rt[0][:, :]), c3(rt[0][:, :]), bc(rev[:, :]), ALU.mult))
            link(nc.vector.tensor_reduce(sm[:, 1, :], c3(rt[0][:, :]), AX.X, ALU.max))
            nc.vector.tensor_tensor(c3(ohb[:, :]), c3(rt[0][:, :]), big(sm[:, 1, :]), ALU.is_equal).then_inc(oh_ready, 1)
            dve.wait_ge(softexp_out, 1)
            link(nc.vector.tensor_scalar(t[2][:, :], t[1][:, :], 2.0, None, ALU.add))
            link(nc.vector.reciprocal(t[2][:, :], t[2][:, :]))
            link(nc.vector.tensor_tensor(t[1][:, :], t[1][:, :], t[2][:, :], ALU.mult))
            link(nc.vector.tensor_tensor(t[2][:, :], t[1][:, :], t[1][:, :], ALU.mult))
            link(nc.vector.tensor_scalar(t[3][:, :], t[2][:, :], 1.0 / 15, None, ALU.mult))
            for k in (13, 11, 9, 7, 5, 3):
                link(nc.vector.scalar_tensor_tensor(t[3][:, :], t[3][:, :], 1.0 / k, t[2][:, :], ALU.add, ALU.mult))
            link(nc.vector.scalar_tensor_tensor(t[3][:, :], t[3][:, :], 1.0, t[1][:, :], ALU.add, ALU.mult))
            link(nc.vector.tensor_scalar(t[0][:, :], t[0][:, :], 0.0, None, ALU.max))
            link(nc.vector.scalar_tensor_tensor(dt_all[:, :, :].rearrange("p c h -> p (c h)"), t[3][:, :], 2.0, t[0][:, :], ALU.mult, ALU.add))
            nc.vector.tensor_tensor(c3(t[0][:, :]), dt_all[:, :, :], bc(a_bc[:, :]), ALU.mult).then_inc(a_ready, 1)
            dve.wait_ge(rank_mm, 1)
            dve.wait_ge(const_ready, 2)
            e3 = lambda a: a.rearrange("p (e c) -> p e c", c=NCH)
            ec = lambda a: a.rearrange("p (c e) -> p e c", e=E)
            link(nc.vector.tensor_copy(e3(rt[1][:, :]), ec(bankL[:, 512:1024])))
            link(nc.vector.tensor_tensor_scan(rt[2][:, :], keep[:, :, :].rearrange("p e c -> p (e c)"), rt[1][:, :], 0.0, ALU.mult, ALU.add))
            link(nc.vector.tensor_tensor(rt[1][:, :], rt[2][:, :], rt[1][:, :], ALU.subtract))
            link(nc.vector.tensor_scalar(smi[:, :].unsqueeze(2), e3(rt[2][:, :])[:, :, NCH - 1:NCH], float(P - 1), None, ALU.add))
            link(nc.vector.tensor_scalar(smi[:, :], smi[:, :], 7, None, ALU.arith_shift_right))
            link(nc.vector.tensor_copy(sm[:, 2, 0:E], smi[:, :]))
            link(nc.vector.tensor_tensor_scan(sm[:, 3, 0:E], ones[:, 0:E], sm[:, 2, 0:E], 0.0, ALU.mult, ALU.add))
            link(nc.vector.tensor_tensor(sm[:, 2, 0:E], sm[:, 3, 0:E], sm[:, 2, 0:E], ALU.subtract))
            link(nc.vector.tensor_scalar(sm[:, 2, 0:E], sm[:, 2, 0:E], float(P), None, ALU.mult))
            link(nc.vector.tensor_tensor(c3(rt[0][:, :]), c3(bankL[:, 0:512]), e3(rt[1][:, :]).rearrange("p e c -> p c e"), ALU.add))
            link(nc.vector.tensor_tensor(c3(rt[0][:, :]), c3(rt[0][:, :]), bc(sm[:, 2, 0:E]), ALU.add))
            link(nc.vector.tensor_tensor(rt[0][:, :], rt[0][:, :], ohb[:, :], ALU.mult))
            link(nc.vector.tensor_reduce(sm[:, 4, :], c3(rt[0][:, :]), AX.X, ALU.add))
            link(nc.vector.tensor_copy(pos_all[:, :], sm[:, 4, :]))
            tv = rt[2][:, 0:FT // 2 * E].rearrange("p (n e) -> p n e", e=E)
            for half in range(2):
                f0 = half * (FT // 2)
                link(nc.vector.tensor_tensor(tv, t[5][:, f0:f0 + FT // 2].unsqueeze(2).to_broadcast([P, FT // 2, E]),
                                             sm[:, 3, 0:E].unsqueeze(1).to_broadcast([P, FT // 2, E]), ALU.is_ge))
                link(nc.vector.tensor_reduce(t[4][:, f0:f0 + FT // 2], tv, AX.X, ALU.add))
            link(nc.vector.tensor_scalar(t[4][:, 0:FT], t[4][:, 0:FT], float(E - 1), None, ALU.min))
            nc.vector.tensor_copy(te[:, :], t[4][:, 0:FT]).then_inc(pos_ready, 1)

            dve.wait_ge(cs_mm, 1)
            nc.vector.tensor_copy(t[2][:, :], bank[0][:, :]).then_inc(cs_copied, 1)
            dve.wait_ge(cs_copied, 1)
            top = -65536
            part = lambda k: csp[:, :, k * H:(k + 1) * H]
            link(nc.vector.tensor_scalar(t[3][:, :].bitcast(i32), t[2][:, :].bitcast(i32), top, None, ALU.bitwise_and))
            nc.vector.tensor_copy(part(0), c3(t[3][:, :]))
            link(nc.vector.tensor_tensor(t[3][:, :], t[2][:, :], t[3][:, :], ALU.subtract))
            link(nc.vector.tensor_scalar(t[4][:, :].bitcast(i32), t[3][:, :].bitcast(i32), top, None, ALU.bitwise_and))
            nc.vector.tensor_copy(part(1), c3(t[4][:, :]))
            nc.vector.tensor_tensor(part(2), c3(t[3][:, :]), c3(t[4][:, :]), ALU.subtract).then_inc(csp_ready, 1)
            dve.wait_ge(exps_done, 3)
            link(nc.vector.tensor_tensor(w_all[:, :, :], w_all[:, :, :], dt_all[:, :, :], ALU.mult))
            for g in range(8):
                dve.wait_ge(csT_done, g + 1)
                if g == 4:
                    dve.wait_ge(cs_stored, 16)
                nc.vector.tensor_copy(csT[:, (g % 4) * 1024:(g % 4 + 1) * 1024],
                                      bank[3 + g % 2][0:PARTS * H, :].bitcast(bf16)).then_inc(csT_evac, 1)
            fs = [0]

            def fl(ins):
                fs[0] += 1
                ins.then_inc(fstep, 1)
                dve.wait_ge(fstep, fs[0])

            for k in range(KT):
                dve.wait_ge(fw_loaded[k], 16)
                fl(nc.vector.tensor_scalar(fw[:, 0, k, :, :], fstage[:, k, :, :], WS, None, ALU.mult))
                last = nc.vector.scalar_tensor_tensor(fw[:, 1, k, :, :].rearrange("p e d -> p (e d)"), fstage[:, k, :, :].rearrange("p e d -> p (e d)"),
                                                      WS, fw[:, 0, k, :, :].rearrange("p e d -> p (e d)"), ALU.mult, ALU.subtract)
            last.then_inc(fw_split, 1)
            dve.wait_ge(fb_loaded, 16)
            f2 = lambda a: a.rearrange("p e d -> p (e d)")
            fl(nc.vector.tensor_scalar(f2(fb[0:64, :, :]), f2(fstage[0:64, 0, :, :]), WS, None, ALU.mult))
            nc.vector.scalar_tensor_tensor(f2(fb[32:64, :, :]), f2(fstage[32:64, 0, :, :]), WS, f2(fb[32:64, :, :]), ALU.mult, ALU.subtract).then_inc(fw_ready, 1)

            def lows(q):
                for r in range(4):
                    n = 4 * q + r
                    dve.wait_ge(fhi, n + 1)
                    nc.vector.tensor_tensor(fxT[:, r % 2, 1, :, :], bank[r % 2][:, 0:DM].rearrange("p (k t) -> p k t", k=KT),
                                            fxT[:, r % 2, 0, :, :], ALU.subtract).then_inc(flo, 1)

            with dve.Fori(0, FT // 4) as q:
                lows(q)
            for r in range(4):
                dve.wait_ge(g_stored[r], 16 * (FT // 4))
            dve.wait_ge(cs_stored, 32)
            for b in range(2):
                last = nc.vector.tensor_copy(csr[0:PARTS * H, b, :, :, :], blk[:, :, :].unsqueeze(2).to_broadcast([PARTS * H, H, CPS, P]))
            last.then_inc(main_const, 1)

            def conv(s, b, g, part):
                for tap, i in ((1, 0), (1, 1), (2, 0), (2, 1), (3, 0), (3, 1))[3 * part:3 * part + 3]:
                    m = 2 * g + i
                    if tap == 1:
                        dve.wait_ge(tap0, 6 * s + m + 1)
                    else:
                        dve.wait_ge(conv_step, 18 * s + 6 * g + 2 * (tap - 2) + i + 1)
                    nc.vector.scalar_tensor_tensor(xc[:, b, m, :], vraw[:, m, TAPS - 1 - tap:TAPS - 1 - tap + SEQ],
                                                   cw[:, m, TAPS - 1 - tap:TAPS - tap], xc[:, b, m, :], ALU.mult, ALU.add).then_inc(conv_step, 1)

            def finish(s, b, c):
                n = 4 * s + c
                i = c % 2
                dve.wait_ge(o_done, n + 1)
                dve.wait_ge(rstd_ready, n + 1)
                dve.wait_ge(xn_done, n + 1)
                if c == 0:
                    dve.wait_ge(g_loaded[b], 32 * (s - b) + 64)
                    dve.wait_ge(xin_loaded[b], 8 * (s - b) + 16)
                    if not (isinstance(s, int) and s == 0):
                        dve.wait_ge(out_stored, 16 * s)
                nc.vector.scalar_tensor_tensor(fo[:, i, :], bank[5][:, 0:DM], rstd[:, c:c + 1], xn[:, c, :], ALU.mult, ALU.add).then_inc(fin_step, 1)
                dve.wait_ge(fin_step, 3 * n + 1)
                nc.vector.tensor_tensor(fo[:, i, :], fo[:, i, :], gin[:, b, c, :], ALU.mult).then_inc(fin_step, 1)
                dve.wait_ge(fin_step, 3 * n + 2)
                nc.vector.tensor_tensor(ob[:, c, :], fo[:, i, :], xin[:, b, c, :], ALU.add).then_inc(fin_step, 1)

            h3 = lambda a: a.rearrange("p (h d) -> p h d", d=HD)
            hb = lambda a: a.unsqueeze(2).to_broadcast([P, H, HD])

            def front(n, c):
                dve.wait_ge(exp_done, n + 1)
                dve.wait_ge(B_done, n + 1)
                nc.vector.scalar_tensor_tensor(Em[:, c % 2, :, :], Em[:, c % 2, :, :], 1.0, bank[3][:, 0:P].unsqueeze(1).to_broadcast([P, H, P]),
                                               ALU.min, ALU.mult).then_inc(M_ready, 1)
                nc.vector.tensor_copy(BT[:, :], bank[3][:, P:2 * P]).then_inc(B_evac, 1)
                dve.wait_ge(xsT_evac, n + 1)
                nc.vector.tensor_tensor(h3(Xdt[:, c % 2, :]), h3(xsT[:, c % 2, :]), hb(w_of(dt_all, n)), ALU.mult).then_inc(X_ready, 1)

            def main(s, b, first, more):
                for c in range(CPS):
                    n = 4 * s + c
                    if c > 0:
                        dve.wait_ge(yoff_done, 3 * s + c)
                        nc.vector.tensor_tensor(h3(yo[:, :]), h3(bank[5][:, :]), hb(w_of(ea_all, n)), ALU.mult).then_inc(yo_ready, 1)
                        dve.wait_ge(yd_done, n + 1)
                        dve.wait_ge(yo_ready, 3 * s + c)
                        nc.vector.tensor_tensor(y[:, c % 2, :], bank[4][:, :], yo[:, :], ALU.add).then_inc(y_raw, 1)
                    else:
                        dve.wait_ge(yd_done, n + 1)
                        dve.wait_ge(xD_ready, n + 1)
                        nc.vector.tensor_tensor(y[:, c % 2, :], bank[4][:, :], xD[:, c % 2, :], ALU.add).then_inc(y_raw, 1)
                    if c < CPS - 1:
                        dve.wait_ge(snew_done, 3 * s + c + 1)
                        if c == 0:
                            nc.vector.tensor_copy(S[:, :], bank[5][:, :]).then_inc(S_ready, 1)
                        else:
                            dve.wait_ge(Sd_ready, 2 * s + c)
                            nc.vector.tensor_tensor(S[:, :], bank[5][:, :], Sd[:, :], ALU.add).then_inc(S_ready, 1)
                    nxt = c < CPS - 1 or more
                    conv_now = more and c < 3
                    late = c == CPS - 1
                    if late and not first_chunk(first, c):
                        finish(s, b, c - 1)
                    if nxt:
                        front(n + 1, (c + 1) % CPS)
                    if conv_now:
                        conv(s + 1, 1 - b, c, 0)
                        if c == 2:
                            conv(s + 1, 1 - b, c, 1)
                    if not late and not first_chunk(first, c):
                        if c == 0:
                            finish(s - 1, 1 - b, CPS - 1)
                        else:
                            finish(s, b, c - 1)
                    if conv_now and c < 2:
                        conv(s + 1, 1 - b, c, 1)

            for g in range(3):
                for part in range(2):
                    conv(0, 0, g, part)
            front(0, 0)
            main(0, 0, True, True)
            with dve.Fori(0, SEQS // 2 - 1) as p:
                main(2 * p + 1, 1, False, True)
                main(2 * p + 2, 0, False, True)
            main(SEQS - 1, 1, False, False)
            finish(SEQS - 1, 1, CPS - 1)

        @block.tensor
        def _(pe):
            mm, tr = nc.tensor.matmul, nc.tensor.transpose
            pe.wait_ge(const_ready, 1)
            pe.wait_ge(w_loaded, 64)
            n = 0
            for k in range(KT):
                for m, (c0, cn) in enumerate(wcols):
                    if n >= 2:
                        pe.wait_ge(wtr_evac, n - 1)
                    tr(bank[n % 2][:, 0:cn], wrow[0:cn, m, k * P:(k + 1) * P], ident[0:cn, 0:cn]).then_inc(wtr_done, 1)
                    n += 1
            for kc in range(ZT):
                pe.wait_ge(wtr_evac, n - 1)
                for m in range(KT):
                    last = tr(bank[n % 2][:, m * P:(m + 1) * P], worow[:, m, kc * P:(kc + 1) * P], ident[:, :])
                last.then_inc(wtr_done, 1)
                n += 1
            pe.wait_ge(wtr_evac, n - 1)
            for k in range(KT):
                last = tr(bank[n % 2][:, k * E:(k + 1) * E], sig[0:E, k * P:(k + 1) * P], ident[0:E, 0:E])
            last.then_inc(wtr_done, 1)
            pe.wait_ge(nb_ready, 1)
            pe.wait_ge(wtr_evac, 2 * NW)
            for k in range(KT):
                mm(bank[2][:, :], nbrep[:, k, :], wT[:, k, 0:DI], start=(k == 0), stop=(k == KT - 1))
            for m in range(XT):
                for k in range(KT):
                    mm(bank[3][:, m:m + 1], wT[:, k, DI + m * P:DI + (m + 1) * P], nwb[:, 1, k:k + 1], start=(k == 0), stop=(k == KT - 1))
            for k in range(KT):
                last = mm(bank[4][:, 0:H], nbrep[:, k, :], wT[:, k, DPROJ - H:DPROJ], start=(k == 0), stop=(k == KT - 1))
            last.then_inc(bias_mm, 1)
            pe.wait_ge(setup_done, 2)

            def scores(j, r):
                pe.wait_ge(lo_ready, j + 1)
                for c in range(CPS):
                    o = (r % 2) * 512 + c * 2 * H
                    terms = [(xTs[:, r % 2, a, k, c * P:(c + 1) * P], w[:, k, :]) for k in range(KT) for a, w in ((0, mhi), (1, mhi), (0, mlo))]
                    for i, (lhs, rhs) in enumerate(terms):
                        last = mm(bankL[:, o:o + 2 * H], lhs, rhs, start=(i == 0), stop=(i == len(terms) - 1))
                last.then_inc(sc_done, 1)

            def first_pass(q, first):
                for r in range(4):
                    j = 4 * q + r
                    if not (first and r == 0):
                        scores(j - 1, (r - 1) % 4)
                    pe.wait_ge(x1_ready, j + 1)
                    for c in range(CPS):
                        for k in range(KT):
                            last = tr(bank[2 * (r % 2) + k][:, c * P:(c + 1) * P], x1g[:, r % 2, c, k * P:(k + 1) * P], ident[:, :])
                    last.then_inc(T_done, 1)

            first_pass(0, True)
            with pe.Fori(1, 4) as q:
                first_pass(q, False)
            scores(SEQS - 1, 3)
            pe.wait_ge(oh_ready, 1)
            mm(bankL[:, 0:512], stri_b[:, :], ohb[:, :], start=True, stop=True)
            mm(bankL[:, 512:1024], ones_b[:, :], ohb[:, :], start=True, stop=True).then_inc(rank_mm, 1)
            pe.wait_ge(a_ready, 1)
            for i, m in enumerate((tri, ones, suf)):
                last = mm(bank[i][:, :], m[:, :], t[0][:, :], start=True, stop=True)
            last.then_inc(cs_mm, 1)
            pe.wait_ge(csp_ready, 1)
            for g in range(8):
                if g >= 2:
                    pe.wait_ge(csT_evac, g - 1)
                for i in range(8):
                    last = tr(bank[3 + g % 2][0:PARTS * H, :].bitcast(bf16)[:, i * P:(i + 1) * P], csp[:, 8 * g + i, :], ident_b[:, :])
                last.then_inc(csT_done, 1)
            pe.wait_ge(pos_ready, 1)
            pe.wait_ge(fw_ready, 1)

            def transposes(n, r, q):
                pe.wait_ge(ft_loaded[r], 16 * (q + 1))
                for k in range(KT):
                    last = tr(bank[r % 2][:, k * P:(k + 1) * P], ft[:, r, k * P:(k + 1) * P], ident[:, :])
                last.then_inc(fT_done, 1)

            def experts(q, more, first):
                for r in range(4):
                    n = 4 * q + r
                    if r < 3:
                        transposes(n + 1, r + 1, q)
                    elif more:
                        transposes(n + 1, 0, q + 1)
                    e = nc.tensor.value_load(te[0:1, bass.ds(n, 1)], min_val=0, max_val=E - 1)
                    pe.wait_ge(flo, n + 1)
                    if not (first and r < 2):
                        pe.wait_ge(fsilu, n - 1)
                    o = bank[2 + r % 2][:, 0:DM]
                    mm(o, pick[:, :], fb[:, bass.ds(e, 1), :].rearrange("p e d -> p (e d)"), start=True, stop=False)
                    i = 0
                    for k in range(KT):
                        for a, w in ((0, 0), (1, 0), (0, 1)):
                            i += 1
                            last = mm(o, fxT[:, r % 2, a, k, :], fw[:, w, k, bass.ds(e, 1), :].rearrange("p e d -> p (e d)"),
                                      start=False, stop=(i == 3 * KT))
                    last.then_inc(fmm, 1)

            transposes(0, 0, 0)
            experts(0, True, True)
            with pe.Fori(1, FT // 4 - 1) as q:
                experts(q, True, False)
            experts(FT // 4 - 1, False, False)
            pe.wait_ge(main_const, 3)

            def in_proj(s, b, u, first):
                if u == 0:
                    pe.wait_ge(xT_loaded[b], 8 * (s - b) + 16)
                if not (first and u < 2):
                    pe.wait_ge(inproj_evac, 10 * s + u - 1)
                o = bank[u % 2][:, :]
                i = 0
                if u >= XT:
                    mm(o, pick[:, :], zbias[:, :], start=True, stop=False)
                for k in range(KT):
                    for a, w in ((0, 0), (1, 0), (0, 1)):
                        i += 1
                        if u < XT:
                            last = mm(o, wz[:, w, k, DI + u * P:DI + (u + 1) * P], xT[:, b, a, k, :], start=(i == 1), stop=(i == 3 * KT))
                        else:
                            c = u - XT
                            last = mm(o, xT[:, b, a, k, c * P:(c + 1) * P], wz[:, w, k, 0:DI], start=False, stop=(i == 3 * KT))
                last.then_inc(inproj_done, 1)

            def yT_in(n, c):
                pe.wait_ge(gated, n + 1)
                for k in range(ZT):
                    last = tr(bank[2][:, k * P:(k + 1) * P], y[:, c % 2, k * P:(k + 1) * P], ident[:, :])
                last.then_inc(yT_done, 1)

            def out_proj(n):
                pe.wait_ge(yT_evac, n + 1)
                for k in range(ZT):
                    last = mm(bank[5][:, 0:DM], yT[:, k, :], wo[:, k, :], start=(k == 0), stop=(k == ZT - 1))
                last.then_inc(o_done, 1)

            def x_by_token(n, b, c, s, head):
                if c == 0:
                    pe.wait_ge(xc_ready, s + 1)
                if not head:
                    pe.wait_ge(xsT_evac, n)
                    if not (isinstance(n, int) and n < 2):
                        pe.wait_ge(yT_evac, n - 1)
                for k in range(ZT):
                    last = tr(bank[2][:, k * P:(k + 1) * P], xc[:, b, k, c * P:(c + 1) * P], ident[:, :])
                last.then_inc(xsT_done, 1)

            def decay(n, b, c, s, head):
                if not head:
                    pe.wait_ge(exp_done, n)
                if c == 0:
                    pe.wait_ge(cs_loaded[b], 16 * (s - b) + 32)
                for half in range(2):
                    hs = slice(half * 4, half * 4 + 4)
                    o = bankL[:, half * 512:(half + 1) * 512]
                    mm(o, csl[0:PARTS * H + PARTS, b, c * P:(c + 1) * P], csr[0:PARTS * H + PARTS, b, hs, c, :], start=True, stop=False)
                    last = mm(o, ident_b[:, :], maskneg[:, :].unsqueeze(1).to_broadcast([P, 4, P]), start=False, stop=True)
                last.then_inc(L_done, 1)

            def CB(n, b, c, head):
                tok = slice(c * P, (c + 1) * P)
                if not head:
                    pe.wait_ge(B_evac, n)
                mm(bank[3][:, 0:P], xc[:, b, ZT, tok], xc[:, b, ZT + 1, tok], start=True, stop=True)
                tr(bank[3][:, P:2 * P], xc[:, b, ZT, tok], ident[:, :]).then_inc(B_done, 1)

            def main(s, b, first, more, more2):
                for c in range(CPS):
                    n = 4 * s + c
                    tok = slice(c * P, (c + 1) * P)
                    def c_state():
                        if not (first and c < 2):
                            pe.wait_ge(fin_step, 3 * (n - 2) + 1)
                        pe.wait_ge(S_ready, 3 * s + c)
                        mm(bank[5][:, :], xc[:, b, ZT + 1, tok], S[:, :], start=True, stop=True).then_inc(yoff_done, 1)

                    if c in (1, 2):
                        c_state()
                    pe.wait_ge(X_ready, n + 1)
                    pe.wait_ge(M_ready, n + 1)
                    for h in range(H):
                        last = mm(bank[4][:, h * HD:(h + 1) * HD], Em[:, c % 2, h, :], Xdt[:, c % 2, h * HD:(h + 1) * HD], start=True, stop=True)
                    last.then_inc(yd_done, 1)
                    if c == 3:
                        c_state()
                    if c < CPS - 1:
                        decay(n + 1, b, c + 1, s, False)
                        x_by_token(n + 1, b, c + 1, s, False)
                        pe.wait_ge(Xw_ready, 3 * s + c + 1)
                        pe.wait_ge(B_evac, n + 1)
                        if c > 0:
                            pe.wait_ge(yo_ready, 3 * s + c)
                        elif not first:
                            pe.wait_ge(fin_step, 3 * (n - 2) + 1)
                        mm(bank[5][:, :], BT[:, :], Xw[:, c % 2, :], start=True, stop=True).then_inc(snew_done, 1)
                        CB(n + 1, b, c + 1, False)
                    elif more:
                        decay(n + 1, 1 - b, 0, s + 1, False)
                    now = units(c, b, more, more2)
                    if c < CPS - 1:
                        for ds, bb, u in now[:1]:
                            in_proj(s + ds, bb, u, False)
                        now = now[1:]
                    if not first_chunk(first, c):
                        if c < CPS - 1:
                            pe.wait_ge(S_ready, 3 * s + c + 1)
                        else:
                            pe.wait_ge(yo_ready, 3 * s + c)
                        out_proj(n - 1)
                    if c == CPS - 1 and more:
                        x_by_token(n + 1, 1 - b, 0, s + 1, False)
                        CB(n + 1, 1 - b, 0, False)
                    for ds, bb, u in now:
                        in_proj(s + ds, bb, u, False)
                    if c < CPS - 1 or more:
                        pe.wait_ge(xsT_evac, n + 2)
                    yT_in(n, c)

            for u in range(XT + CPS):
                in_proj(0, 0, u, True)
            for u in range(2):
                in_proj(1, 1, u, False)
            decay(0, 0, 0, 0, True)
            x_by_token(0, 0, 0, 0, True)
            CB(0, 0, 0, True)
            main(0, 0, True, True, True)
            with pe.Fori(0, SEQS // 2 - 2) as p:
                main(2 * p + 1, 1, False, True, True)
                main(2 * p + 2, 0, False, True, True)
            main(SEQS - 3, 1, False, True, True)
            main(SEQS - 2, 0, False, True, False)
            main(SEQS - 1, 1, False, False, False)
            pe.wait_ge(fin_step, 3 * (NCH - 2) + 1)
            out_proj(NCH - 1)


def units(c, b, more, more2):
    if c == CPS - 1:
        return [(2, b, u) for u in (0, 1)] if more2 else []
    return [(1, 1 - b, u) for u in ((2, 3, 4), (5, 6, 7), (8, 9))[c]] if more else []


def first_chunk(first, c):
    return first and c == 0


def w_of(a, n):
    return a[:, bass.ds(n, 1), :].rearrange("p o h -> p (o h)") if not isinstance(n, int) else a[:, n, :]


def st_of(a, n, k):
    return a[:, bass.ds(n, 1), k:k + 1].rearrange("p o k -> p (o k)") if not isinstance(n, int) else a[:, n, k:k + 1]


def row_of(a, n):
    return a[:, bass.ds(n, 1), :].rearrange("p o d -> p (o d)") if not isinstance(n, int) else a[:, n, :]


_INS = ["L0_attn_x", "L0_attn_norm_w", "L0_attn_norm_b", "L0_attn_in_proj_w", "L0_attn_conv_w", "L0_attn_conv_b", "L0_attn_dt_bias",
        "L0_attn_A_log", "L0_attn_D", "L0_attn_rms_w", "L0_attn_out_proj_w", "L0_ffn_tile_sigs", "L0_ffn_W", "L0_ffn_b"]


def kernel(**inputs):
    import concourse.bacc as _bacc
    from concourse.bass_utils import run_bass_kernel_spmd as _run

    nc = _bacc.Bacc("TRN2", target_bir_lowering=False, num_devices=1)
    arrays, args = {}, []
    for name in _INS:
        a = np.ascontiguousarray(inputs[name])
        arrays[f"in_{name}"] = a
        args.append(nc.dram_tensor(f"in_{name}", a.shape, mybir.dt.from_np(a.dtype), kind="ExternalInput").ap())
    out = nc.dram_tensor("out_0", (SEQS, SEQ, DM), mybir.dt.float32, kind="ExternalOutput").ap()
    program(nc, *args, out)
    r = _run(nc, [arrays], core_ids=[0])
    return r.results[0]["out_0"]
```

```python
import concourse.bass as bass
from concourse import mybir
from contextlib import ExitStack
import numpy as np

P = 128
SEQS, SEQ, DM = 16, 512, 256
TOK = SEQS * SEQ
NCH = TOK // P
CPS = SEQ // P
KT = DM // P
H, HD, NST = 8, 64, 128
DI = H * HD
ZT = DI // P
XT = (DI + 2 * NST) // P
DPROJ = 2 * DI + 2 * NST + H
TAPS = 4
E = 8
FT = NCH + E
ACT_X1 = 2
FG = 8
WEIGHTS_REST, ROWS_REST = 2384 + 1536, 1024
EPS = 1e-5
WS = 64.0
PARTS = 3


def program(nc, x, norm_w, norm_b, in_proj_w, conv_w, conv_b, dt_bias, A_log, D, rms_w, out_proj_w,
            tile_sigs, ffn_W, ffn_b, out):
    fp32, fp16, bf16, i32 = mybir.dt.float32, mybir.dt.float16, mybir.dt.bfloat16, mybir.dt.int32
    ACT, ALU, AX = mybir.ActivationFunctionType, mybir.AluOpType, mybir.AxisListType

    xT_d = nc.dram_tensor("xT_scratch", (SEQS, P, 2 * KT * SEQ), fp16).ap()
    cs_d = nc.dram_tensor("cs_scratch", (PARTS * H, TOK), bf16).ap()
    sorted_d = nc.dram_tensor("sorted_scratch", (FT * P, DM), fp32).ap()
    gate_d = nc.dram_tensor("gate_scratch", (FT * P, DM), fp32).ap()

    x_g = x.rearrange("b (c p) d -> b p c d", p=P)
    out_g = out.rearrange("b (c p) d -> b p c d", p=P)

    ctx = ExitStack()
    with ctx:
        def sem(name):
            return ctx.enter_context(nc.semaphore(name))

        def sbuf(stack, name, shape, dt=fp32):
            return stack.enter_context(nc.sbuf_tensor(name, shape, dt))

        bankL = ctx.enter_context(nc.psum_tensor("bankL", [P, 2 * 512], fp32))
        bank = [ctx.enter_context(nc.psum_tensor(f"bank{i}", [P, 512], fp32)) for i in range(6)]

        ident = sbuf(ctx, "ident", [P, P])
        ident_b = sbuf(ctx, "ident_b", [P, P], bf16)
        wz = sbuf(ctx, "w_in", [P, 2, KT, DPROJ], fp16)
        wo = sbuf(ctx, "w_out", [P, 2, ZT, DM], fp16)
        zbias = sbuf(ctx, "zbias", [P, DI], fp16)
        pick = sbuf(ctx, "pick", [P, P], fp16)
        xbias = sbuf(ctx, "xbias", [P, XT])
        cw = sbuf(ctx, "cw", [P, XT, TAPS])
        cb = sbuf(ctx, "cb", [P, XT])
        D_bc = sbuf(ctx, "D_bc", [P, H])
        blk = sbuf(ctx, "blk", [P, H, P], bf16)
        later = sbuf(ctx, "later", [P, 2, P], bf16)
        norm_st = sbuf(ctx, "norm_st", [P, NCH, 2])
        dt_all = sbuf(ctx, "dt_all", [P, NCH, H])
        w_all = sbuf(ctx, "w_all", [P, NCH, H])
        ea_all = sbuf(ctx, "ea_all", [P, NCH, H])
        tot_all = sbuf(ctx, "tot_all", [P, NCH, H])
        pos_all = sbuf(ctx, "pos_all", [P, NCH], i32)
        epsc = sbuf(ctx, "epsc", [P, 1])
        mhalf = sbuf(ctx, "mhalf", [P, 8])

        low_stack, high_stack = ExitStack(), ExitStack()
        sd_all = sbuf(low_stack, "sd_all", [P, NCH, 2 * H])
        mhi = sbuf(low_stack, "mhi", [P, KT, 2 * H], fp16)
        mlo = sbuf(low_stack, "mlo", [P, KT, 2 * H], fp16)
        dtb = sbuf(low_stack, "dtb", [P, H])
        a_bc = sbuf(low_stack, "a_bc", [P, H])
        nwb = sbuf(low_stack, "nwb", [P, 2, KT])
        rev = sbuf(low_stack, "rev", [P, E])
        octal = sbuf(low_stack, "octal", [P, FG])
        tri = sbuf(low_stack, "tri", [P, P])
        suf = sbuf(low_stack, "suf", [P, P])
        ones = sbuf(low_stack, "ones", [P, P])
        ones_b = sbuf(low_stack, "ones_b", [P, P], bf16)
        stri_b = sbuf(low_stack, "stri_b", [P, P], bf16)
        zrow = sbuf(low_stack, "zrow", [P, DM * 4])
        xg = sbuf(low_stack, "xg", [P, 4, CPS, DM])
        w_stack = ExitStack()
        wrow = sbuf(w_stack, "wrow", [P, 11, DM])
        wT = sbuf(w_stack, "wT", [P, KT, DPROJ])
        worow = sbuf(w_stack, "worow", [P, KT, DI])
        wo32 = sbuf(w_stack, "wo32", [P, ZT, DM])
        rmsw = sbuf(w_stack, "rmsw", [P, ZT])
        sig = sbuf(w_stack, "sig", [P, DM])
        neg = sbuf(w_stack, "neg", [P, KT, E])
        nbrep = sbuf(w_stack, "nbrep", [P, KT, P])
        nw64 = sbuf(w_stack, "nw64", [P, KT])
        w_stack.close()
        p1_stack = ExitStack()
        nb1 = sbuf(p1_stack, "nb1", [P, 2, CPS, 1])
        x1g = sbuf(p1_stack, "x1g", [P, 2, CPS, DM])
        xTs = sbuf(p1_stack, "xTs", [P, 2, 2, KT, SEQ], fp16)
        bst = sbuf(p1_stack, "bst", [P, 2, CPS, 6])
        mv = sbuf(p1_stack, "mv", [P, 2, CPS, 2])
        var2 = sbuf(p1_stack, "var2", [P, 2, CPS, 2])
        rs2 = sbuf(p1_stack, "rs2", [P, 2, CPS, 2])
        p1_stack.close()
        t = [sbuf(low_stack, f"t{i}", [P, NCH * H]) for i in range(5)]
        csp = sbuf(low_stack, "csp", [P, NCH, PARTS * H], bf16)
        csT = sbuf(low_stack, "csT", [PARTS * H, TOK], bf16)
        rt = [sbuf(low_stack, f"rt{i}", [P, NCH * H]) for i in range(3)]
        ohb = sbuf(low_stack, "ohb", [P, NCH * E], bf16)
        keep = sbuf(low_stack, "keep", [P, E, NCH])
        sm = sbuf(low_stack, "sm", [P, 6, NCH])
        smi = sbuf(low_stack, "smi", [P, E], i32)
        tile_no = sbuf(low_stack, "tile_no", [P, FT])
        tmp_te = sbuf(low_stack, "tmp_te", [P, FT])
        wide_te = sbuf(low_stack, "wide_te", [P, FT // 2 * E])
        fstage = sbuf(low_stack, "fstage", [P, E, DM])
        fw = sbuf(high_stack, "ffn_w", [P, 2, KT, E, DM], fp16)
        fb = sbuf(high_stack, "ffn_b", [P, E, DM], fp16)
        te = sbuf(high_stack, "tile_expert", [P, FT // FG], i32)
        rows_stack = ExitStack()
        xn_all = sbuf(rows_stack, "xn_all", [P, NCH, DM])
        sx = sbuf(rows_stack, "sx", [P, 4, CPS, DM])
        idx = sbuf(rows_stack, "idx", [P, 4, CPS], i32)
        rows_stack.close()
        ft = sbuf(high_stack, "ffn_x", [P, FG, DM])
        fxT = sbuf(high_stack, "ffn_xT", [P, 4, 2, KT, P], fp16)
        gt = sbuf(high_stack, "ffn_gate", [P, 4, DM])
        high_stack.close()
        low_stack.close()

        xT = sbuf(ctx, "xT", [P, 2, 2, KT, SEQ], fp16)
        vraw = sbuf(ctx, "vraw", [P, XT, TAPS - 1 + SEQ])
        xc = sbuf(ctx, "xc", [P, 2, XT, SEQ])
        sz = sbuf(ctx, "sz", [P, 2, CPS, DI])
        y = sbuf(ctx, "y", [P, 2, DI])
        yo = sbuf(ctx, "yo", [P, DI])
        S = sbuf(ctx, "S", [P, DI])
        Sd = sbuf(ctx, "Sd", [P, DI])
        yT = sbuf(ctx, "yT", [P, 2, DI], fp16)
        yn = sbuf(ctx, "yn", [P, DI])
        ysq = sbuf(ctx, "ysq", [P, DI])
        xn = sbuf(ctx, "xn", [P, CPS, DM])
        ssq = sbuf(ctx, "ssq", [P, CPS])
        ms = sbuf(ctx, "ms", [P, CPS])
        rstd = sbuf(ctx, "rstd", [P, CPS])
        gidx = sbuf(ctx, "gidx", [P, 2, CPS], i32)
        sbuf(ctx, "expert_weights_rest", [P, WEIGHTS_REST])
        fo = sbuf(ctx, "fo", [P, 2, DM])
        gin = sbuf(ctx, "gin", [P, 2, CPS, DM])
        ob = sbuf(ctx, "ob", [P, CPS, DM])
        sbuf(ctx, "expert_rows_rest", [P, ROWS_REST])
        xin = sbuf(ctx, "xin", [P, 2, CPS, DM])
        csl = sbuf(ctx, "csl", [P, 2, 2, SEQ], bf16)
        csr = sbuf(ctx, "csr", [P, 2, H, CPS, P], bf16)
        Em = sbuf(ctx, "Em", [P, 2, H, P])
        xsT = sbuf(ctx, "xsT", [P, 2, DI])
        Xdt = sbuf(ctx, "Xdt", [P, 2, DI])
        Xw = sbuf(ctx, "Xw", [P, 2, DI])
        xD = sbuf(ctx, "xD", [P, 2, DI])
        BT = sbuf(ctx, "BT", [P, NST])

        w_loaded, small_loaded, fw_loaded = sem("w_loaded"), sem("small_loaded"), [sem("fw_loaded0"), sem("fw_loaded1")]
        fb_loaded, fw_split, fstep, fw_ready, st_ready = (sem(n) for n in ("fb_loaded", "fw_split", "ffn_weight_step", "fw_ready", "st_ready"))
        xs_ready, x1_ready_act = sem("xs_ready"), sem("x1_ready_act")
        yT_lo, yn_ready = sem("yT_lo"), sem("yn_ready")
        te_ready, vraw_ready = sem("te_ready"), sem("vraw_ready")
        const_ready, pstep = sem("const_ready"), sem("pool_setup_step")
        wtr_done, wtr_evac = sem("wtr_done"), sem("wtr_evac")
        wlink, bias_mm, nb_ready = sem("setup_vector_step"), sem("bias_mm"), sem("nb_ready")
        setup_done, zero_written, z_ready = sem("setup_done"), sem("zero_written"), sem("zeros_ready")
        x_loaded = [sem(f"x_loaded{r}") for r in range(4)]
        aggr_go, scatter_go, gather_go = sem("aggr_go"), sem("scatter_go"), sem("gather_go")
        stats, aggr, var_ready, rs_ready, x1_ready, xn_ready = (
            sem(n) for n in ("stats_done", "aggr_done", "var_ready", "rs_ready", "x1_ready", "xn_ready"))
        T_done, hi_ready, lo_ready, sc_done, sd_ready = (sem(n) for n in ("T_done", "hi_ready", "lo_ready", "sc_done", "sd_ready"))
        xT_stored = [sem(f"xT_stored{r}") for r in range(2)]
        vstep, softexp_in, softexp_out, a_ready, cs_mm, cs_copied, exps_done = (sem(n) for n in (
            "vstep", "softexp_in", "softexp_out", "a_ready", "cs_mm", "cs_copied", "exps_done"))
        csp_ready, csT_done, csT_evac, cs_stored = (sem(n) for n in ("csp_ready", "csT_done", "csT_evac", "cs_stored"))
        oh_ready, rank_mm, pos_ready = (sem(n) for n in ("oh_ready", "rank_mm", "pos_ready"))
        sx_loaded = [sem(f"sx_loaded{r}") for r in range(4)]
        scattered = [sem(f"scattered{r}") for r in range(4)]
        ft_loaded = [sem(f"ft_loaded{r}") for r in range(FG)]
        fT_done, fhi, flo, fmm, fsilu = (sem(n) for n in ("fT_done", "ffn_hi", "ffn_lo", "ffn_mm", "ffn_silu"))
        g_stored = [sem(f"g_stored{r}") for r in range(4)]
        main_const = sem("main_const")
        xT_loaded = [sem(f"xT_loaded{b}") for b in range(2)]
        cs_loaded = [sem(f"cs_loaded{b}") for b in range(2)]
        xin_loaded = [sem(f"xin_loaded{b}") for b in range(2)]
        g_loaded = [sem(f"g_loaded{b}") for b in range(2)]
        inproj_done, inproj_evac, tap0, conv_step, xc_ready, sz_ready = (sem(n) for n in (
            "inproj_done", "inproj_evac", "tap0_ready", "conv_step", "xc_ready", "sz_ready"))
        xsT_done, xsT_evac, L_done, exp_done, B_done, B_evac, G_done = (sem(n) for n in (
            "xsT_done", "xsT_evac", "L_done", "exp_done", "B_done", "B_evac", "G_done"))
        yoff_done, yd_done, snew_done, yT_done, yT_hi, o_done = (sem(n) for n in (
            "yoff_done", "yd_done", "snew_done", "yT_done", "yT_hi", "o_done"))
        X_ready, M_ready, yo_ready, y_raw, S_ready, fin_step = (sem(n) for n in (
            "X_ready", "M_ready", "yo_ready", "y_raw", "S_ready", "fin_step"))
        Xw_ready, xD_ready, Sd_ready, yD_ready, gated, sq_done, ms_ready, rstd_ready, gidx_ready, xn_done = (sem(n) for n in (
            "Xw_ready", "xD_ready", "Sd_ready", "yD_ready", "gated", "sq_done", "ms_ready", "rstd_ready", "gidx_ready", "xn_done"))
        out_stored = sem("out_stored")

        NW = 11
        wcols = [(i * P, min(P, DPROJ - i * P)) for i in range(NW)]
        N_SMALL = 16 * 11

        f_in = lambda r: (bank[0], bank[1], bank[4], bank[5])[r % 4][:, 0:DM]
        f_out = lambda r: (bank[2][:, 0:DM], bank[3][:, 0:DM], bankL[:, 0:DM], bankL[:, 512:512 + DM])[r % 4]

        block = ctx.enter_context(nc.Block())

        @block.sync
        def _(sp):
            sp.dma_start(wrow[:, 0:10, :], in_proj_w[0:10 * P, :].rearrange("(m p) d -> p m d", p=P)).then_inc(w_loaded, 16)
            sp.dma_start(wrow[0:H, 10, :], in_proj_w[10 * P:DPROJ, :]).then_inc(w_loaded, 16)
            sp.dma_start(worow[:, :, :], out_proj_w.rearrange("(m p) c -> p m c", p=P)).then_inc(w_loaded, 16)
            sp.dma_start(sig[0:E, :], tile_sigs).then_inc(w_loaded, 16)
            with nc.allow_non_contiguous_dma(reason="small vectors by channel"):
                sp.dma_start(nwb[:, 0, :], norm_w.rearrange("(k p) -> p k", p=P)).then_inc(small_loaded, 16)
                sp.dma_start(nwb[:, 1, :], norm_b.rearrange("(k p) -> p k", p=P)).then_inc(small_loaded, 16)
                sp.dma_start(rmsw[:, :], rms_w.rearrange("(k p) -> p k", p=P)).then_inc(small_loaded, 16)
                sp.dma_start(cw[:, :, :], conv_w.rearrange("(m p) t -> p m t", p=P)).then_inc(small_loaded, 16)
                sp.dma_start(cb[:, :], conv_b.rearrange("(m p) -> p m", p=P)).then_inc(small_loaded, 16)
                sp.dma_start(dtb[:, :], dt_bias.partition_broadcast(P)).then_inc(small_loaded, 16)
                sp.dma_start(a_bc[:, :], A_log.partition_broadcast(P)).then_inc(small_loaded, 16)
                sp.dma_start(D_bc[:, :], D.partition_broadcast(P)).then_inc(small_loaded, 16)
            for r in range(4):
                sp.dma_start(xg[:, r, :, :], x_g[r]).then_inc(x_loaded[r], 16)
            sp.dma_start(fstage[:, :, :], ffn_W[:, 0:P, :].rearrange("e p d -> p e d")).then_inc(fw_loaded[0], 16)
            def zeros(n):
                sp.dma_start(sorted_d.rearrange("(n p c) d -> n p (c d)", p=P, c=4)[n], zrow[:, :]).then_inc(zero_written, 16)

            sp.wait_ge(z_ready, 1)

            def first_pass(q, more):
                for r in range(4):
                    j = 4 * q + r
                    sp.wait_ge(xn_ready, j + 1)
                    sp.wait_ge(x1_ready, j + 1)
                    if more:
                        sp.dma_start(xg[:, r, :, :], x_g[j + 4]).then_inc(x_loaded[r], 16)
                    sp.wait_ge(lo_ready, j + 1)
                    sp.dma_start(xT_d[j], xTs[:, r % 2, :, :, :].rearrange("p a k t -> p (a k t)")).then_inc(xT_stored[r % 2], 16)
                    zeros(j)

            with sp.Fori(0, 3) as q:
                first_pass(q, True)
            first_pass(3, False)
            for n in range(SEQS, FT // 4):
                zeros(n)
            def rows(g, r, q):
                if q is not None:
                    sp.wait_ge(scattered[r], 16 * CPS * q)
                sp.dma_start(sx[:, r, :, :].rearrange("p c d -> p (c d)"),
                             xn_all[:, bass.ts(g, CPS), :].rearrange("p c d -> p (c d)")).then_inc(sx_loaded[r], 16)
                sp.dma_start(idx[:, r, :], pos_all[:, bass.ts(g, CPS)]).then_inc(sx_loaded[r], 16)

            sp.wait_ge(pos_ready, 1)
            for g in range(4):
                rows(g, g, None)
            with sp.Fori(1, SEQS // 4) as q:
                for r in range(4):
                    rows(4 * q + r, r, q)
            def load_rest(s, b):
                sp.dma_start(xin[:, b, :, :], x_g[s]).then_inc(xin_loaded[b], 16)
                src = cs_d.rearrange("r (s t) -> s r t", t=SEQ)[s]
                for f in range(2):
                    sp.dma_start(csl[0:PARTS * H, b, f, :], src).then_inc(cs_loaded[b], 16)
                sp.dma_start(csr[PARTS * H:PARTS * (H + 1), b, :, :, :].rearrange("o h c l -> o h (c l)"),
                             src.rearrange("(o h) t -> o h t", h=H)).then_inc(cs_loaded[b], 16)

            for r in range(4):
                sp.wait_ge(scattered[r], 16 * SEQS)
            for r in range(FG):
                sp.dma_start(ft[:, r, :], sorted_d[r * P:(r + 1) * P, :]).then_inc(ft_loaded[r], 16)

            def expert_io(q, more, first):
                for r in range(FG):
                    if first and r == 3:
                        sp.wait_ge(cs_stored, 16)
                        sp.wait_ge(main_const, 1)
                        load_rest(0, 0)
                    n = FG * q + r
                    if more:
                        sp.wait_ge(fT_done, n + 1)
                        sp.dma_start(ft[:, r, :], sorted_d.rearrange("(n p) d -> n p d", p=P)[n + FG]).then_inc(ft_loaded[r], 16)
                    sp.wait_ge(fsilu, n + 1)
                    sp.dma_start(gate_d.rearrange("(n p) d -> n p d", p=P)[n], gt[:, r % 4, :]).then_inc(g_stored[r % 4], 16)

            expert_io(0, True, True)
            with sp.Fori(1, FT // FG - 1) as q:
                expert_io(q, True, False)
            expert_io(FT // FG - 1, False, False)
            def load_seq(s, b):
                sp.dma_start(xT[:, b, :, :, :].rearrange("p a k t -> p (a k t)"), xT_d[s]).then_inc(xT_loaded[b], 16)

            def main_io(s, b, first, last):
                if not last:
                    if first:
                        sp.wait_ge(main_const, 2)
                    else:
                        sp.wait_ge(fin_step, 12 * s)
                    load_rest(s + 1, 1 - b)
                    sp.wait_ge(inproj_done, 10 * (s + 1))
                    if not isinstance(s, int) or s < SEQS - 2:
                        load_seq(s + 2, b)
                if not first:
                    sp.wait_ge(fin_step, 12 * s)
                    sp.dma_start(out_g[s - 1], ob[:, :, :]).then_inc(out_stored, 16)

            main_io(0, 0, True, False)
            with sp.Fori(0, SEQS // 2 - 2) as p:
                main_io(2 * p + 1, 1, False, False)
                main_io(2 * p + 2, 0, False, False)
            main_io(SEQS - 3, 1, False, False)
            main_io(SEQS - 2, 0, False, False)
            main_io(SEQS - 1, 1, False, True)
            sp.wait_ge(fin_step, 12 * SEQS)
            sp.dma_start(out_g[SEQS - 1], ob[:, :, :]).then_inc(out_stored, 16)
            sp.wait_ge(out_stored, 16 * SEQS)

        @block.gpsimd
        def _(pool):
            steps = [0]

            def link(ins):
                steps[0] += 1
                ins.then_inc(pstep, 1)
                pool.wait_ge(pstep, steps[0])

            link(pool.memset(ident[:, :], 0.0))
            pool.affine_select(out=ident[:, :], in_=ident[:, :], compare_op=ALU.not_equal, fill=1.0, base=0,
                               pattern=[[-1, P]], channel_multiplier=1).then_inc(const_ready, 1)
            pool.memset(zrow[:, :], 0.0).then_inc(z_ready, 1)
            pool.memset(tri[:, :], 1.0)
            pool.memset(suf[:, :], 1.0)
            pool.memset(ones[:, :], 1.0)
            pool.memset(ones_b[:, :], 1.0)
            pool.memset(stri_b[:, :], 1.0)
            pool.memset(later[:, :, :], 1.0)
            pool.memset(mhalf[:, :], -0.5)
            for i in range(FG):
                pool.memset(octal[:, i:i + 1], float(E ** i))
            pool.memset(epsc[:, :], EPS)
            pool.memset(blk[:, :, :], 0.0)
            pool.memset(pick[:, :], 0.0)
            pool.memset(zbias[:, :], 0.0)
            pool.memset(fb[:, :, :], 0.0)
            link(pool.memset(mlo[:, :, :], 0.0))
            link(pool.memset(pick[0:1, :], 1.0))
            link(pool.memset(pick[32:33, :], 1.0))
            pool.affine_select(out=tri[:, :], in_=tri[:, :], compare_op=ALU.is_ge, fill=0.0, base=0,
                               pattern=[[1, P]], channel_multiplier=-1)
            pool.affine_select(out=suf[:, :], in_=suf[:, :], compare_op=ALU.is_gt, fill=0.0, base=0,
                               pattern=[[-1, P]], channel_multiplier=1)
            pool.affine_select(out=stri_b[:, :], in_=stri_b[:, :], compare_op=ALU.is_gt, fill=0.0, base=0,
                               pattern=[[1, P]], channel_multiplier=-1)
            for f in range(2):
                link(pool.affine_select(out=later[:, f, :], in_=later[:, f, :], compare_op=ALU.is_ge, fill=0.0,
                                        base=P // 2 - 1 - f * (P // 2), pattern=[[1, P]], channel_multiplier=-1))
            pool.memset(later[0:P // 2, 1, :], 1.0)
            link(pool.affine_select(out=blk[:, :, :], in_=blk[:, :, :], compare_op=ALU.not_equal, fill=-1e30, base=-(P // 2),
                                    pattern=[[0, 2 * H], [-1, P // 2]], channel_multiplier=1))
            link(pool.iota(rev[:, :], pattern=[[-1, E]], base=E, channel_multiplier=0, allow_small_or_imprecise_dtypes=True))
            for part in range(PARTS):
                link(pool.affine_select(out=blk[:, :, :], in_=blk[:, :, :], compare_op=ALU.not_equal, fill=-1.0, base=-part * H,
                                        pattern=[[-1, H], [0, P]], channel_multiplier=1))
            pool.wait_ge(const_ready, 1)
            pool.tensor_copy(ident_b[:, :], ident[:, :]).then_inc(const_ready, 1)
            def roots(q):
                for r in range(4):
                    pool.wait_ge(var_ready, 4 * q + r + 1)
                    pool.tensor_tensor(rs2[:, r % 2, :, :], var2[:, r % 2, :, :], mhalf[:, :].rearrange("p (c k) -> p c k", k=2), ALU.pow).then_inc(rs_ready, 1)

            with pool.Fori(0, 4) as q:
                roots(q)
            pool.wait_ge(sd_ready, SEQS)
            pool.memset(keep[:, :, :], 1.0)
            link(pool.iota(tile_no[:, :], pattern=[[1, FT]], base=0, channel_multiplier=0, allow_small_or_imprecise_dtypes=True))
            pool.memset(keep[:, :, 0:1], 0.0).then_inc(const_ready, 1)
            def scatter(q):
                for r in range(4):
                    pool.wait_ge(sx_loaded[r], 32 * (q + 1))
                    pool.sem_inc(scatter_go, 1)
                    for c in range(CPS):
                        pool.indirect_dma_start(out=sorted_d, out_offset=bass.IndirectOffsetOnAxis(ap=idx[:, r, c:c + 1], axis=0),
                                                in_=sx[:, r, c, :], in_offset=None).then_inc(scattered[r], 16)

            pool.wait_ge(zero_written, 16 * (FT // 4))
            with pool.Fori(0, SEQS // 4) as q:
                scatter(q)
            for r in range(4):
                pool.wait_ge(scattered[r], 16 * SEQS)

            def x_products(s, c):
                n = 4 * s + c
                hb = lambda a: a.unsqueeze(2).to_broadcast([P, H, HD])
                xs3 = xsT[:, c % 2, :].rearrange("p (h d) -> p h d", d=HD)
                pool.wait_ge(xsT_evac, n + 1)
                if c < CPS - 1:
                    pool.tensor_tensor(Xw[:, c % 2, :].rearrange("p (h d) -> p h d", d=HD), xs3, hb(w_of(w_all, n)), ALU.mult).then_inc(Xw_ready, 1)
                pool.tensor_tensor(xD[:, c % 2, :].rearrange("p (h d) -> p h d", d=HD), xs3, hb(D_bc[:, :]), ALU.mult).then_inc(xD_ready, 1)
                if c in (1, 2):
                    pool.wait_ge(S_ready, 3 * s + c)
                    pool.tensor_tensor(Sd[:, :].rearrange("p (h d) -> p h d", d=HD), S[:, :].rearrange("p (h d) -> p h d", d=HD),
                                       hb(w_of(tot_all, n)), ALU.mult).then_inc(Sd_ready, 1)

            def root(n, c):
                pool.wait_ge(sq_done, n + 1)
                pool.tensor_tensor(ms[:, c:c + 1], ssq[:, c:c + 1], epsc[:, :], ALU.add).then_inc(ms_ready, 1)
                pool.wait_ge(ms_ready, n + 1)
                pool.tensor_tensor(rstd[:, c:c + 1], ms[:, c:c + 1], mhalf[:, 0:1], ALU.pow).then_inc(rstd_ready, 1)

            def gather(s, b, chunks, fin):
                if chunks[0] == 0:
                    if fin is not None:
                        pool.wait_ge(fin_step, fin)
                    pool.tensor_copy(gidx[:, b, :], pos_all[:, bass.ts(s, CPS)]).then_inc(gidx_ready, 1)
                    pool.wait_ge(gidx_ready, s + 1)
                    pool.sem_inc(gather_go, 1)
                for c in chunks:
                    pool.indirect_dma_start(out=gin[:, b, c, :], out_offset=None, in_=gate_d,
                                            in_offset=bass.IndirectOffsetOnAxis(ap=gidx[:, b, c:c + 1], axis=0)).then_inc(g_loaded[b], 16)

            def main(s, b, first, more):
                for c in range(CPS):
                    n = 4 * s + c
                    if not (first and c == 0):
                        root(n - 1, (c - 1) % CPS)
                    pool.wait_ge(y_raw, n + 1)
                    if c > 0:
                        pool.tensor_tensor(y[:, c % 2, :], y[:, c % 2, :], xD[:, c % 2, :], ALU.add).then_inc(yD_ready, 1)
                        pool.wait_ge(yD_ready, 3 * s + c)
                    if c == 0:
                        pool.wait_ge(sz_ready, s + 1)
                        pool.wait_ge(inproj_evac, 10 * (s + 1))
                    pool.tensor_tensor(y[:, c % 2, :], y[:, c % 2, :], sz[:, b, c, :], ALU.mult).then_inc(gated, 1)
                    if first and c == 0:
                        for r in range(4):
                            pool.wait_ge(g_stored[r], 16 * (FT // 4))
                        gather(0, 0, (0, 1, 2, 3), None)
                    if c < CPS - 1:
                        x_products(s, c + 1)
                    elif more:
                        x_products(s + 1, 0)
                    if more and c > 1:
                        gather(s + 1, 1 - b, ((0, 1), (2, 3))[c - 2], None if first else 12 * s)

            x_products(0, 0)
            main(0, 0, True, True)
            with pool.Fori(0, SEQS // 2 - 1) as p:
                main(2 * p + 1, 1, False, True)
                main(2 * p + 2, 0, False, True)
            main(SEQS - 1, 1, False, False)
            root(NCH - 1, CPS - 1)

        @block.scalar
        def _(act):
            n = 0
            for k in range(KT):
                for m, (c0, cn) in enumerate(wcols):
                    act.wait_ge(wtr_done, n + 1)
                    act.activation(wT[:, k, c0:c0 + cn], (bank[0], bank[1], bank[5])[n % 3][:, 0:cn], ACT.Copy).then_inc(wtr_evac, 1)
                    n += 1
            act.wait_ge(small_loaded, 16 * 8)
            for kc in range(ZT):
                act.wait_ge(wtr_done, n + 1)
                act.activation(wo32[:, kc, :], (bank[0], bank[1], bank[5])[n % 3][:, 0:DM], ACT.Identity, scale=rmsw[:, kc:kc + 1]).then_inc(wtr_evac, 1)
                n += 1
            act.wait_ge(wtr_done, n + 1)
            act.activation(neg[:, :, :], (bank[0], bank[1], bank[5])[n % 3][:, 0:KT * E].rearrange("p (k e) -> p k e", e=E), ACT.Copy).then_inc(wtr_evac, 1)
            act.activation(a_bc[:, :], a_bc[:, :], ACT.Exp).then_inc(setup_done, 1)

            def highs(q):
                for r in range(4):
                    j = 4 * q + r
                    act.wait_ge(st_ready, j + 1)
                    for c in range(CPS - ACT_X1, CPS):
                        last = act.activation(x1g[:, r % 2, c, :], xg[:, r, c, :], ACT.Identity, bias=nb1[:, r % 2, c, :], scale=rs2[:, r % 2, c, 1:2])
                    last.then_inc(x1_ready_act, 1)
                    for c in range(CPS):
                        last = act.activation(row_of(xn_all, 4 * j + c), xg[:, r, c, :], ACT.Identity, bias=st_of(norm_st, 4 * j + c, 1),
                                              scale=st_of(norm_st, 4 * j + c, 0))
                    last.then_inc(xn_ready, 1)
                    act.wait_ge(T_done, j + 1)
                    act.wait_ge(xT_stored[r % 2], 16 * (2 * q + r // 2 + 1))
                    for k in range(KT):
                        act.activation(xTs[:, r % 2, 0, k, :], bank[2 * (r % 2) + k][:, :], ACT.Copy).then_inc(hi_ready, 1)

            act.sem_inc(xT_stored[0], 16)
            act.sem_inc(xT_stored[1], 16)
            with act.Fori(0, 4) as q:
                highs(q)
            act.wait_ge(softexp_in, 1)
            act.activation(t[1][:, :], t[1][:, :], ACT.Exp).then_inc(softexp_out, 1)
            act.wait_ge(cs_copied, 1)
            act.activation(ea_all[:, :, :].rearrange("p c h -> p (c h)"), t[2][:, :], ACT.Exp).then_inc(exps_done, 1)
            act.activation(tot_all[:, :, :].rearrange("p c h -> p (c h)"), bank[1][:, :], ACT.Exp).then_inc(exps_done, 1)
            act.activation(w_all[:, :, :].rearrange("p c h -> p (c h)"), bank[2][:, :], ACT.Exp).then_inc(exps_done, 1)

            act.wait_ge(csT_evac, 8)
            act.dma_start(cs_d, csT[:, :]).then_inc(cs_stored, 16)
            act.wait_ge(cs_stored, 16)
            act.wait_ge(zero_written, 16 * (FT // 4))
            for b in range(2):
                act.wait_ge(xT_stored[b], 16 * (SEQS // 2 + 1))
            for b in range(2):
                act.dma_start(xT[:, b, :, :, :].rearrange("p a k t -> p (a k t)"), xT_d[b]).then_inc(xT_loaded[b], 16)
            act.wait_ge(fw_split, 1)
            act.dma_start(fstage[:, :, :], ffn_W[:, P:2 * P, :].rearrange("e p d -> p e d")).then_inc(fw_loaded[1], 16)
            def evac(s, b, u, first, early):
                act.wait_ge(inproj_done, 10 * s + u + 1)
                if u < XT:
                    if not first:
                        act.wait_ge(conv_step, 18 * (s - 1) + 6 * (u // 2 + 1))
                    act.activation(vraw[:, u, TAPS - 1:], bank[u % 2][:, :], ACT.Identity, bias=xbias[:, u:u + 1], scale=1.0 / WS).then_inc(inproj_evac, 1)
                    act.wait_ge(inproj_evac, 10 * s + u + 1)
                    act.activation(xc[:, b, u, :], vraw[:, u, TAPS - 1:], ACT.Identity, bias=cb[:, u:u + 1],
                                   scale=cw[:, u, TAPS - 1:TAPS]).then_inc(tap0, 1)
                else:
                    act.activation(sz[:, b, u - XT, :], bank[u % 2][:, :], ACT.Silu if early or u >= XT + 2 else ACT.Copy, scale=1.0 / WS).then_inc(inproj_evac, 1)

            def silu_x(s, b):
                act.wait_ge(conv_step, 18 * s + 12)
                act.activation(xc[:, b, 0:ZT, :], xc[:, b, 0:ZT, :], ACT.Silu).then_inc(xs_ready, 1)

            def silu_BC(s, b):
                act.wait_ge(conv_step, 18 * (s + 1))
                act.activation(xc[:, b, ZT:, :], xc[:, b, ZT:, :], ACT.Silu).then_inc(xc_ready, 1)

            def silu_z(s, b):
                act.wait_ge(inproj_evac, 10 * s + XT + 2)
                act.activation(sz[:, b, 0:2, :], sz[:, b, 0:2, :], ACT.Silu).then_inc(sz_ready, 1)

            act.wait_ge(xT_loaded[0], 16)
            for s in range(2):
                for u in range(XT + CPS):
                    evac(s, s, u, s == 0, True)
                    if s == 0 and u == XT:
                        act.wait_ge(fw_split, 2)
                        act.dma_start(fstage[0:64, :, :], ffn_b.partition_broadcast(64)).then_inc(fb_loaded, 16)
                act.sem_inc(sz_ready, 1)
                if s == 0:
                    silu_x(s, s)
                    silu_BC(s, s)

            def split_hi(n, r):
                act.wait_ge(fT_done, n + 1)
                act.activation(fxT[:, r % 4, 0, :, :], f_in(r).rearrange("p (k t) -> p k t", k=KT), ACT.Copy).then_inc(fhi, 1)

            def experts(q, more, first):
                for r in range(FG):
                    n = FG * q + r
                    if more or r < FG - 2:
                        split_hi(n + 2, (r + 2) % FG)
                    act.wait_ge(fmm, n + 1)
                    if not (first and r < 4):
                        act.wait_ge(g_stored[r % 4], 16 * (2 * q + r // 4))
                    act.activation(gt[:, r % 4, :], f_out(r), ACT.Silu, scale=1.0 / WS).then_inc(fsilu, 1)
                    if not more and r < XT:
                        if r == 0:
                            act.wait_ge(conv_step, 36)
                        last = act.activation(xc[:, 1, r, :], xc[:, 1, r, :], ACT.Silu)
                        if r == ZT - 1:
                            last.then_inc(xs_ready, 1)
                        if r == XT - 1:
                            last.then_inc(xc_ready, 1)

            def exponential(n, c):
                act.wait_ge(L_done, n + 1)
                act.activation(Em[:, c % 2, :, :].rearrange("p h (f l) -> p f h l", f=2), bankL[:, :].rearrange("p (f h l) -> p f h l", f=2, h=H), ACT.Exp).then_inc(exp_done, 1)

            def x_by_token(n, c):
                act.wait_ge(xsT_done, n + 1)
                act.activation(xsT[:, c % 2, :], bank[2][:, :], ACT.Copy).then_inc(xsT_evac, 1)

            def y_over_rms(n, c):
                act.wait_ge(rstd_ready, n + 1)
                act.activation(yn[:, :], y[:, c % 2, :], ACT.Identity, scale=rstd[:, c:c + 1]).then_inc(yn_ready, 1)

            def y_high(n):
                act.wait_ge(yT_done, n + 1)
                act.activation(yT[:, 0, :], bank[2][:, :], ACT.Copy).then_inc(yT_hi, 1)

            split_hi(0, 0)
            split_hi(1, 1)
            experts(0, True, True)
            exponential(0, 0)
            x_by_token(0, 0)
            experts(1, True, False)
            with act.Fori(2, FT // FG - 1) as q:
                experts(q, True, False)
            experts(FT // FG - 1, False, False)
            def main(s, b, first, more, more2):
                for c in range(CPS):
                    n = 4 * s + c
                    now = units(c, b, first, more, more2)
                    if c < CPS - 1:
                        exponential(n + 1, c + 1)
                    if c == CPS - 1 and more:
                        x_by_token(n + 1, 0)
                    if not first_chunk(first, c):
                        y_over_rms(n - 1, (c - 1) % CPS)
                    if c < CPS - 1:
                        x_by_token(n + 1, c + 1)
                    if c == CPS - 2 and more:
                        exponential(n + 2, 0)
                    before = 0 if c == CPS - 2 else 1
                    for ds, bb, u in now[:before]:
                        evac(s + ds, bb, u, False, False)
                    if not first_chunk(first, c):
                        y_high(n - 1)
                    if c == CPS - 2 and now:
                        ds, bb, u = now[0]
                        evac(s + ds, bb, u, False, False)
                        silu_x(s + 1, 1 - b)
                    for ds, bb, u in now[1:]:
                        evac(s + ds, bb, u, False, False)
                    if not first:
                        act.wait_ge(fin_step, 3 * (n - 3))
                    if c == 0:
                        act.wait_ge(xin_loaded[b], 8 * (s - b) + 16)
                    act.activation(xn[:, c, :], xin[:, b, c, :], ACT.Identity, bias=st_of(norm_st, n, 1), scale=st_of(norm_st, n, 0)).then_inc(xn_done, 1)
                    if c == CPS - 2 and now:
                        silu_BC(s + 1, 1 - b)
                    act.wait_ge(gated, n + 1)
                    act.activation(ysq[:, :], y[:, c % 2, :], ACT.Square, scale=float(DI ** -0.5), accum_out=ssq[:, c:c + 1]).then_inc(sq_done, 1)
                    if c == CPS - 1 and more and not first:
                        silu_z(s + 1, 1 - b)

            main(0, 0, True, True, True)
            with act.Fori(0, SEQS // 2 - 2) as p:
                main(2 * p + 1, 1, False, True, True)
                main(2 * p + 2, 0, False, True, True)
            main(SEQS - 3, 1, False, True, True)
            main(SEQS - 2, 0, False, True, False)
            main(SEQS - 1, 1, False, False, False)
            y_over_rms(NCH - 1, CPS - 1)
            y_high(NCH - 1)

        @block.vector
        def _(dve):
            steps = [0]

            def wl(ins):
                steps[0] += 1
                ins.then_inc(wlink, 1)
                dve.wait_ge(wlink, steps[0])

            dve.wait_ge(const_ready, 2)
            dve.wait_ge(small_loaded, 16 * 8)
            for k in range(KT):
                last = nc.vector.tensor_scalar(nbrep[:, k, :], ones[:, :], nwb[:, 1, k:k + 1], WS, ALU.mult, ALU.mult)
            last.then_inc(nb_ready, 1)
            wl(nc.vector.tensor_scalar(nw64[:, :], nwb[:, 0, :], WS, None, ALU.mult))
            dve.wait_ge(wtr_evac, 2 * NW)
            for k in range(KT):
                wl(nc.vector.tensor_scalar(wz[:, 0, k, :], wT[:, k, :], nw64[:, k:k + 1], None, ALU.mult))
                wl(nc.vector.scalar_tensor_tensor(wz[:, 1, k, :], wT[:, k, :], nw64[:, k:k + 1], wz[:, 0, k, :], ALU.mult, ALU.subtract))
            dve.wait_ge(wtr_evac, 2 * NW + ZT + 1)
            wl(nc.vector.tensor_scalar(wo[:, 0, :, :], wo32[:, :, :], WS, None, ALU.mult))
            wl(nc.vector.scalar_tensor_tensor(wo[:, 1, :, :].rearrange("p k d -> p (k d)"), wo32[:, :, :].rearrange("p k d -> p (k d)"),
                                              WS, wo[:, 0, :, :].rearrange("p k d -> p (k d)"), ALU.mult, ALU.subtract))
            wl(nc.vector.tensor_scalar(mhi[:, :, 0:E], neg[:, :, :], 0.0, None, ALU.is_gt))
            wl(nc.vector.tensor_scalar(neg[:, :, :], neg[:, :, :], 0.0, None, ALU.is_lt))
            wl(nc.vector.tensor_tensor(mhi[:, :, 0:E], mhi[:, :, 0:E], neg[:, :, :], ALU.subtract))
            wl(nc.vector.tensor_copy(mhi[:, :, E:2 * E], wz[:, 0, :, DPROJ - H:DPROJ]))
            wl(nc.vector.tensor_copy(mlo[:, :, E:2 * E], wz[:, 1, :, DPROJ - H:DPROJ]))
            dve.wait_ge(bias_mm, 1)
            wl(nc.vector.tensor_copy(zbias[0:64, :], bank[2][0:64, :]))
            wl(nc.vector.tensor_tensor(zbias[32:64, :], bank[2][32:64, :], zbias[32:64, :], ALU.subtract))
            wl(nc.vector.tensor_copy(xbias[:, :], bank[3][:, 0:XT]))
            wl(nc.vector.scalar_tensor_tensor(dtb[:, :], bank[4][:, 0:H], 1.0 / WS, dtb[:, :], ALU.mult, ALU.add))
            dve.wait_ge(setup_done, 1)
            nc.vector.tensor_scalar(a_bc[:, :], a_bc[:, :], -1.0, None, ALU.mult).then_inc(setup_done, 1)

            def moments(r, q):
                dve.wait_ge(x_loaded[r], 16 * (q + 1))
                for c in range(CPS):
                    last = nc.vector.bn_stats(bst[:, r % 2, c, :], xg[:, r, c, :])
                last.then_inc(stats, 1)

            def low(j, r):
                dve.wait_ge(hi_ready, 2 * (j + 1))
                for k in range(KT):
                    last = nc.vector.tensor_tensor(xTs[:, r % 2, 1, k, :], bank[2 * (r % 2) + k][:, :], xTs[:, r % 2, 0, k, :], ALU.subtract)
                last.then_inc(lo_ready, 1)

            def scores(j, r):
                dve.wait_ge(sc_done, j + 1)
                nc.vector.tensor_copy(sd_all[:, bass.ts(j, CPS), :], bankL[:, (r % 2) * 512:(r % 2) * 512 + CPS * 2 * H].rearrange(
                    "p (c k) -> p c k", k=2 * H)).then_inc(sd_ready, 1)

            def norm(q, first, last_q):
                for r in range(4):
                    j = 4 * q + r
                    dve.wait_ge(stats, j + 1)
                    dve.sem_inc(aggr_go, 1)
                    for c in range(CPS):
                        last = nc.vector.bn_aggr(mv[:, r % 2, c, :], bst[:, r % 2, c, :])
                    last.then_inc(aggr, 1)
                    dve.wait_ge(aggr, j + 1)
                    nc.vector.tensor_scalar(var2[:, r % 2, :, 0:1], mv[:, r % 2, :, 1:2], EPS, None, ALU.add)
                    nc.vector.tensor_scalar(var2[:, r % 2, :, 1:2], mv[:, r % 2, :, 1:2], 1.0 + EPS, EPS * EPS, ALU.mult, ALU.add).then_inc(var_ready, 1)
                    if r < 3:
                        moments(r + 1, q)
                    elif not last_q:
                        moments(0, q + 1)
                    if not (first and r < 2):
                        scores(j - 2, r)
                    dve.wait_ge(rs_ready, j + 1)
                    nc.vector.scalar_tensor_tensor(nb1[:, r % 2, :, :], mv[:, r % 2, :, 0:1], -1.0, rs2[:, r % 2, :, 1:2], ALU.mult, ALU.mult)
                    nc.vector.tensor_copy(norm_st[:, bass.ts(j, CPS), 0:1], rs2[:, r % 2, :, 0:1])
                    nc.vector.scalar_tensor_tensor(norm_st[:, bass.ts(j, CPS), 1:2], mv[:, r % 2, :, 0:1], -1.0, rs2[:, r % 2, :, 0:1], ALU.mult, ALU.mult).then_inc(st_ready, 1)
                    for c in range(CPS - ACT_X1):
                        last = nc.vector.tensor_scalar(x1g[:, r % 2, c, :], xg[:, r, c, :], mv[:, r % 2, c, 0:1], rs2[:, r % 2, c, 1:2], ALU.subtract, ALU.mult)
                    last.then_inc(x1_ready, 1)
                    if not (first and r == 0):
                        low(j - 1, (r - 1) % 4)

            moments(0, 0)
            norm(0, True, False)
            with dve.Fori(1, 3) as q:
                norm(q, False, False)
            norm(3, False, True)
            scores(SEQS - 2, 2)
            low(SEQS - 1, 3)
            scores(SEQS - 1, 3)

            vs = [0]

            def link(ins):
                vs[0] += 1
                ins.then_inc(vstep, 1)
                dve.wait_ge(vstep, vs[0])

            c3 = lambda a: a.rearrange("p (c h) -> p c h", h=H)
            bc = lambda a: a.unsqueeze(1).to_broadcast([P, NCH, H])
            dve.wait_ge(sd_ready, SEQS)
            sc = sd_all[:, :, 0:E]
            big = lambda a: a.unsqueeze(2).to_broadcast([P, NCH, E])
            link(nc.vector.tensor_reduce(sm[:, 0, :], sc, AX.X, ALU.max))
            link(nc.vector.tensor_tensor(c3(rt[0][:, :]), sc, big(sm[:, 0, :]), ALU.is_ge))
            link(nc.vector.tensor_tensor(c3(rt[0][:, :]), c3(rt[0][:, :]), bc(rev[:, :]), ALU.mult))
            link(nc.vector.tensor_reduce(sm[:, 1, :], c3(rt[0][:, :]), AX.X, ALU.max))
            nc.vector.tensor_tensor(c3(ohb[:, :]), c3(rt[0][:, :]), big(sm[:, 1, :]), ALU.is_equal).then_inc(oh_ready, 1)
            dve.wait_ge(rank_mm, 1)
            dve.wait_ge(const_ready, 3)
            e3 = lambda a: a.rearrange("p (e c) -> p e c", c=NCH)
            ec = lambda a: a.rearrange("p (c e) -> p e c", e=E)
            link(nc.vector.tensor_copy(e3(rt[1][:, :]), ec(bankL[:, 512:1024])))
            link(nc.vector.tensor_tensor_scan(rt[2][:, :], keep[:, :, :].rearrange("p e c -> p (e c)"), rt[1][:, :], 0.0, ALU.mult, ALU.add))
            link(nc.vector.tensor_tensor(rt[1][:, :], rt[2][:, :], rt[1][:, :], ALU.subtract))
            link(nc.vector.tensor_scalar(smi[:, :].unsqueeze(2), e3(rt[2][:, :])[:, :, NCH - 1:NCH], float(P - 1), None, ALU.add))
            link(nc.vector.tensor_scalar(smi[:, :], smi[:, :], 7, None, ALU.arith_shift_right))
            link(nc.vector.tensor_copy(sm[:, 2, 0:E], smi[:, :]))
            link(nc.vector.tensor_tensor_scan(sm[:, 3, 0:E], ones[:, 0:E], sm[:, 2, 0:E], 0.0, ALU.mult, ALU.add))
            link(nc.vector.tensor_tensor(sm[:, 2, 0:E], sm[:, 3, 0:E], sm[:, 2, 0:E], ALU.subtract))
            link(nc.vector.tensor_scalar(sm[:, 2, 0:E], sm[:, 2, 0:E], float(P), None, ALU.mult))
            link(nc.vector.tensor_tensor(c3(rt[0][:, :]), c3(bankL[:, 0:512]), e3(rt[1][:, :]).rearrange("p e c -> p c e"), ALU.add))
            link(nc.vector.tensor_tensor(c3(rt[0][:, :]), c3(rt[0][:, :]), bc(sm[:, 2, 0:E]), ALU.add))
            link(nc.vector.tensor_tensor(rt[0][:, :], rt[0][:, :], ohb[:, :], ALU.mult))
            link(nc.vector.tensor_reduce(sm[:, 4, :], c3(rt[0][:, :]), AX.X, ALU.add))
            nc.vector.tensor_copy(pos_all[:, :], sm[:, 4, :]).then_inc(pos_ready, 1)
            for b in range(2):
                dve.wait_ge(xT_stored[b], 16 * (SEQS // 2 + 1))
            link(nc.vector.tensor_scalar(c3(t[0][:, :]), sd_all[:, :, H:2 * H], 1.0 / WS, None, ALU.mult))
            link(nc.vector.tensor_tensor(c3(t[0][:, :]), c3(t[0][:, :]), bc(dtb[:, :]), ALU.add))
            nc.vector.scalar_tensor_tensor(t[1][:, :], t[0][:, :], -1.0, t[0][:, :], ALU.mult, ALU.min).then_inc(softexp_in, 1)
            tv = rt[2][:, 0:FT // 2 * E].rearrange("p (n e) -> p n e", e=E)
            for half in range(2):
                f0 = half * (FT // 2)
                link(nc.vector.tensor_tensor(tv, tile_no[:, f0:f0 + FT // 2].unsqueeze(2).to_broadcast([P, FT // 2, E]),
                                             sm[:, 3, 0:E].unsqueeze(1).to_broadcast([P, FT // 2, E]), ALU.is_ge))
                link(nc.vector.tensor_reduce(tmp_te[:, f0:f0 + FT // 2], tv, AX.X, ALU.add))
            link(nc.vector.tensor_scalar(tmp_te[:, 0:FT], tmp_te[:, 0:FT], float(E - 1), None, ALU.min))
            f3 = lambda a: a.rearrange("p (g i) -> p g i", i=FG)
            link(nc.vector.tensor_tensor(f3(tmp_te[:, 0:FT]), f3(tmp_te[:, 0:FT]), octal[:, :].unsqueeze(1).to_broadcast([P, FT // FG, FG]), ALU.mult))
            link(nc.vector.tensor_reduce(wide_te[:, 0:FT // FG], f3(tmp_te[:, 0:FT]), AX.X, ALU.add))
            nc.vector.tensor_copy(te[:, :], wide_te[:, 0:FT // FG]).then_inc(te_ready, 1)

            dve.wait_ge(softexp_out, 1)
            link(nc.vector.tensor_scalar(t[2][:, :], t[1][:, :], 2.0, None, ALU.add))
            link(nc.vector.reciprocal(t[2][:, :], t[2][:, :]))
            link(nc.vector.tensor_tensor(t[1][:, :], t[1][:, :], t[2][:, :], ALU.mult))
            link(nc.vector.tensor_tensor(t[2][:, :], t[1][:, :], t[1][:, :], ALU.mult))
            link(nc.vector.tensor_scalar(t[3][:, :], t[2][:, :], 1.0 / 15, None, ALU.mult))
            for k in (13, 11, 9, 7, 5, 3):
                link(nc.vector.scalar_tensor_tensor(t[3][:, :], t[3][:, :], 1.0 / k, t[2][:, :], ALU.add, ALU.mult))
            link(nc.vector.scalar_tensor_tensor(t[3][:, :], t[3][:, :], 1.0, t[1][:, :], ALU.add, ALU.mult))
            link(nc.vector.tensor_scalar(t[0][:, :], t[0][:, :], 0.0, None, ALU.max))
            link(nc.vector.scalar_tensor_tensor(dt_all[:, :, :].rearrange("p c h -> p (c h)"), t[3][:, :], 2.0, t[0][:, :], ALU.mult, ALU.add))
            nc.vector.tensor_tensor(c3(t[0][:, :]), dt_all[:, :, :], bc(a_bc[:, :]), ALU.mult).then_inc(a_ready, 1)
            dve.wait_ge(cs_mm, 1)
            nc.vector.tensor_copy(t[2][:, :], bank[0][:, :]).then_inc(cs_copied, 1)
            dve.wait_ge(cs_copied, 1)
            top = -65536
            part = lambda k: csp[:, :, k * H:(k + 1) * H]
            link(nc.vector.tensor_scalar(t[3][:, :].bitcast(i32), t[2][:, :].bitcast(i32), top, None, ALU.bitwise_and))
            nc.vector.tensor_copy(part(0), c3(t[3][:, :]))
            link(nc.vector.tensor_tensor(t[3][:, :], t[2][:, :], t[3][:, :], ALU.subtract))
            link(nc.vector.tensor_scalar(t[4][:, :].bitcast(i32), t[3][:, :].bitcast(i32), top, None, ALU.bitwise_and))
            nc.vector.tensor_copy(part(1), c3(t[4][:, :]))
            nc.vector.tensor_tensor(part(2), c3(t[3][:, :]), c3(t[4][:, :]), ALU.subtract).then_inc(csp_ready, 1)
            dve.wait_ge(exps_done, 3)
            link(nc.vector.tensor_tensor(w_all[:, :, :], w_all[:, :, :], dt_all[:, :, :], ALU.mult))
            for g in range(8):
                dve.wait_ge(csT_done, g + 1)
                nc.vector.tensor_copy(csT[:, g * 1024:(g + 1) * 1024],
                                      bank[3 + g % 2][0:PARTS * H, :].bitcast(bf16)).then_inc(csT_evac, 1)
            fs = [0]

            def fl(ins):
                fs[0] += 1
                ins.then_inc(fstep, 1)
                dve.wait_ge(fstep, fs[0])

            f2 = lambda a: a.rearrange("p e d -> p (e d)")
            def split_weights(k):
                dve.wait_ge(fw_loaded[k], 16)
                fl(nc.vector.tensor_scalar(f2(fw[:, 0, k, :, :]), f2(fstage[:, :, :]), WS, None, ALU.mult))
                nc.vector.scalar_tensor_tensor(f2(fw[:, 1, k, :, :]), f2(fstage[:, :, :]), WS, f2(fw[:, 0, k, :, :]), ALU.mult, ALU.subtract).then_inc(fw_split, 1)

            split_weights(0)

            def split_bias():
                dve.wait_ge(fb_loaded, 16)
                fl(nc.vector.tensor_scalar(f2(fb[0:64, :, :]), f2(fstage[0:64, :, :]), WS, None, ALU.mult))
                nc.vector.scalar_tensor_tensor(f2(fb[32:64, :, :]), f2(fstage[32:64, :, :]), WS, f2(fb[32:64, :, :]), ALU.mult, ALU.subtract).then_inc(fw_ready, 1)

            def conv(s, b, g, part):
                for tap, i in ((1, 0), (1, 1), (2, 0), (2, 1), (3, 0), (3, 1))[3 * part:3 * part + 3]:
                    m = 2 * g + i
                    if tap == 1:
                        dve.wait_ge(tap0, 6 * s + m + 1)
                    else:
                        dve.wait_ge(conv_step, 18 * s + 6 * g + 2 * (tap - 2) + i + 1)
                    nc.vector.scalar_tensor_tensor(xc[:, b, m, :], vraw[:, m, TAPS - 1 - tap:TAPS - 1 - tap + SEQ],
                                                   cw[:, m, TAPS - 1 - tap:TAPS - tap], xc[:, b, m, :], ALU.mult, ALU.add).then_inc(conv_step, 1)

            dve.wait_ge(cs_stored, 16)
            dve.wait_ge(zero_written, 16 * (FT // 4))
            nc.vector.memset(vraw[:, :, 0:TAPS - 1], 0.0).then_inc(vraw_ready, 1)
            dve.wait_ge(vraw_ready, 1)
            for s in range(2):
                for g in range(3):
                    for part in range(2):
                        conv(s, s, g, part)
                    if s == 0 and g == 0:
                        split_weights(1)
                if s == 0:
                    split_bias()

            def low_part(n, r):
                dve.wait_ge(fhi, n + 1)
                nc.vector.tensor_tensor(fxT[:, r % 4, 1, :, :], f_in(r).rearrange("p (k t) -> p k t", k=KT),
                                        fxT[:, r % 4, 0, :, :], ALU.subtract).then_inc(flo, 1)

            def lows(q):
                for r in range(FG):
                    low_part(FG * q + r, r)

            h3 = lambda a: a.rearrange("p (h d) -> p h d", d=HD)
            hb = lambda a: a.unsqueeze(2).to_broadcast([P, H, HD])

            def front(n, c):
                dve.wait_ge(exp_done, n + 1)
                dve.wait_ge(B_done, n + 1)
                nc.vector.scalar_tensor_tensor(Em[:, c % 2, :, :], Em[:, c % 2, :, :], 1.0, bank[3][:, 0:P].unsqueeze(1).to_broadcast([P, H, P]),
                                               ALU.min, ALU.mult).then_inc(M_ready, 1)
                dve.wait_ge(xsT_evac, n + 1)
                nc.vector.tensor_tensor(h3(Xdt[:, c % 2, :]), h3(xsT[:, c % 2, :]), hb(w_of(dt_all, n)), ALU.mult).then_inc(X_ready, 1)
                nc.vector.tensor_copy(BT[:, :], bank[3][:, P:2 * P]).then_inc(B_evac, 1)

            def const_l(b):
                for f in range(2):
                    nc.vector.tensor_copy(csl[:, b, f, :].rearrange("p (c t) -> p c t", t=P), later[:, f, :].unsqueeze(1).to_broadcast([P, CPS, P]))

            def const_r(b):
                nc.vector.tensor_copy(csr[:, b, :, :, :], blk[:, :, :].unsqueeze(2).to_broadcast([P, H, CPS, P])).then_inc(main_const, 1)

            for r in range(4):
                dve.wait_ge(scattered[r], 16 * SEQS)
            low_part(0, 0)
            low_part(1, 1)
            const_l(0)
            low_part(2, 2)
            const_r(0)
            for r in range(3, FG):
                low_part(r, r)
            front(0, 0)
            const_l(1)
            const_r(1)
            with dve.Fori(1, FT // FG) as q:
                lows(q)

            def finish(s, b, c):
                n = 4 * s + c
                i = c % 2
                dve.wait_ge(o_done, n + 1)
                dve.wait_ge(xn_done, n + 1)
                if c == 0:
                    dve.wait_ge(g_loaded[b], 32 * (s - b) + 64)
                    dve.wait_ge(xin_loaded[b], 8 * (s - b) + 16)
                    if not (isinstance(s, int) and s == 0):
                        dve.wait_ge(out_stored, 16 * s)
                nc.vector.scalar_tensor_tensor(fo[:, i, :], bank[3][:, 2 * P:], 1.0 / WS, xn[:, c, :], ALU.mult, ALU.add).then_inc(fin_step, 1)
                dve.wait_ge(fin_step, 3 * n + 1)
                nc.vector.tensor_tensor(fo[:, i, :], fo[:, i, :], gin[:, b, c, :], ALU.mult).then_inc(fin_step, 1)
                dve.wait_ge(fin_step, 3 * n + 2)
                nc.vector.tensor_tensor(ob[:, c, :], fo[:, i, :], xin[:, b, c, :], ALU.add).then_inc(fin_step, 1)

            def y_low(n):
                dve.wait_ge(yT_hi, n + 1)
                nc.vector.tensor_tensor(yT[:, 1, :], bank[2][:, :], yT[:, 0, :], ALU.subtract).then_inc(yT_lo, 1)

            def main(s, b, first, more):
                for c in range(CPS):
                    n = 4 * s + c
                    if c > 0:
                        dve.wait_ge(yoff_done, 3 * s + c)
                        nc.vector.tensor_tensor(h3(yo[:, :]), h3(bank[5][:, :]), hb(w_of(ea_all, n)), ALU.mult).then_inc(yo_ready, 1)
                        dve.wait_ge(yd_done, n + 1)
                        dve.wait_ge(yo_ready, 3 * s + c)
                        nc.vector.tensor_tensor(y[:, c % 2, :], bank[4][:, :], yo[:, :], ALU.add).then_inc(y_raw, 1)
                    else:
                        dve.wait_ge(yd_done, n + 1)
                        dve.wait_ge(xD_ready, n + 1)
                        nc.vector.tensor_tensor(y[:, c % 2, :], bank[4][:, :], xD[:, c % 2, :], ALU.add).then_inc(y_raw, 1)
                    if not (first and c < 2):
                        if c < 2:
                            finish(s - 1, 1 - b, c + 2)
                        else:
                            finish(s, b, c - 2)
                    if c < CPS - 1:
                        dve.wait_ge(snew_done, 3 * s + c + 1)
                        if c == 0:
                            nc.vector.tensor_copy(S[:, :], bank[5][:, :]).then_inc(S_ready, 1)
                        else:
                            dve.wait_ge(Sd_ready, 2 * s + c)
                            nc.vector.tensor_tensor(S[:, :], bank[5][:, :], Sd[:, :], ALU.add).then_inc(S_ready, 1)
                    conv_now = more and c < 3 and not first
                    if c < CPS - 1 or more:
                        front(n + 1, (c + 1) % CPS)
                    if conv_now:
                        conv(s + 1, 1 - b, c, 0)
                    if not first_chunk(first, c):
                        y_low(n - 1)
                    if conv_now:
                        conv(s + 1, 1 - b, c, 1)

            main(0, 0, True, True)
            with dve.Fori(0, SEQS // 2 - 1) as p:
                main(2 * p + 1, 1, False, True)
                main(2 * p + 2, 0, False, True)
            main(SEQS - 1, 1, False, False)
            y_low(NCH - 1)
            finish(SEQS - 1, 1, CPS - 2)
            finish(SEQS - 1, 1, CPS - 1)

        @block.tensor
        def _(pe):
            mm, tr = nc.tensor.matmul, nc.tensor.transpose
            pe.wait_ge(const_ready, 1)
            pe.wait_ge(w_loaded, 64)
            n = 0
            for k in range(KT):
                for m, (c0, cn) in enumerate(wcols):
                    if n >= 3:
                        pe.wait_ge(wtr_evac, n - 2)
                    tr((bank[0], bank[1], bank[5])[n % 3][:, 0:cn], wrow[0:cn, m, k * P:(k + 1) * P], ident[0:cn, 0:cn]).then_inc(wtr_done, 1)
                    n += 1
            for kc in range(ZT):
                pe.wait_ge(wtr_evac, n - 2)
                for m in range(KT):
                    last = tr((bank[0], bank[1], bank[5])[n % 3][:, m * P:(m + 1) * P], worow[:, m, kc * P:(kc + 1) * P], ident[:, :])
                last.then_inc(wtr_done, 1)
                n += 1
            pe.wait_ge(wtr_evac, n - 2)
            for k in range(KT):
                last = tr((bank[0], bank[1], bank[5])[n % 3][:, k * E:(k + 1) * E], sig[0:E, k * P:(k + 1) * P], ident[0:E, 0:E])
            last.then_inc(wtr_done, 1)
            pe.wait_ge(nb_ready, 1)
            pe.wait_ge(wtr_evac, 2 * NW)
            for k in range(KT):
                mm(bank[2][:, :], nbrep[:, k, :], wT[:, k, 0:DI], start=(k == 0), stop=(k == KT - 1))
            for m in range(XT):
                for k in range(KT):
                    mm(bank[3][:, m:m + 1], wT[:, k, DI + m * P:DI + (m + 1) * P], nwb[:, 1, k:k + 1], start=(k == 0), stop=(k == KT - 1))
            for k in range(KT):
                last = mm(bank[4][:, 0:H], nbrep[:, k, :], wT[:, k, DPROJ - H:DPROJ], start=(k == 0), stop=(k == KT - 1))
            last.then_inc(bias_mm, 1)
            pe.wait_ge(setup_done, 2)

            def scores(j, r):
                pe.wait_ge(lo_ready, j + 1)
                for c in range(CPS):
                    o = (r % 2) * 512 + c * 2 * H
                    terms = [(xTs[:, r % 2, a, k, c * P:(c + 1) * P], w[:, k, :]) for k in range(KT) for a, w in ((0, mhi), (1, mhi), (0, mlo))]
                    for i, (lhs, rhs) in enumerate(terms):
                        last = mm(bankL[:, o:o + 2 * H], lhs, rhs, start=(i == 0), stop=(i == len(terms) - 1))
                last.then_inc(sc_done, 1)

            def first_pass(q, first):
                for r in range(4):
                    j = 4 * q + r
                    pe.wait_ge(x1_ready, j + 1)
                    for c in range(CPS):
                        if c == CPS - ACT_X1:
                            pe.wait_ge(x1_ready_act, j + 1)
                        for k in range(KT):
                            last = tr(bank[2 * (r % 2) + k][:, c * P:(c + 1) * P], x1g[:, r % 2, c, k * P:(k + 1) * P], ident[:, :])
                    last.then_inc(T_done, 1)
                    if not (first and r == 0):
                        scores(j - 1, (r - 1) % 4)

            first_pass(0, True)
            with pe.Fori(1, 4) as q:
                first_pass(q, False)
            scores(SEQS - 1, 3)
            pe.wait_ge(oh_ready, 1)
            mm(bankL[:, 0:512], stri_b[:, :], ohb[:, :], start=True, stop=True)
            mm(bankL[:, 512:1024], ones_b[:, :], ohb[:, :], start=True, stop=True).then_inc(rank_mm, 1)
            pe.wait_ge(a_ready, 1)
            for i, m in enumerate((tri, ones, suf)):
                last = mm(bank[i][:, :], m[:, :], t[0][:, :], start=True, stop=True)
            last.then_inc(cs_mm, 1)
            pe.wait_ge(csp_ready, 1)
            for g in range(8):
                if g >= 2:
                    pe.wait_ge(csT_evac, g - 1)
                for i in range(8):
                    last = tr(bank[3 + g % 2][0:PARTS * H, :].bitcast(bf16)[:, i * P:(i + 1) * P], csp[:, 8 * g + i, :], ident_b[:, :])
                last.then_inc(csT_done, 1)
            def in_proj(s, b, u, first):
                if u == 0:
                    pe.wait_ge(xT_loaded[b], 8 * (s - b) + 16)
                if not (first and u < 2):
                    pe.wait_ge(inproj_evac, 10 * s + u - 1)
                o = bank[u % 2][:, :]
                i = 0
                if u >= XT:
                    mm(o, pick[:, :], zbias[:, :], start=True, stop=False)
                for k in range(KT):
                    for a, w in ((0, 0), (1, 0), (0, 1)):
                        i += 1
                        if u < XT:
                            last = mm(o, wz[:, w, k, DI + u * P:DI + (u + 1) * P], xT[:, b, a, k, :], start=(i == 1), stop=(i == 3 * KT))
                        else:
                            c = u - XT
                            last = mm(o, xT[:, b, a, k, c * P:(c + 1) * P], wz[:, w, k, 0:DI], start=False, stop=(i == 3 * KT))
                last.then_inc(inproj_done, 1)

            pe.wait_ge(exps_done, 2)
            for s in range(2):
                for u in range(XT + CPS):
                    in_proj(s, s, u, s == 0)
            pe.wait_ge(te_ready, 1)
            pe.wait_ge(fw_ready, 1)
            pe.wait_ge(inproj_evac, 20)

            def transposes(n, r, q):
                pe.wait_ge(ft_loaded[r], 16 * (q + 1))
                for k in range(KT):
                    last = tr(f_in(r)[:, k * P:(k + 1) * P], ft[:, r, k * P:(k + 1) * P], ident[:, :])
                last.then_inc(fT_done, 1)

            def experts(q, more, first):
                word = nc.tensor.value_load(te[0:1, bass.ds(q, 1)], min_val=0, max_val=E ** FG - 1)
                for r in range(FG):
                    n = FG * q + r
                    if r < FG - 2:
                        transposes(n + 2, r + 2, q)
                    elif more:
                        transposes(n + 2, r + 2 - FG, q + 1)
                    e = (word >> (3 * r)) & (E - 1)
                    pe.wait_ge(flo, n + 1)
                    if not (first and r < 4):
                        pe.wait_ge(fsilu, n - 3)
                    o = f_out(r)
                    mm(o, pick[:, :], fb[:, bass.ds(e, 1), :].rearrange("p e d -> p (e d)"), start=True, stop=False)
                    terms = [(k, a, w) for k in range(KT) for a, w in ((0, 0), (1, 0), (0, 1))]
                    for i, (k, a, w) in enumerate(terms):
                        last = mm(o, fxT[:, r % 4, a, k, :], fw[:, w, k, bass.ds(e, 1), :].rearrange("p e d -> p (e d)"),
                                  start=False, stop=(i == len(terms) - 1))
                    last.then_inc(fmm, 1)

            def x_by_token(n, b, c, s, head):
                if c == 0:
                    pe.wait_ge(xs_ready, s + 1)
                if not head:
                    pe.wait_ge(xsT_evac, n)
                    if not (isinstance(n, int) and n < 3):
                        pe.wait_ge(yT_lo, n - 2)
                for k in range(ZT):
                    last = tr(bank[2][:, k * P:(k + 1) * P], xc[:, b, k, c * P:(c + 1) * P], ident[:, :])
                last.then_inc(xsT_done, 1)

            def decay(n, b, c, s, head):
                if not head:
                    pe.wait_ge(exp_done, n)
                if c == 0:
                    pe.wait_ge(cs_loaded[b], 24 * (s - b) + 48)
                for f in range(2):
                    last = mm(bankL[:, f * 512:(f + 1) * 512], csl[:, b, f, c * P:(c + 1) * P], csr[:, b, :, c, f * (P // 2):(f + 1) * (P // 2)],
                              start=True, stop=True)
                last.then_inc(L_done, 1)

            def CB(n, b, c, s, head):
                tok = slice(c * P, (c + 1) * P)
                if c == 0:
                    pe.wait_ge(xc_ready, s + 1)
                if not head:
                    pe.wait_ge(B_evac, n)
                mm(bank[3][:, 0:P], xc[:, b, ZT, tok], xc[:, b, ZT + 1, tok], start=True, stop=True)
                tr(bank[3][:, P:2 * P], xc[:, b, ZT, tok], ident[:, :]).then_inc(B_done, 1)

            transposes(0, 0, 0)
            transposes(1, 1, 0)
            experts(0, True, True)
            pe.wait_ge(fsilu, FG)
            decay(0, 0, 0, 0, True)
            x_by_token(0, 0, 0, 0, True)
            CB(0, 0, 0, 0, True)
            pe.wait_ge(exp_done, 1)
            pe.wait_ge(xsT_evac, 1)
            pe.wait_ge(B_evac, 1)
            with pe.Fori(1, FT // FG - 1) as q:
                experts(q, True, False)
            experts(FT // FG - 1, False, False)
            pe.wait_ge(fsilu, FT)

            def y_by_channel(n):
                pe.wait_ge(yn_ready, n + 1)
                for k in range(ZT):
                    last = tr(bank[2][:, k * P:(k + 1) * P], yn[:, k * P:(k + 1) * P], ident[:, :])
                last.then_inc(yT_done, 1)

            def out_proj(n):
                pe.wait_ge(yT_lo, n + 1)
                terms = [(k, a, w) for k in range(ZT) for a, w in ((0, 0), (1, 0), (0, 1))]
                for i, (k, a, w) in enumerate(terms):
                    last = mm(bank[3][:, 2 * P:], yT[:, a, k * P:(k + 1) * P], wo[:, w, k, :], start=(i == 0), stop=(i == len(terms) - 1))
                last.then_inc(o_done, 1)

            def main(s, b, first, more, more2):
                for c in range(CPS):
                    n = 4 * s + c
                    tok = slice(c * P, (c + 1) * P)

                    def c_state():
                        pe.wait_ge(S_ready, 3 * s + c)
                        mm(bank[5][:, :], xc[:, b, ZT + 1, tok], S[:, :], start=True, stop=True).then_inc(yoff_done, 1)

                    if c in (1, 2):
                        c_state()
                    pe.wait_ge(X_ready, n + 1)
                    pe.wait_ge(M_ready, n + 1)
                    for h in range(H):
                        last = mm(bank[4][:, h * HD:(h + 1) * HD], Em[:, c % 2, h, :], Xdt[:, c % 2, h * HD:(h + 1) * HD], start=True, stop=True)
                    last.then_inc(yd_done, 1)
                    if c == 3:
                        c_state()
                    if not (first and c < 2):
                        pe.wait_ge(B_evac, n + 1)
                        out_proj(n - 2)
                    now = units(c, b, first, more, more2)
                    if c < CPS - 1:
                        decay(n + 1, b, c + 1, s, False)
                        x_by_token(n + 1, b, c + 1, s, False)
                        pe.wait_ge(Xw_ready, 3 * s + c + 1)
                        pe.wait_ge(B_evac, n + 1)
                        if c > 0:
                            pe.wait_ge(yo_ready, 3 * s + c)
                        mm(bank[5][:, :], BT[:, :], Xw[:, c % 2, :], start=True, stop=True).then_inc(snew_done, 1)
                    elif more:
                        x_by_token(n + 1, 1 - b, 0, s + 1, False)
                        for ds, bb, u in now[:1]:
                            in_proj(s + ds, bb, u, False)
                    if c < CPS - 1 or more:
                        if not (first and c < 2):
                            pe.wait_ge(fin_step, 3 * (n - 2) + 1)
                        CB(n + 1, b if c < CPS - 1 else 1 - b, (c + 1) % CPS, s + (c + 1) // CPS, False)
                    if c == CPS - 2 and more:
                        decay(n + 2, 1 - b, 0, s + 1, False)
                    ahead = 2 if c == 0 else 1
                    if c < CPS - 1:
                        for ds, bb, u in now[:ahead]:
                            in_proj(s + ds, bb, u, False)
                    else:
                        for ds, bb, u in now[1:]:
                            in_proj(s + ds, bb, u, False)
                    if not first_chunk(first, c):
                        if c < CPS - 1 or more:
                            pe.wait_ge(xsT_evac, n + 2)
                        y_by_channel(n - 1)
                    if c < CPS - 1:
                        for ds, bb, u in now[ahead:]:
                            in_proj(s + ds, bb, u, False)

            main(0, 0, True, True, True)
            with pe.Fori(0, SEQS // 2 - 2) as p:
                main(2 * p + 1, 1, False, True, True)
                main(2 * p + 2, 0, False, True, True)
            main(SEQS - 3, 1, False, True, True)
            main(SEQS - 2, 0, False, True, False)
            main(SEQS - 1, 1, False, False, False)
            pe.wait_ge(fin_step, 3 * (NCH - 3) + 1)
            out_proj(NCH - 2)
            y_by_channel(NCH - 1)
            pe.wait_ge(fin_step, 3 * (NCH - 2) + 1)
            out_proj(NCH - 1)


def units(c, b, first, more, more2):
    if c == CPS - 1:
        return [(2, b, u) for u in (0, 1)] if more2 else []
    return [(1, 1 - b, u) for u in ((2, 3, 4), (5, 6, 7), (8, 9))[c]] if more and not first else []


def first_chunk(first, c):
    return first and c == 0


def w_of(a, n):
    return a[:, bass.ds(n, 1), :].rearrange("p o h -> p (o h)") if not isinstance(n, int) else a[:, n, :]


def st_of(a, n, k):
    return a[:, bass.ds(n, 1), k:k + 1].rearrange("p o k -> p (o k)") if not isinstance(n, int) else a[:, n, k:k + 1]


def row_of(a, n):
    return a[:, bass.ds(n, 1), :].rearrange("p o d -> p (o d)") if not isinstance(n, int) else a[:, n, :]


_INS = ["L0_attn_x", "L0_attn_norm_w", "L0_attn_norm_b", "L0_attn_in_proj_w", "L0_attn_conv_w", "L0_attn_conv_b", "L0_attn_dt_bias",
        "L0_attn_A_log", "L0_attn_D", "L0_attn_rms_w", "L0_attn_out_proj_w", "L0_ffn_tile_sigs", "L0_ffn_W", "L0_ffn_b"]


def kernel(**inputs):
    import concourse.bacc as _bacc
    from concourse.bass_utils import run_bass_kernel_spmd as _run

    nc = _bacc.Bacc("TRN2", target_bir_lowering=False, num_devices=1)
    arrays, args = {}, []
    for name in _INS:
        a = np.ascontiguousarray(inputs[name])
        arrays[f"in_{name}"] = a
        args.append(nc.dram_tensor(f"in_{name}", a.shape, mybir.dt.from_np(a.dtype), kind="ExternalInput").ap())
    out = nc.dram_tensor("out_0", (SEQS, SEQ, DM), mybir.dt.float32, kind="ExternalOutput").ap()
    program(nc, *args, out)
    r = _run(nc, [arrays], core_ids=[0])
    return r.results[0]["out_0"]
```
